# Optimizing a Trainium2 kernel written in Bass

```python
import numpy as np
import jax
import jax.numpy as jnp

def _softmax(x, axis=-1):
    return jax.nn.softmax(x, axis=axis)

def _gelu(x):
    return jax.nn.gelu(x, approximate=True)

def _silu(x):
    return jax.nn.silu(x)

def _sigmoid(x):
    return jax.nn.sigmoid(x)

def _layernorm(x, axis=-1, eps=1e-05):
    m = jnp.mean(x, axis=axis, keepdims=True)
    v = jnp.var(x, axis=axis, keepdims=True)
    return (x - m) / jnp.sqrt(v + eps)

def _scatter_add(tgt, idx, src, axis=0):
    return tgt.at[idx].add(src)

def _segment_sum(src, seg, n):
    return jax.ops.segment_sum(src, seg, n)
kernel_name = 'mk_gnn_ffn_d2_gnn_r8_702215'

def setup_inputs(seed: int=0):
    np.random.seed(seed)
    _w = jnp.asarray

    def _rec_inputs():
        import jax
        import jax.numpy as jnp
        _gk = jax.random.key(seed)
        x = -0.0002928 + 1 * jax.random.normal(jax.random.fold_in(_gk, 1), (1250, 512), jnp.float32)
        _s = jax.random.randint(jax.random.fold_in(_gk, 2), (10000,), 0, 1250, jnp.int32)
        _d = jax.random.randint(jax.random.fold_in(_gk, 3), (10000,), 0, 1250, jnp.int32)
        _loop = jnp.arange(1250, dtype=jnp.int32)
        src = jnp.concatenate([_s, _d, _loop])
        dst = jnp.concatenate([_d, _s, _loop])
        _o = jnp.argsort(dst, stable=True)
        src = src[_o]
        dst = dst[_o]
        edge_attr_64 = 0.000189758 + 1.00013 * jax.random.normal(jax.random.fold_in(_gk, 12), (21250, 64), jnp.float32)
        return (x, src, dst, edge_attr_64)
    x, src, dst, edge_attr_64 = _rec_inputs()

    def _L0_gnn_setup():
        import jax, jax.numpy as jnp
        import numpy as np
        N, IN_DIM, OUT_DIM, H = (1024, 512, 512, 4)
        E = 16384
        HC = H * OUT_DIM
        key = jax.random.key(seed)
        ks = jax.random.split(key, 12)
        s = 1.0 / np.sqrt(IN_DIM)
        return {'x': jax.random.normal(ks[0], (N, IN_DIM), dtype=jnp.float32), 'edge_index': jax.random.randint(ks[1], (2, E), 0, N, dtype=jnp.int64), 'Wq': jax.random.normal(ks[2], (IN_DIM, HC), dtype=jnp.float32) * s, 'bq': jnp.zeros((HC,), dtype=jnp.float32), 'Wk': jax.random.normal(ks[3], (IN_DIM, HC), dtype=jnp.float32) * s, 'bk': jnp.zeros((HC,), dtype=jnp.float32), 'Wv': jax.random.normal(ks[4], (IN_DIM, HC), dtype=jnp.float32) * s, 'bv': jnp.zeros((HC,), dtype=jnp.float32), 'Wskip': jax.random.normal(ks[5], (IN_DIM, HC), dtype=jnp.float32) * s, 'bskip': jnp.zeros((HC,), dtype=jnp.float32), 'Wlin': jax.random.normal(ks[6], (HC, OUT_DIM), dtype=jnp.float32) / np.sqrt(HC), 'blin': jnp.zeros((OUT_DIM,), dtype=jnp.float32), 'gamma': jnp.ones((OUT_DIM,), dtype=jnp.float32), 'beta': jnp.zeros((OUT_DIM,), dtype=jnp.float32)}
    _L0_gnn_all = _L0_gnn_setup()
    _L0_gnn_in = {k: v for k, v in _L0_gnn_all.items() if k in ('Wq', 'bq', 'Wk', 'bk', 'Wv', 'bv', 'Wskip', 'bskip', 'Wlin', 'blin', 'gamma', 'beta')}
    del _L0_gnn_all

    def _L0_ffn_setup():
        import jax, jax.numpy as jnp
        import numpy as np
        B, T, H = (8, 1024, 512)
        E, R = (4, 16)
        SCALE = 0.04
        key = jax.random.key(seed)
        ks = jax.random.split(key, 7)
        return {'x': jax.random.normal(ks[0], (B, T, H), jnp.float32), 'gate_w': jax.random.normal(ks[1], (E, H), jnp.float32) * SCALE, 'thr_w': jax.random.normal(ks[2], (1, H), jnp.float32) * SCALE, 'fc1_w': jax.random.normal(ks[3], (E, H, H), jnp.float32) * SCALE, 'lora_A': jax.random.normal(ks[4], (E, H, R), jnp.float32) * SCALE, 'lora_B': jax.random.normal(ks[5], (E, R, H), jnp.float32) * SCALE, 'fc2_w': jax.random.normal(ks[6], (E, H, H), jnp.float32) * SCALE}
    _L0_ffn_all = _L0_ffn_setup()
    _L0_ffn_in = {k: v for k, v in _L0_ffn_all.items() if k in ('gate_w', 'thr_w', 'fc1_w', 'lora_A', 'lora_B', 'fc2_w')}
    del _L0_ffn_all

    def _L1_gnn_setup():
        import jax, jax.numpy as jnp
        import numpy as np
        N_NODES = 6250
        N_EDGES = 100000
        NODE_IN = 512
        EDGE_IN = 64
        HID = 1024
        key = jax.random.key(seed)
        ks = jax.random.split(key, 6)
        x = jax.random.normal(ks[0], (N_NODES, NODE_IN), dtype=jnp.float32)
        edge_index = jax.random.randint(ks[1], (2, N_EDGES), 0, N_NODES, dtype=jnp.int64)
        edge_attr = jax.random.normal(ks[2], (N_EDGES, EDGE_IN), dtype=jnp.float32)
        u = jnp.zeros((1, 16), dtype=jnp.float32)
        batch = jnp.zeros((N_NODES,), dtype=jnp.int64)
        s1 = 1.0 / np.sqrt(NODE_IN + EDGE_IN)
        s2 = 1.0 / np.sqrt(HID)
        W1 = jax.random.normal(ks[3], (NODE_IN + EDGE_IN, HID), dtype=jnp.float32) * s1
        b1 = jnp.zeros((HID,), dtype=jnp.float32)
        W2 = jax.random.normal(ks[4], (HID, NODE_IN), dtype=jnp.float32) * s2
        b2 = jnp.zeros((NODE_IN,), dtype=jnp.float32)
        return {'x': x, 'edge_index': edge_index, 'edge_attr': edge_attr, 'u': u, 'batch': batch, 'W1': W1, 'b1': b1, 'W2': W2, 'b2': b2}
    _L1_gnn_all = _L1_gnn_setup()
    _L1_gnn_in = {k: v for k, v in _L1_gnn_all.items() if k in ('u', 'W1', 'b1', 'W2', 'b2')}
    del _L1_gnn_all

    def _L1_ffn_setup():
        import jax, jax.numpy as jnp
        import numpy as np
        D, NH, HID, E = (512, 8, 256, 8)
        EPS = 1e-05

        def _layernorm(x, g, b):
            mu = jnp.mean(x, axis=-1, keepdims=True)
            var = jnp.mean(jnp.square(x - mu), axis=-1, keepdims=True)
            return (x - mu) * jax.lax.rsqrt(var + EPS) * g + b
        key = jax.random.key(seed)
        ks = jax.random.split(key, 20)
        s = 0.02
        inp = {'x': jax.random.normal(ks[0], (4, 1024, D), jnp.float32), 'Wq': jax.random.normal(ks[1], (D, D), jnp.float32) * s, 'bq': jnp.zeros((D,), jnp.float32), 'Wk': jax.random.normal(ks[2], (D, D), jnp.float32) * s, 'bk': jnp.zeros((D,), jnp.float32), 'Wv': jax.random.normal(ks[3], (D, D), jnp.float32) * s, 'bv': jnp.zeros((D,), jnp.float32), 'Wo': jax.random.normal(ks[4], (D, D), jnp.float32) * s, 'bo': jnp.zeros((D,), jnp.float32), 'g1': jnp.ones((D,), jnp.float32), 'beta1': jnp.zeros((D,), jnp.float32), 'g2': jnp.ones((D,), jnp.float32), 'beta2': jnp.zeros((D,), jnp.float32), 'Wg': jax.random.normal(ks[5], (D, E), jnp.float32) * s, 'bg': jnp.zeros((E,), jnp.float32), 'W1': jax.random.normal(ks[6], (E, D, HID), jnp.float32) * s, 'b1': jnp.zeros((E, HID), jnp.float32), 'W2': jax.random.normal(ks[7], (E, HID, D), jnp.float32) * s, 'b2': jnp.zeros((E, D), jnp.float32)}
        return inp
    _L1_ffn_all = _L1_ffn_setup()
    _L1_ffn_in = {k: v for k, v in _L1_ffn_all.items() if k in ('Wq', 'bq', 'Wk', 'bk', 'Wv', 'bv', 'Wo', 'bo', 'g1', 'beta1', 'g2', 'beta2', 'Wg', 'bg', 'W1', 'b1', 'W2', 'b2')}
    del _L1_ffn_all
    return {'x': x, 'src': src, 'dst': dst, 'edge_attr_64': edge_attr_64, 'L0_gnn_Wq': _L0_gnn_in['Wq'], 'L0_gnn_bq': _L0_gnn_in['bq'], 'L0_gnn_Wk': _L0_gnn_in['Wk'], 'L0_gnn_bk': _L0_gnn_in['bk'], 'L0_gnn_Wv': _L0_gnn_in['Wv'], 'L0_gnn_bv': _L0_gnn_in['bv'], 'L0_gnn_Wskip': _L0_gnn_in['Wskip'], 'L0_gnn_bskip': _L0_gnn_in['bskip'], 'L0_gnn_Wlin': _L0_gnn_in['Wlin'], 'L0_gnn_blin': _L0_gnn_in['blin'], 'L0_gnn_gamma': _L0_gnn_in['gamma'], 'L0_gnn_beta': _L0_gnn_in['beta'], 'L0_ffn_gate_w': _L0_ffn_in['gate_w'], 'L0_ffn_thr_w': _L0_ffn_in['thr_w'], 'L0_ffn_fc1_w': _L0_ffn_in['fc1_w'], 'L0_ffn_lora_A': _L0_ffn_in['lora_A'], 'L0_ffn_lora_B': _L0_ffn_in['lora_B'], 'L0_ffn_fc2_w': _L0_ffn_in['fc2_w'], 'L1_gnn_u': _L1_gnn_in['u'], 'L1_gnn_W1': _L1_gnn_in['W1'], 'L1_gnn_b1': _L1_gnn_in['b1'], 'L1_gnn_W2': _L1_gnn_in['W2'], 'L1_gnn_b2': _L1_gnn_in['b2'], 'L1_ffn_Wq': _L1_ffn_in['Wq'], 'L1_ffn_bq': _L1_ffn_in['bq'], 'L1_ffn_Wk': _L1_ffn_in['Wk'], 'L1_ffn_bk': _L1_ffn_in['bk'], 'L1_ffn_Wv': _L1_ffn_in['Wv'], 'L1_ffn_bv': _L1_ffn_in['bv'], 'L1_ffn_Wo': _L1_ffn_in['Wo'], 'L1_ffn_bo': _L1_ffn_in['bo'], 'L1_ffn_g1': _L1_ffn_in['g1'], 'L1_ffn_beta1': _L1_ffn_in['beta1'], 'L1_ffn_g2': _L1_ffn_in['g2'], 'L1_ffn_beta2': _L1_ffn_in['beta2'], 'L1_ffn_Wg': _L1_ffn_in['Wg'], 'L1_ffn_bg': _L1_ffn_in['bg'], 'L1_ffn_W1': _L1_ffn_in['W1'], 'L1_ffn_b1': _L1_ffn_in['b1'], 'L1_ffn_W2': _L1_ffn_in['W2'], 'L1_ffn_b2': _L1_ffn_in['b2']}

def reference(x, src, dst, edge_attr_64, L0_gnn_Wq, L0_gnn_bq, L0_gnn_Wk, L0_gnn_bk, L0_gnn_Wv, L0_gnn_bv, L0_gnn_Wskip, L0_gnn_bskip, L0_gnn_Wlin, L0_gnn_blin, L0_gnn_gamma, L0_gnn_beta, L0_ffn_gate_w, L0_ffn_thr_w, L0_ffn_fc1_w, L0_ffn_lora_A, L0_ffn_lora_B, L0_ffn_fc2_w, L1_gnn_u, L1_gnn_W1, L1_gnn_b1, L1_gnn_W2, L1_gnn_b2, L1_ffn_Wq, L1_ffn_bq, L1_ffn_Wk, L1_ffn_bk, L1_ffn_Wv, L1_ffn_bv, L1_ffn_Wo, L1_ffn_bo, L1_ffn_g1, L1_ffn_beta1, L1_ffn_g2, L1_ffn_beta2, L1_ffn_Wg, L1_ffn_bg, L1_ffn_W1, L1_ffn_b1, L1_ffn_W2, L1_ffn_b2):
    import jax
    import jax.numpy as jnp

    def _L0_gnn_ref(x, edge_index, Wq, bq, Wk, bk, Wv, bv, Wskip, bskip, Wlin, blin, gamma, beta):
        import jax, jax.numpy as jnp
        import numpy as np
        N, IN_DIM, OUT_DIM, H = (1024, 512, 512, 4)
        E = 16384
        HC = H * OUT_DIM
        n = x.shape[0]
        src, dst = (edge_index[0], edge_index[1])
        q = (x @ Wq + bq).reshape(n, H, OUT_DIM)
        k = (x @ Wk + bk).reshape(n, H, OUT_DIM)
        v = (x @ Wv + bv).reshape(n, H, OUT_DIM)
        alpha = jnp.einsum('ehc,ehc->eh', q[dst], k[src]) / np.sqrt(OUT_DIM)
        amax = jax.ops.segment_max(alpha, dst, num_segments=n)
        ex = jnp.exp(alpha - amax[dst])
        denom = jax.ops.segment_sum(ex, dst, num_segments=n)
        attn = ex / denom[dst]
        msg = attn[:, :, None] * v[src]
        agg = jax.ops.segment_sum(msg, dst, num_segments=n).reshape(n, HC)
        x_attn = agg + x @ Wskip + bskip
        x_lin = x_attn @ Wlin + blin
        h = x_lin + x_attn[:, :OUT_DIM]
        mu = jnp.mean(h, axis=-1, keepdims=True)
        var = jnp.mean((h - mu) ** 2, axis=-1, keepdims=True)
        return gamma * (h - mu) / jnp.sqrt(var + 1e-05) + beta

    def _L0_ffn_ref(x, gate_w, thr_w, fc1_w, lora_A, lora_B, fc2_w):
        import jax, jax.numpy as jnp
        import numpy as np
        B, T, H = (8, 1024, 512)
        E, R = (4, 16)
        SCALE = 0.04
        b, t, h = x.shape
        e = gate_w.shape[0]
        xf = x.reshape(-1, h)
        gate_logits = jax.nn.softmax(xf @ gate_w.T, axis=-1)
        thresholds = jax.nn.sigmoid(xf @ thr_w.T) * (1.0 / e)
        adapted = gate_logits - thresholds
        selected = (adapted >= 0).astype(xf.dtype)
        weights = adapted * selected
        wsum = jnp.sum(weights, axis=-1, keepdims=True)
        wsum = jnp.where(wsum == 0, jnp.ones_like(wsum), wsum)
        weights = weights / wsum
        hidden = jax.nn.relu(jnp.einsum('ni,ehi->neh', xf, fc1_w))
        lo = jnp.einsum('neh,ehr->ner', hidden, lora_A)
        lo = jnp.einsum('ner,ero->neo', lo, lora_B)
        expert_out = jnp.einsum('neo,edo->ned', lo, fc2_w)
        out = jnp.einsum('ne,ned->nd', weights, expert_out)
        return out.reshape(b, t, h)

    def _L1_gnn_ref(x, edge_index, edge_attr, u, batch, W1, b1, W2, b2):
        import jax, jax.numpy as jnp
        import numpy as np
        N_NODES = 6250
        N_EDGES = 100000
        NODE_IN = 512
        EDGE_IN = 64
        HID = 1024
        col = edge_index[1]
        summed = jax.ops.segment_sum(edge_attr, col, num_segments=x.shape[0])
        count = jax.ops.segment_sum(jnp.ones((edge_attr.shape[0],), dtype=x.dtype), col, num_segments=x.shape[0])
        agg = summed / jnp.maximum(count, 1.0)[:, None]
        h = jnp.concatenate([x, agg], axis=-1)
        h = jax.nn.relu(h @ W1 + b1)
        return x + h @ W2 + b2

    def _L1_ffn_ref(x, Wq, bq, Wk, bk, Wv, bv, Wo, bo, g1, beta1, g2, beta2, Wg, bg, W1, b1, W2, b2):
        import jax, jax.numpy as jnp
        import numpy as np
        D, NH, HID, E = (512, 8, 256, 8)
        EPS = 1e-05

        def _layernorm(x, g, b):
            mu = jnp.mean(x, axis=-1, keepdims=True)
            var = jnp.mean(jnp.square(x - mu), axis=-1, keepdims=True)
            return (x - mu) * jax.lax.rsqrt(var + EPS) * g + b
        B, S, _ = x.shape
        dh = D // NH
        q = (x @ Wq + bq).reshape(B, S, NH, dh)
        k = (x @ Wk + bk).reshape(B, S, NH, dh)
        v = (x @ Wv + bv).reshape(B, S, NH, dh)
        scores = jnp.einsum('bqhd,bkhd->bhqk', q, k) / jnp.sqrt(jnp.float32(dh)).astype(x.dtype)
        attn = jax.nn.softmax(scores, axis=-1)
        ctx = jnp.einsum('bhqk,bkhd->bqhd', attn, v).reshape(B, S, D)
        sa = ctx @ Wo + bo
        x = _layernorm(x + sa, g1, beta1)
        t = x.reshape(-1, D)
        logits = t @ Wg + bg
        idx = jnp.argmax(logits, axis=-1)
        h = jax.nn.gelu(jnp.einsum('td,edh->teh', t, W1) + b1, approximate=False)
        y = jnp.einsum('teh,ehd->ted', h, W2) + b2
        onehot = jax.nn.one_hot(idx, E, dtype=t.dtype)
        moe = jnp.einsum('ted,te->td', y, onehot).reshape(B, S, D)
        return _layernorm(x + moe, g2, beta2)
    edge_index = jnp.stack([src, dst])
    batch0 = jnp.zeros((1250,), jnp.int32)
    x = x + _L0_gnn_ref(_layernorm(x, axis=-1), edge_index, L0_gnn_Wq, L0_gnn_bq, L0_gnn_Wk, L0_gnn_bk, L0_gnn_Wv, L0_gnn_bv, L0_gnn_Wskip, L0_gnn_bskip, L0_gnn_Wlin, L0_gnn_blin, L0_gnn_gamma, L0_gnn_beta)
    x = x + _L0_ffn_ref(_layernorm(x, axis=-1)[None], L0_ffn_gate_w, L0_ffn_thr_w, L0_ffn_fc1_w, L0_ffn_lora_A, L0_ffn_lora_B, L0_ffn_fc2_w)[0]
    x = x + _L1_gnn_ref(_layernorm(x, axis=-1), edge_index, edge_attr_64, L1_gnn_u, batch0, L1_gnn_W1, L1_gnn_b1, L1_gnn_W2, L1_gnn_b2)
    x = x + _L1_ffn_ref(_layernorm(x, axis=-1)[None], L1_ffn_Wq, L1_ffn_bq, L1_ffn_Wk, L1_ffn_bk, L1_ffn_Wv, L1_ffn_bv, L1_ffn_Wo, L1_ffn_bo, L1_ffn_g1, L1_ffn_beta1, L1_ffn_g2, L1_ffn_beta2, L1_ffn_Wg, L1_ffn_bg, L1_ffn_W1, L1_ffn_b1, L1_ffn_W2, L1_ffn_b2)[0]
    return x

_drawn_inputs = setup_inputs


def setup_inputs(seed=0):
    import zlib

    import numpy as np

    out = dict(_drawn_inputs(seed))
    spreads = {'L0_gnn_bq': (0.0, 0.383),
     'L0_gnn_bk': (0.0, 0.8),
     'L0_gnn_bv': (0.0, 0.1),
     'L0_gnn_bskip': (0.0, 0.1),
     'L0_gnn_blin': (0.0, 0.1),
     'L0_gnn_gamma': (1.0, 0.2),
     'L0_gnn_beta': (0.0, 0.1),
     'L1_gnn_u': (0.0, 0.1),
     'L1_gnn_b1': (0.0, 0.286),
     'L1_gnn_b2': (0.0, 0.1),
     'L1_ffn_bq': (0.0, 0.8),
     'L1_ffn_bk': (0.0, 0.8),
     'L1_ffn_bv': (0.0, 0.513),
     'L1_ffn_bo': (0.0, 0.1),
     'L1_ffn_g1': (1.0, 0.2),
     'L1_ffn_beta1': (0.0, 0.1),
     'L1_ffn_g2': (1.0, 0.2),
     'L1_ffn_beta2': (0.0, 0.28),
     'L1_ffn_bg': (0.0, 0.356),
     'L1_ffn_b1': (0.0, 0.8),
     'L1_ffn_b2': (0.0, 0.283)}
    factors = {'L0_ffn_thr_w': 8.0,
     'L1_ffn_Wq': 8.0,
     'L1_ffn_Wk': 8.0,
     'L1_ffn_Wv': 3.859,
     'L1_ffn_Wo': 2.686}
    for name, (base, spread) in spreads.items():
        noise = np.random.default_rng([zlib.crc32(name.encode()), seed]).standard_normal(out[name].shape)
        drawn = base * np.exp(spread * noise) if base else spread * noise
        out[name] = jnp.asarray(drawn.astype(out[name].dtype))
    for name, factor in factors.items():
        out[name] = (out[name] * factor).astype(out[name].dtype)
    return out
```

```python
from contextlib import ExitStack

import numpy as np
import concourse.bass as bass
from concourse import mybir

F32 = mybir.dt.float32
F32R = mybir.dt.float32r
BF16 = mybir.dt.bfloat16
F16 = mybir.dt.float16
U16 = mybir.dt.uint16
I32 = mybir.dt.int32
ALU = mybir.AluOpType
ACT = mybir.ActivationFunctionType
AX = mybir.AxisListType

N, D = 1250, 512
P = 125
NT = N // P
CH = 2 * P
NC = N // CH
KT = D // 128
EDGES = 21250
EP = EDGES // (2 * P)
EDGE_D = 64
PARTS = 3 * EDGE_D + 2
BANK = 512
SPANS = [(0, 512), (512, 1024), (1024, N)]
HEADS = 4
EPS = 1e-5
OFF = -1e30


class Tick:

    def __init__(self, first=0):
        self.base, self.n, self.kept = first, 0, []

    def step(self, k=1):
        self.n += k
        return self.base + self.n

    def enter(self, turn, per):
        self.kept.append((self.base, self.n, per))
        self.base, self.n = self.base + self.n + turn * per, 0

    def leave(self, turns):
        base, n, per = self.kept.pop()
        if self.n != per:
            raise AssertionError(f"a turn counts {self.n}, not {per}")
        self.base, self.n = base, n + turns * per


class Link(Tick):

    def __init__(self, eng, sem):
        super().__init__()
        self.eng, self.sem = eng, sem

    def on(self, eng):
        self.eng = eng
        return self

    def __call__(self, ins):
        ins.then_inc(self.sem, 1)
        self.eng.wait_ge(self.sem, self.step())


def bc(ap, t):
    return ap.rearrange("p (a n) -> p a n", a=1).broadcast_to([ap.shape[0], t, ap.shape[1]])


CREDITS = {"hot_free": 2, "count_copied": 2, "count_stored0": 16, "count_stored1": 16,
           "raw0_free": 1, "raw1_free": 1, "pp_free": 2, "pp_done": 1, "s_free": 1, "tp_free": 3, "tp_done": 6,
           "cnt_free0": 1, "cnt_free1": 1, "hid_free": 2, "lora_done": 2, "lw_ready": 1, "ffn_x_added": 2,
           "gh_bank_free": 2, "gh_lo_done": 2, "gnn_x_added": 2,
           "at_e_ready": 2, "at_pp_free": 2, "at_stored": 16,
           "moe_bank_free": 2, "moe_lo": 2, "moe_out_done": 2, "moe_added": 2}


class Core:

    def __init__(self, nc, stack):
        self.nc, self.stack = nc, stack
        self.bottom = -(-nc.sbuf_base // 128) * 128
        self.psum = stack.enter_context(nc.psum_tensor("psum", [128, 8, BANK], F32))
        self.link = Link(None, stack.enter_context(nc.semaphore("dve_link")))
        self.credits = {name: stack.enter_context(nc.semaphore(name)) for name in CREDITS}

    def at(self, name, shape, dtype, kb):
        return self.nc.alloc_sbuf_tensor_at(name, shape, dtype, offset=self.bottom + int(kb * 1024))

    def sem(self, name):
        return self.credits.get(name) or self.stack.enter_context(self.nc.semaphore(name))

    def bank(self, b):
        return self.psum[:, b, :]


def three_pass(nc, out, lhs, rhs, start, stop):
    (lh, ll), (rh, rl) = lhs, rhs
    nc.tensor.matmul(out, lh, rh, start=start, stop=False)
    nc.tensor.matmul(out, lh, rl, start=False, stop=False)
    return nc.tensor.matmul(out, ll, rh, start=False, stop=stop)


def layer_stats(nc, link, x, s, turn):
    for t in range(NT):
        link(nc.vector.bn_stats(s.stats[:, t, :], x[:, t, :]))
    for t in range(NT):
        link(nc.vector.bn_aggr(s.mv[:, t, :], s.stats[:, t, :]))
    nc.vector.tensor_scalar(s.ve[:], s.mv[:, :, 1], EPS, None, ALU.add).then_inc(s.var_ready, 1)
    link.eng.wait_ge(s.std_ready, turn)
    r, r2 = s.r, s.r2
    link(nc.vector.reciprocal(r[:], s.sd[:]))
    link(nc.vector.tensor_tensor(r2[:], r[:], r[:], ALU.mult))
    link(nc.vector.tensor_tensor(r2[:], r2[:], s.ve[:], ALU.mult))
    link(nc.vector.tensor_scalar(r2[:], r2[:], -0.5, 1.5, ALU.mult, ALU.add))
    link(nc.vector.tensor_tensor(r[:], r[:], r2[:], ALU.mult))


def normalise(nc, link, x, out, s, turn):
    layer_stats(nc, link, x, s, turn)
    for t in range(NT):
        link(nc.vector.tensor_scalar(out[:, t, :], x[:, t, :], s.mv[:, t, 0:1], s.r[:, t:t + 1],
                                     ALU.subtract, ALU.mult))


def affine(nc, link, x, out, s, turn, gain, shift, ready):
    layer_stats(nc, link, x, s, turn)
    for t in range(NT):
        nc.vector.scalar_tensor_tensor(x[:, t, :], x[:, t, :], s.mv[:, t, 0:1], gain[:], ALU.subtract, ALU.mult)
    link(nc.vector.memset(s.r2[:], 0.0))
    for t in range(NT):
        last = nc.vector.scalar_tensor_tensor(out[:, t, :], x[:, t, :], s.r[:, t:t + 1], shift[t], ALU.mult, ALU.add)
        if ready is None:
            link(last)
        else:
            last.then_inc(ready, 1)


class NormState:

    def __init__(self, core, kb):
        at = core.at
        self.stats = at("ln_stats", [P, NT, 6], F32, kb)
        self.mv = at("ln_mean_var", [P, NT, 2], F32, kb + 0.25)
        self.ve = at("ln_var_eps", [P, NT], F32, kb + 0.375)
        self.sd = at("ln_std", [P, NT], F32, kb + 0.5)
        self.r = at("ln_rstd", [P, NT], F32, kb + 0.625)
        self.r2 = at("ln_newton", [P, NT], F32, kb + 0.75)
        self.var_ready, self.std_ready = core.sem("ln_var_ready"), core.sem("ln_std_ready")
        self.turn = 0

    def root(self, nc, eng):
        self.root_at(nc, eng, self.turn)

    def root_at(self, nc, eng, turn):
        eng.wait_ge(self.var_ready, turn)
        nc.scalar.activation(self.sd[:], self.ve[:], ACT.Sqrt).then_inc(self.std_ready, 1)


def edge_ranges(core, g, dst_pairs, src_cols, dst_cols, x_in, attr_in):
    nc, at, sem = core.nc, core.at, core.sem
    base = 140
    g.src_i = at("src_i", [P, 2 * EP], I32, base)
    g.dst_i = at("dst_i", [P, 2 * EP], I32, base + 1)
    dst_p = at("dst_pairs", [EP, 2 * P], I32, base + 2)
    g.src_f = at("src_f", [P, 2 * EP], F32, base + 3)
    g.dst_f = at("dst_f", [P, 2 * EP], F32, base + 4)
    small = at("range_small", [128, 8], F32, base + 5)
    tile_first = at("tile_first", [128, NT], F32, base + 5.25)
    hit = at("hit", [128, NT], F32, base + 5.5)
    cand = at("cand", [128, 2 * NT], F32, base + 5.75)
    best = at("best", [128, 2 * NT], F32, base + 6)
    lohi_f = at("lohi_f", [128, 2 * NT], F32, base + 6.25)
    s_load, s_iota, s_cand, s_best = sem("edges_loaded"), sem("range_iota"), sem("range_cand"), sem("range_best")
    s_pool = sem("range_pool")
    g.node_i = at("node_ids_i", [128, N], I32, base + 7)
    g.ids_ready, g.x_loaded = sem("ids_ready"), sem("x_loaded")
    attr = at("edge_attr", [P, 2 * EP, EDGE_D], F32, 84)
    g.parts = at("edge_parts", [P, 2 * EP, PARTS], BF16, 12)
    HALF = EP
    halves = [slice(i * HALF, (i + 1) * HALF) for i in range(2)]
    attr_loaded = [sem("attr_loaded0"), sem("attr_loaded1")]
    part_ready, rest_ready = sem("part_ready"), sem("rest_ready")

    with nc.Block() as block:
        @block.sync
        def _(sp):
            for name, n in CREDITS.items():
                sp.sem_inc(core.credits[name], n)
            sp.dma_start(dst_p[:], dst_pairs).then_inc(s_load, 16)
            sp.dma_start(g.dst_i[:], dst_cols).then_inc(s_load, 16)
            sp.dma_start(g.src_i[:], src_cols).then_inc(s_load, 16)
            for i, h in enumerate(halves):
                sp.dma_start(attr[:, h, :], attr_in[:, h, :]).then_inc(attr_loaded[i], 16)
            sp.dma_start(g.x[:], x_in.rearrange("(t p) d -> p t d", p=P)).then_inc(g.x_loaded, 16)

        @block.gpsimd
        def _(pool):
            nc.gpsimd.memset(g.ident[:], 0.0).then_inc(s_pool, 1)
            nc.gpsimd.memset(cand[:], 0.0).then_inc(s_iota, 1)
            nc.gpsimd.iota(tile_first[:], pattern=[[P, NT]], base=0, channel_multiplier=0,
                           allow_small_or_imprecise_dtypes=True).then_inc(s_iota, 1)
            nc.gpsimd.iota(small[:, 0:1], pattern=[[0, 1]], base=1, channel_multiplier=1,
                           allow_small_or_imprecise_dtypes=True).then_inc(s_iota, 1)
            nc.gpsimd.iota(g.node_ids[:], pattern=[[1, N]], base=0, channel_multiplier=0,
                           allow_small_or_imprecise_dtypes=True).then_inc(g.ids_ready, 1)
            pool.wait_ge(s_pool, 1)
            nc.gpsimd.affine_select(out=g.ident[:], in_=g.ident[:], compare_op=ALU.not_equal, fill=1.0,
                                    base=0, pattern=[[-1, 128]], channel_multiplier=1).then_inc(s_pool, 1)
            pool.wait_ge(s_cand, 1)
            nc.gpsimd.partition_all_reduce(best[:], cand[:], 128, bass.bass_isa.ReduceOp.max).then_inc(s_best, 1)

        @block.scalar
        def _(act):
            for n in range(3):
                for i, h in enumerate(halves):
                    if n == 0:
                        act.wait_ge(attr_loaded[i], 16)
                    else:
                        act.wait_ge(rest_ready, 2 * (n - 1) + i + 1)
                    nc.scalar.activation(g.parts[:, h, n * EDGE_D:(n + 1) * EDGE_D], attr[:, h, :],
                                         ACT.Copy).then_inc(part_ready, 1)

        @block.vector
        def _(dve):
            link = core.link.on(dve)
            nc.vector.memset(g.parts[:, :, 3 * EDGE_D:], 1.0)
            dve.wait_ge(s_load, 48)
            dve.wait_ge(s_iota, 3)
            nc.vector.tensor_copy(g.dst_f[:], g.dst_i[:])
            nc.vector.tensor_copy(g.src_f[:], g.src_i[:])
            link(nc.vector.tensor_reduce(small[0:EP, 1:2], dst_p[:], AX.X, ALU.max))
            link(nc.vector.tensor_reduce(small[0:EP, 2:3], dst_p[:], AX.X, ALU.min))
            link(nc.vector.tensor_scalar(small[0:EP, 3:4], small[0:EP, 0:1], -1.0, EP + 1.0, ALU.mult, ALU.add))
            link(nc.vector.tensor_scalar(hit[0:EP, :], tile_first[0:EP, :], small[0:EP, 1:2], None, ALU.is_le))
            link(nc.vector.tensor_scalar(cand[0:EP, 0:NT], tile_first[0:EP, :], float(P), small[0:EP, 2:3],
                                         ALU.add, ALU.is_gt))
            link(nc.vector.tensor_tensor(hit[0:EP, :], hit[0:EP, :], cand[0:EP, 0:NT], ALU.mult))
            link(nc.vector.tensor_scalar(cand[0:EP, 0:NT], hit[0:EP, :], small[0:EP, 0:1], None, ALU.mult))
            nc.vector.tensor_scalar(cand[0:EP, NT:], hit[0:EP, :], small[0:EP, 3:4], None,
                                    ALU.mult).then_inc(s_cand, 1)
            dve.wait_ge(s_best, 1)
            hi, lo = lohi_f[:, NT:], lohi_f[:, 0:NT]
            link(nc.vector.tensor_scalar(hi, best[:, 0:NT], 1.0, None, ALU.max))
            link(nc.vector.tensor_scalar(lo, best[:, NT:], -1.0, float(EP), ALU.mult, ALU.add))
            link(nc.vector.tensor_scalar(cand[:, 0:NT], hi, -1.0, None, ALU.add))
            link(nc.vector.tensor_tensor(lo, lo, cand[:, 0:NT], ALU.min))
            link(nc.vector.tensor_copy(g.lohi[:], lohi_f[:]))
            for n in range(2):
                for i, h in enumerate(halves):
                    dve.wait_ge(part_ready, 2 * n + i + 1)
                    nc.vector.tensor_tensor(attr[:, h, :], attr[:, h, :], g.parts[:, h, n * EDGE_D:(n + 1) * EDGE_D],
                                            ALU.subtract).then_inc(rest_ready, 1)


def pair_range(eng, g, t):
    lo = eng.value_load(g.lohi[0:1, bass.ds(t, 1)], min_val=0, max_val=EP - 1)
    hi = eng.value_load(g.lohi[0:1, bass.ds(t + NT, 1)], min_val=1, max_val=EP)
    return lo, hi


def count_edges(core, g):
    nc, at, sem = core.nc, core.at, core.sem
    base = 84
    hot_src = at("hot_src", [P, 2, N], BF16, base)
    hot_dst = at("hot_dst", [P, 2, 128], BF16, base + 6)
    zero = at("zero_bf", [128, BANK], BF16, base + 7)
    sums = g.attr_sums
    out = at("counts_out", [P, 2, N], U16, base + 9)
    ready, free = sem("hot_ready"), sem("hot_free")
    tile_done = sem("count_tile_done")
    copied, zeroed = sem("count_copied"), sem("zeroed")
    stored = [sem("count_stored0"), sem("count_stored1")]
    rows = g.counts.rearrange("(t p) s -> t p s", p=P)

    with nc.Block() as block:
        @block.vector
        def _(dve):
            nc.vector.memset(zero[:], 0.0).then_inc(zeroed, 1)
            dve.wait_ge(g.ids_ready, 1)
            turn = dve.alloc_register("hot_turn_dve")
            dve.reg_mov(turn, 1)
            with dve.Fori(0, NT) as t:
                lo, hi = pair_range(dve, g, t)
                with dve.Fori(lo, hi) as j:
                    for a in range(2):
                        dve.wait_ge(free, turn)
                        dve.reg_add(turn, turn, 1)
                        nc.vector.tensor_scalar(hot_src[:, a, :], g.node_ids[0:P, :], g.src_f[:, bass.ds(2 * j + a, 1)],
                                                None, ALU.is_equal)
                        nc.vector.tensor_scalar(hot_dst[:, a, 0:P], g.node_ids[0:P, bass.ds(t * P, P)],
                                                g.dst_f[:, bass.ds(2 * j + a, 1)], None,
                                                ALU.is_equal).then_inc(ready, 1)

        @block.tensor
        def _(pe):
            pe.wait_ge(zeroed, 1)
            turn = pe.alloc_register("hot_turn_pe")
            pe.reg_mov(turn, 1)
            with pe.Fori(0, NT // 2) as t2:
                for par in range(2):
                    lo, hi = pair_range(pe, g, 2 * t2 + par)
                    acc = core.psum[0:P, 3 * par:3 * par + 3, :].rearrange("p b n -> p (b n)")
                    pe.wait_ge(copied, 2 * t2 + par + 1)
                    att = core.bank(6 + par)[0:P, 0:PARTS]
                    for a, b in SPANS:
                        nc.tensor.matmul(acc[:, a:b], zero[:, 0:P], zero[:, 0:b - a], start=True, stop=False)
                    nc.tensor.matmul(att, zero[:, 0:P], zero[:, 0:PARTS], start=True, stop=False)
                    with pe.Fori(lo, hi) as j:
                        for s in range(2):
                            pe.wait_ge(ready, turn)
                            pe.reg_add(turn, turn, 1)
                            for a, b in SPANS:
                                nc.tensor.matmul(acc[:, a:b], hot_dst[:, s, 0:P], hot_src[:, s, a:b],
                                                 start=False, stop=False)
                            last = nc.tensor.matmul(att, hot_dst[:, s, 0:P],
                                                    g.parts[:, bass.ds(2 * j + s, 1), :].rearrange("p a n -> p (a n)"),
                                                    start=False, stop=False)
                            last.then_inc(free, 1)
                    for a, b in SPANS:
                        nc.tensor.matmul(acc[:, a:b], zero[:, 0:P], zero[:, 0:b - a], start=False, stop=True)
                    last = nc.tensor.matmul(att, zero[:, 0:P], zero[:, 0:PARTS], start=False, stop=True)
                    last.then_inc(tile_done, 1)

        @block.scalar
        def _(act):
            with act.Fori(0, NT // 2) as t2:
                for par in range(2):
                    acc = core.psum[0:P, 3 * par:3 * par + 3, :].rearrange("p b n -> p (b n)")
                    act.wait_ge(tile_done, 2 * t2 + par + 1)
                    act.wait_ge(stored[par], 16 * t2 + 16)
                    nc.scalar.activation(sums[:, bass.ds(2 * t2 + par, 1), :].rearrange("p a n -> p (a n)"),
                                         core.bank(6 + par)[0:P, 0:PARTS], ACT.Copy)
                    nc.scalar.activation(out[:, par, :], acc[:, 0:N], ACT.Copy).then_inc(copied, 1)
            
        @block.sync
        def _(sp):
            with sp.Fori(0, NT // 2) as t2:
                for par in range(2):
                    sp.wait_ge(copied, 2 * t2 + par + 3)
                    sp.dma_start(rows[bass.ds(2 * t2 + par, 1), :, :].rearrange("a p s -> (a p) s"),
                                 out[:, par, :]).then_inc(stored[par], 16)
            for par in range(2):
                sp.wait_ge(stored[par], 16 * (NT // 2) + 16)


def f32(ap):
    return ap.bitcast(F32)


class Turned:

    def __init__(self, core):
        self.done, self.hi, self.lo = (core.sem(f"turned{x}") for x in ("", "_hi", "_lo"))
        self.before = -NT

    def again(self):
        self.before += NT
        return self

    def bank(self, core, t):
        return core.bank(t % 8)[:, 0:KT * P].rearrange("p (k n) -> p k n", k=KT)

    def tensor(self, core, pe, xs, ident):
        for t in range(NT):
            if t >= 8:
                pe.wait_ge(self.lo, self.before + t - 7)
            for k in range(KT):
                last = core.nc.tensor.transpose(self.bank(core, t)[:, k, :], xs[:, t, k * 128:(k + 1) * 128],
                                                ident[0:P, 0:P])
            last.then_inc(self.done, 1)

    def scalar(self, core, act, hi):
        for t in range(NT):
            act.wait_ge(self.done, self.before + t + 1)
            core.nc.scalar.activation(hi[:, :, t * P:(t + 1) * P], self.bank(core, t),
                                      ACT.Copy).then_inc(self.hi, 1)

    def vector(self, core, dve, hi, lo):
        for t in range(NT):
            dve.wait_ge(self.hi, self.before + t + 1)
            core.nc.vector.tensor_tensor(lo[:, :, t * P:(t + 1) * P], self.bank(core, t),
                                         f32(hi[:, :, t * P:(t + 1) * P]), ALU.subtract).then_inc(self.lo, 1)


def first_features(core, g, ln):
    nc, sem = core.nc, core.sem
    turned = g.turned.again()
    xs_ready, nm_hi = sem("f0_xs"), sem("f0_nm_hi")
    ln.turn += 1
    with nc.Block() as block:
        @block.vector
        def _(dve):
            link = core.link.on(dve)
            dve.wait_ge(g.x_loaded, 16)
            normalise(nc, link, g.x, g.xs, ln, ln.turn)
            link(nc.vector.memset(g.acc[:], 0.0))
            link(nc.vector.memset(g.gs_acc[:], 0.0))
            sums, cnt = g.attr_sums, g.attr_sums[:, :, 3 * EDGE_D:3 * EDGE_D + 1]
            link(nc.vector.tensor_tensor(g.agg[:], sums[:, :, 0:EDGE_D], sums[:, :, EDGE_D:2 * EDGE_D], ALU.add))
            link(nc.vector.tensor_tensor(g.agg[:], g.agg[:], sums[:, :, 2 * EDGE_D:3 * EDGE_D], ALU.add))
            link(nc.vector.tensor_scalar(cnt, cnt, 1.0, None, ALU.max))
            link(nc.vector.reciprocal(cnt, cnt))
            link(nc.vector.tensor_tensor(g.agg[:], g.agg[:], cnt.broadcast_to([P, NT, EDGE_D]), ALU.mult))
            link(nc.vector.memset(g.gcol[:], 0.0))
            link(nc.vector.memset(g.headflag[:], 0.0))
            nc.vector.memset(g.headflag[:, 0:1], 1.0).then_inc(xs_ready, 1)
            dve.wait_ge(nm_hi, 1)
            nc.vector.tensor_tensor(g.xn_lo[:], g.xs[:], f32(g.xn_hi[:]), ALU.subtract)
            turned.vector(core, dve, g.xt_hi, g.xt_lo)

        @block.scalar
        def _(act):
            ln.root(nc, act)
            act.wait_ge(xs_ready, 1)
            nc.scalar.activation(g.xn_hi[:], g.xs[:], ACT.Copy).then_inc(nm_hi, 1)
            turned.scalar(core, act, g.xt_hi)

        @block.tensor
        def _(pe):
            pe.wait_ge(xs_ready, 1)
            turned.tensor(core, pe, g.xs, g.ident)


def graph_attention(core, g, w):
    nc, at, sem = core.nc, core.at, core.sem
    scale = 1.0 / np.sqrt(float(D)).item()
    m_hi, m_lo = at("qk_hi", [128, KT, D], F32R, 112), at("qk_lo", [128, KT, D], F32R, 120)
    g_hi, g_lo = at("vl_hi", [128, KT, D], F32R, 128), at("vl_lo", [128, KT, D], F32R, 136)
    g.g_hi, g.g_lo = g_hi, g_lo
    raw1 = at("raw1", [128, KT, D], F32, 152)
    R = 160
    a_hi, a_lo = at("prep_a_hi", [128, KT, D], F32R, R), at("prep_a_lo", [128, KT, D], F32R, R + 8)
    b_hi, b_lo = at("prep_b_hi", [128, KT, D], F32R, R + 16), at("prep_b_lo", [128, KT, D], F32R, R + 24)
    raw0 = at("raw0", [128, KT, D], F32, R + 32)
    t_hi, t_lo = at("t_hi", [128, KT, CH], F32R, R), at("t_lo", [128, KT, CH], F32R, R + 4)
    yt_hi, yt_lo = at("yt_hi", [128, KT, CH], F32R, R), at("yt_lo", [128, KT, CH], F32R, R + 4)
    pt_hi, pt_lo = at("pt_hi", [P, NT, CH], F32R, R + 8), at("pt_lo", [P, NT, CH], F32R, R + 18)
    prob = at("prob", [P, 2, N], F32, R + 28)
    cnt = at("cnt", [P, 2, N], U16, R + 38)
    maskb = at("maskb", [P, N], BF16, R + 43)
    S = 6
    ubc = at("ubc", [P, D], F32, S)
    junk = at("junk", [P, D], F32, S - 2)
    bkrep = at("bkrep", [128, KT, 128], F32, 205.5)
    tcol = at("tcol", [128, KT], F32, g.small)
    bqbk = at("bqbk", [P, 1], F32, g.small + .0625)
    cd = at("cd", [P, NT], F32, g.small + .125)
    mx, mxc, nb = (at(n, [P, 2], F32, g.small + .25 + i / 32) for i, n in enumerate(("mx", "mxc", "nb")))
    den, rden = (at(n, [P, 2], F32, g.small + .375 + i / 32) for i, n in enumerate(("den", "rden")))
    bq, bk = at("bq_cols", [128, HEADS * KT], F32, g.small + .5), at("bk_cols", [128, HEADS * KT], F32, g.small + .5625)
    bvs = at("bvs_cols", [128, 2, HEADS * KT], F32, g.small + .625)

    cols = sem("bias_cols_loaded")
    wl0, wl1, raw0_free, raw1_free = sem("raw0_loaded"), sem("raw1_loaded"), sem("raw0_free"), sem("raw1_free")
    split_hi, lin_ready = sem("split_hi"), sem("lin_ready")
    pp_done, pp_free, pp_hi = sem("pp_done"), sem("pp_free"), sem("pp_hi")
    bkrep_ready = sem("bkrep_ready")
    s_done, s_free, m_ready, e_ready = sem("s_done"), sem("s_free"), sem("m_ready"), sem("e_ready")
    p_ready = sem("p_ready")
    tp_done, tp_hi, tp_free = sem("tp_done"), sem("tp_hi"), sem("tp_free")
    cl, c_free = [sem("cnt_loaded0"), sem("cnt_loaded1")], [sem("cnt_free0"), sem("cnt_free1")]

    UNITS = 66
    bank = lambda u: core.bank(6 + u % 2)
    score = core.psum[0:P, 0:3, :].rearrange("p b n -> p (b n)")
    SPLITS = 5
    A, B = (a_hi, a_lo), (b_hi, b_lo)
    rows = g.counts.rearrange("(t p) s -> t p s", p=P)
    PIECES = [(0, 4), (4, 8), (8, 10)]

    def piece(q):
        j0, j1 = PIECES[q]
        return core.bank(3 + q)[0:P, 0:(j1 - j0) * P].rearrange("p (j n) -> p j n", n=P)

    def wview(ap, h):
        return ap.rearrange("(h k p) n -> h p k n", p=128, k=KT)[bass.ds(h, 1)].rearrange("a p k n -> (a p) k n")

    with nc.Block() as block:
        @block.sync
        def _(sp):
            for ap, dst in ((w["bq"], bq[:]), (w["bk"], bk[:])):
                sp.dma_start(dst, ap).then_inc(cols, 16)
            sp.dma_start(bvs[:, 0, :], w["bv"]).then_inc(cols, 16)
            sp.dma_start(bvs[:, 1, :], w["bskip"]).then_inc(cols, 16)
            with sp.Fori(0, HEADS) as h:
                sp.wait_ge(tp_done, 6 + 6 * NC * h)
                sp.wait_ge(raw0_free, 3 * h + 1)
                sp.dma_start(raw0[:], wview(w["WqT"], h)).then_inc(wl0, 16)
                sp.wait_ge(raw1_free, 2 * h + 1)
                sp.dma_start(raw1[:], wview(w["WkT"], h)).then_inc(wl1, 16)
                sp.wait_ge(raw0_free, 3 * h + 2)
                sp.wait_ge(pp_done, UNITS * h + 2)
                sp.dma_start(raw0[:], wview(w["WvT"], h)).then_inc(wl0, 16)
                sp.wait_ge(pp_free, 2 + UNITS * h + 3)
                sp.dma_start(raw1[:], wview(w["Wlin"], h)).then_inc(wl1, 16)
                sp.wait_ge(raw0_free, 3 * h + 3)
                sp.dma_start(raw0[:], wview(w["WskipT"], h)).then_inc(wl0, 16)
                with sp.Fori(0, NC) as c:
                    for s in range(2):
                        sp.wait_ge(raw0_free, 3 * h + 4)
                        sp.wait_ge(c_free[s], NC * h + c + 1)
                        sp.dma_start(cnt[:, s, :], rows[bass.ds(2 * c + s, 1), :, :].rearrange("a p s -> (a p) s")
                                     ).then_inc(cl[s], 16)

        @block.scalar
        def _(act):
            pp, tp, sub = Tick(), Tick(), Tick()

            def split_in(loaded, value, dst, src):
                act.wait_ge(loaded, value)
                nc.scalar.activation(dst[:], src[:], ACT.Copy).then_inc(split_hi, 1)

            def unit_to(dst, rows_=128, n=D, bias=None):
                act.wait_ge(pp_done, 1 + pp.step())
                src = bank((pp.n - 1))[0:rows_, 0:n]
                if bias is None:
                    ins = nc.scalar.activation(dst, src, ACT.Copy)
                else:
                    ins = nc.scalar.activation(dst, src, ACT.Identity, bias=bias)
                ins.then_inc(pp_hi, 1)

            def t_units():
                for m in range(KT):
                    unit_to(t_hi[:, m, :], n=CH, bias=tcol[:, m:m + 1])

            def exps():
                for s in range(2):
                    act.wait_ge(m_ready, sub.step())
                    nc.scalar.activation(prob[:, s, :], prob[:, s, :], ACT.Exp, bias=nb[:, s:s + 1],
                                         scale=scale).then_inc(e_ready, 1)

            def y_units():
                for m in range(KT):
                    unit_to(yt_hi[:, m, :], n=CH)

            def turn_hi(s):
                for q, (j0, j1) in enumerate(PIECES):
                    act.wait_ge(tp_done, 6 + tp.step())
                    nc.scalar.activation(pt_hi[:, j0:j1, s * P:(s + 1) * P], piece(q), ACT.Copy).then_inc(tp_hi, 1)

            with act.Fori(0, HEADS) as h:
                pp.enter(h, UNITS), tp.enter(h, 6 * NC), sub.enter(h, 2 * NC)
                act.wait_ge(pp_done, UNITS * h + 1)
                split_in(wl0, 48 * h + 16, a_hi, raw0)
                split_in(wl1, 32 * h + 16, b_hi, raw1)
                pp.step(3)
                for m in range(KT):
                    unit_to(m_hi[:, m, :])
                split_in(wl0, 48 * h + 32, a_hi, raw0)
                split_in(lin_ready, h + 1, b_hi, raw1)
                pp.step(1)
                for m in range(KT):
                    unit_to(g_hi[:, m, :])
                split_in(wl0, 48 * h + 48, a_hi, raw0)
                pp.step(KT)
                act.wait_ge(pp_done, 1 + pp.base + pp.n)
                t_units()
                exps()
                turn_hi(0), turn_hi(1)
                with act.Fori(1, NC) as c:
                    pp.enter(c - 1, 10), tp.enter(c - 1, 6), sub.enter(c - 1, 2)
                    t_units()
                    exps()
                    y_units()
                    turn_hi(0)
                    pp.step(2)
                    turn_hi(1)
                    pp.leave(NC - 1), tp.leave(NC - 1), sub.leave(NC - 1)
                y_units()
                pp.step(2)
                pp.leave(HEADS), tp.leave(HEADS), sub.leave(HEADS)

        @block.vector
        def _(dve):
            link = core.link.on(dve)
            pp, tp, sub, hi, sp_hi = Tick(), Tick(), Tick(), Tick(), Tick()

            def split_lo(dst_hi, dst_lo, src, free):
                dve.wait_ge(split_hi, sp_hi.step())
                nc.vector.tensor_tensor(dst_lo[:], src[:], f32(dst_hi[:]), ALU.subtract).then_inc(free, 1)

            def unit():
                v = pp.step()
                return v, bank(pp.n - 1)

            def unit_lo(dst_hi, dst_lo, n=D, bias=None):
                _, b = unit()
                dve.wait_ge(pp_hi, hi.step())
                if bias is None:
                    ins = nc.vector.tensor_tensor(dst_lo, b[:, 0:n], f32(dst_hi), ALU.subtract)
                else:
                    ins = nc.vector.scalar_tensor_tensor(dst_lo, b[:, 0:n], bias, f32(dst_hi), ALU.add, ALU.subtract)
                ins.then_inc(pp_free, 1)

            def t_units():
                for m in range(KT):
                    unit_lo(t_hi[:, m, :], t_lo[:, m, :], CH, tcol[:, m:m + 1])

            def y_units():
                for m in range(KT):
                    unit_lo(yt_hi[:, m, :], yt_lo[:, m, :], CH)

            def softmax(c, it):
                for s in range(2):
                    v = sub.step()
                    tile = 2 * c + s
                    dve.wait_ge(cl[s], 16 * it + 16)
                    link(nc.vector.tensor_scalar(maskb[:], cnt[:, s, :], 0.0, OFF, ALU.is_equal, ALU.mult))
                    dve.wait_ge(tp_done, 3 * v)
                    dve.wait_ge(s_done, v)
                    nc.vector.memset(mxc[:, s:s + 1], 0.0)
                    nc.vector.tensor_tensor_reduce(out=prob[:, s, :], in0=score[:, 0:N], in1=maskb[:], scale=1.0,
                                                   scalar=-3e38, op0=ALU.add, op1=ALU.max,
                                                   accum_out=mx[:, s:s + 1]).then_inc(s_free, 1)
                    dve.wait_ge(s_free, v + 1)
                    link(nc.vector.tensor_tensor(mxc[:, s:s + 1], mx[:, s:s + 1], cd[:, bass.ds(tile, 1)], ALU.add))
                    nc.vector.tensor_scalar(nb[:, s:s + 1], mxc[:, s:s + 1], cd[:, bass.ds(tile, 1)], -scale,
                                            ALU.subtract, ALU.mult).then_inc(m_ready, 1)
                    dve.wait_ge(e_ready, v)
                    nc.vector.tensor_tensor_reduce(out=prob[:, s, :], in0=prob[:, s, :], in1=cnt[:, s, :], scale=1.0,
                                                   scalar=0.0, op0=ALU.mult, op1=ALU.add,
                                                   accum_out=den[:, s:s + 1]).then_inc(c_free[s], 1)
                    dve.wait_ge(c_free[s], it + 2)
                    link(nc.vector.tensor_scalar(g.has_edge[:, bass.ds(tile, 1)], den[:, s:s + 1], 0.5, None, ALU.is_ge))
                    link(nc.vector.tensor_scalar(den[:, s:s + 1], den[:, s:s + 1], 0.5, None, ALU.max))
                    link(nc.vector.reciprocal(rden[:, s:s + 1], den[:, s:s + 1]))
                    nc.vector.tensor_scalar(prob[:, s, :], prob[:, s, :], rden[:, s:s + 1], None,
                                            ALU.mult).then_inc(p_ready, 1)

            def turn_lo(s):
                for q, (j0, j1) in enumerate(PIECES):
                    dve.wait_ge(tp_hi, tp.step())
                    nc.vector.tensor_tensor(pt_lo[:, j0:j1, s * P:(s + 1) * P], piece(q),
                                            f32(pt_hi[:, j0:j1, s * P:(s + 1) * P]), ALU.subtract).then_inc(tp_free, 1)

            def add_out(c):
                for s in range(2):
                    v, b = unit()
                    dve.wait_ge(pp_done, 1 + v)
                    dst = g.acc[:, bass.ds(2 * c + s, 1), :].rearrange("p a n -> p (a n)")
                    nc.vector.tensor_tensor(dst, dst, b[0:P, :], ALU.add).then_inc(pp_free, 1)

            dve.wait_ge(cols, 64)
            with dve.Fori(0, HEADS) as h:
                pp.enter(h, UNITS), tp.enter(h, 6 * NC), sub.enter(h, 2 * NC), hi.enter(h, 8 + 8 * NC)
                link.enter(h, 20 + 10 * NC), sp_hi.enter(h, SPLITS)
                nc.vector.tensor_copy(bkrep[:], bk[:, bass.ds(KT * h, KT)].unsqueeze(2).broadcast_to([128, KT, 128])
                                      ).then_inc(bkrep_ready, 1)
                split_lo(a_hi, a_lo, raw0, raw0_free)
                split_lo(b_hi, b_lo, raw1, raw1_free)
                v, b = unit()
                dve.wait_ge(pp_done, 1 + v)
                nc.vector.tensor_copy(ubc[:], b[0:P, :]).then_inc(pp_free, 1)
                v, b = unit()
                dve.wait_ge(pp_done, 1 + v)
                nc.vector.tensor_copy(tcol[:], b[:, 0:KT]).then_inc(pp_free, 1)
                v, b = unit()
                dve.wait_ge(pp_done, 1 + v)
                nc.vector.tensor_copy(bqbk[:], b[0:P, 0:1]).then_inc(pp_free, 1)
                for m in range(KT):
                    unit_lo(m_hi[:, m, :], m_lo[:, m, :])
                dve.wait_ge(wl1, 32 * h + 32)
                for k in range(KT):
                    blk = raw1[:, k, k * 128:(k + 1) * 128]
                    last = nc.vector.scalar_tensor_tensor(blk, g.ident[:], g.headflag[:, bass.ds(h, 1)], blk,
                                                          ALU.mult, ALU.add)
                last.then_inc(lin_ready, 1)
                split_lo(a_hi, a_lo, raw0, raw0_free)
                split_lo(b_hi, b_lo, raw1, raw1_free)
                dve.wait_ge(pp_free, pp.base + 5)
                for t in range(NT):
                    link(nc.vector.tensor_tensor_reduce(out=junk[:], in0=f32(g.xn_hi[:, t, :]), in1=ubc[:], scale=1.0,
                                                        scalar=bqbk[:], op0=ALU.mult, op1=ALU.add,
                                                        accum_out=cd[:, t:t + 1]))
                    link(nc.vector.tensor_tensor_reduce(out=junk[:], in0=f32(g.xn_lo[:, t, :]), in1=ubc[:], scale=1.0,
                                                        scalar=cd[:, t:t + 1], op0=ALU.mult, op1=ALU.add,
                                                        accum_out=cd[:, t:t + 1]))
                v, b = unit()
                dve.wait_ge(pp_done, 1 + v)
                nc.vector.tensor_tensor(g.gcol[:], g.gcol[:], b[:, 0:2 * KT].rearrange("p (k i) -> p k i", i=2),
                                        ALU.add).then_inc(pp_free, 1)
                for m in range(KT):
                    unit_lo(g_hi[:, m, :], g_lo[:, m, :])
                split_lo(a_hi, a_lo, raw0, raw0_free)
                for m in range(KT):
                    v, b = unit()
                    dve.wait_ge(pp_done, 1 + v)
                    nc.vector.tensor_tensor(g.gs_acc[:, m, :], g.gs_acc[:, m, :], b, ALU.add).then_inc(pp_free, 1)
                t_units()
                softmax(0, NC * h)
                turn_lo(0), turn_lo(1)
                with dve.Fori(1, NC) as c:
                    pp.enter(c - 1, 10), tp.enter(c - 1, 6), sub.enter(c - 1, 2), hi.enter(c - 1, 8)
                    link.enter(c - 1, 10)
                    t_units()
                    softmax(c, NC * h + c)
                    y_units()
                    turn_lo(0)
                    add_out(c - 1)
                    turn_lo(1)
                    for x in (pp, tp, sub, hi, link):
                        x.leave(NC - 1)
                y_units()
                add_out(NC - 1)
                for x in (pp, tp, sub, hi, link, sp_hi):
                    x.leave(HEADS)

        @block.tensor
        def _(pe):
            pp, tp, sub = Tick(), Tick(), Tick()

            def unit():
                v = pp.step()
                pe.wait_ge(pp_free, v)
                return bank(pp.n - 1)

            def product(lhs, rhs):
                for m in range(KT):
                    out = unit()
                    for k in range(KT):
                        last = three_pass(nc, out, [x[:, k, m * 128:(m + 1) * 128] for x in lhs],
                                          [x[:, k, :] for x in rhs], k == 0, k == KT - 1)
                    last.then_inc(pp_done, 1)

            def t_units(c):
                for m in range(KT):
                    out = unit()
                    for k in range(KT):
                        last = three_pass(nc, out[:, 0:CH], [x[:, k, m * 128:(m + 1) * 128] for x in (m_hi, m_lo)],
                                          [x[:, k, bass.ds(CH * c, CH)] for x in (g.xt_hi, g.xt_lo)],
                                          k == 0, k == KT - 1)
                    last.then_inc(pp_done, 1)

            def scores():
                pe.wait_ge(pp_free, pp.base + pp.n + 2)
                for s in range(2):
                    pe.wait_ge(s_free, sub.step())
                    for a, b in SPANS:
                        for k in range(KT):
                            last = three_pass(nc, score[:, a:b], [x[:, k, s * P:(s + 1) * P] for x in (t_hi, t_lo)],
                                              [x[:, k, a:b] for x in (g.xt_hi, g.xt_lo)], k == 0, k == KT - 1)
                    last.then_inc(s_done, 1)

            def turn(s):
                v = tp.step()
                pe.wait_ge(p_ready, v)
                pe.wait_ge(tp_free, 3 * v)
                for q, (j0, j1) in enumerate(PIECES):
                    for j in range(j0, j1):
                        last = nc.tensor.transpose(piece(q)[:, j - j0, :], prob[:, s, j * P:(j + 1) * P],
                                                   g.ident[0:P, 0:P])
                    last.then_inc(tp_done, 1)

            def y_units():
                for m in range(KT):
                    out = unit()
                    for j in range(NT):
                        last = three_pass(nc, out[:, 0:CH], [x[:, j, m * 128:(m + 1) * 128] for x in (g.xn_hi, g.xn_lo)],
                                          [x[:, j, :] for x in (pt_hi, pt_lo)], j == 0, j == NT - 1)
                    last.then_inc(pp_done, 1)

            def out_units():
                pe.wait_ge(pp_free, pp.base + pp.n + 2)
                for s in range(2):
                    out = unit()
                    for k in range(KT):
                        last = three_pass(nc, out[0:P, :], [x[:, k, s * P:(s + 1) * P] for x in (yt_hi, yt_lo)],
                                          [x[:, k, :] for x in (g_hi, g_lo)], k == 0, k == KT - 1)
                    last.then_inc(pp_done, 1)

            pe.wait_ge(cols, 64)
            with pe.Fori(0, HEADS) as h:
                pp.enter(h, UNITS), tp.enter(h, 2 * NC), sub.enter(h, 2 * NC)
                pe.wait_ge(bkrep_ready, h + 1)
                pe.wait_ge(wl0, 48 * h + 16)
                out = unit()
                for k in range(KT):
                    last = nc.tensor.matmul(out[0:P, :], bkrep[:, k, 0:P], raw0[:, k, :], start=k == 0, stop=k == KT - 1)
                last.then_inc(pp_done, 1)
                pe.wait_ge(wl1, 32 * h + 16)
                out = unit()
                for m in range(KT):
                    for k in range(KT):
                        last = nc.tensor.matmul(out[:, m:m + 1], raw1[:, k, m * 128:(m + 1) * 128],
                                                bq[:, bass.ds(KT * h + k, 1)], start=k == 0, stop=k == KT - 1)
                last.then_inc(pp_done, 1)
                out = unit()
                for k in range(KT):
                    last = nc.tensor.matmul(out[0:P, 0:1], bkrep[:, k, 0:P], bq[:, bass.ds(KT * h + k, 1)],
                                            start=k == 0, stop=k == KT - 1)
                last.then_inc(pp_done, 1)
                pe.wait_ge(raw0_free, 3 * h + 2)
                pe.wait_ge(raw1_free, 2 * h + 2)
                product(A, B)
                pe.wait_ge(lin_ready, h + 1)
                out = unit()
                for m in range(KT):
                    for k in range(KT):
                        last = nc.tensor.matmul(out[:, 2 * m:2 * m + 2], raw1[:, k, m * 128:(m + 1) * 128],
                                                bvs[:, :, bass.ds(KT * h + k, 1)].rearrange("p i a -> p (i a)"),
                                                start=k == 0, stop=k == KT - 1)
                last.then_inc(pp_done, 1)
                pe.wait_ge(raw0_free, 3 * h + 3)
                pe.wait_ge(raw1_free, 2 * h + 3)
                product(A, B)
                pe.wait_ge(raw0_free, 3 * h + 4)
                product(A, B)
                t_units(0)
                scores()
                turn(0), turn(1)
                with pe.Fori(1, NC) as c:
                    pp.enter(c - 1, 10), tp.enter(c - 1, 2), sub.enter(c - 1, 2)
                    t_units(c)
                    scores()
                    pe.wait_ge(tp_free, 3 * (tp.base + tp.n) + 3)
                    y_units()
                    turn(0)
                    out_units()
                    turn(1)
                    for x in (pp, tp, sub):
                        x.leave(NC - 1)
                pe.wait_ge(tp_free, 3 * (tp.base + tp.n) + 3)
                y_units()
                out_units()
                for x in (pp, tp, sub):
                    x.leave(HEADS)


def row_view(ap, rows=P):
    return ap.rearrange("(a n) -> a n", a=1).broadcast_to([rows, ap.shape[0]])


def tiles(ap):
    return ap.rearrange("(t p) d -> p t d", p=P)


def graph_output(core, g, w, ln):
    nc, at, sem = core.nc, core.at, core.sem
    ones = at("ones_f", [128, P], F32, 170)
    diag = at("diag", [128, 2 * KT, 128], F32, 4)
    rows = at("bias_rows", [P, 2, D], F32, 160)
    gamma, beta, blin = (at(n, [P, D], F32, 164 + 2 * i) for i, n in enumerate(("gamma", "beta", "blin")))
    x = g.x
    loaded, x_in = sem("go_rows_loaded"), sem("go_x_loaded")
    gs_hi, gs_lo, diag_ready = sem("go_gs_hi"), sem("go_gs_lo"), sem("go_diag")
    row_done, row_free, done, free = sem("go_row_done"), sem("go_row_free"), sem("go_done"), sem("go_free")
    xb = sem("go_x_beta")
    ln.turn += 1
    turn = ln.turn
    with nc.Block() as block:
        @block.sync
        def _(sp):
            for dst, src in ((blin, w["blin"]), (gamma, w["gamma"]), (beta, w["beta"])):
                sp.dma_start(dst[:], row_view(src)).then_inc(loaded, 16)
            sp.dma_start(x[:], tiles(w["x"])).then_inc(x_in, 16)

        @block.gpsimd
        def _(pool):
            pool.wait_ge(loaded, 48)
            pool.wait_ge(x_in, 16)
            for t in range(NT):
                last = nc.gpsimd.tensor_tensor(x[:, t, :], x[:, t, :], beta[:], ALU.add)
            last.then_inc(xb, 1)

        @block.scalar
        def _(act):
            nc.scalar.activation(g.g_hi[:], g.gs_acc[:], ACT.Copy).then_inc(gs_hi, 1)
            ln.root(nc, act)

        @block.vector
        def _(dve):
            link = core.link.on(dve)
            nc.vector.memset(ones[:], 1.0)
            for i in range(2):
                for k in range(KT):
                    last = nc.vector.tensor_scalar(diag[:, i * KT + k, :], g.ident[:], g.gcol[:, k, i:i + 1], None,
                                                   ALU.mult)
            last.then_inc(diag_ready, 1)
            dve.wait_ge(gs_hi, 1)
            nc.vector.tensor_tensor(g.g_lo[:], g.gs_acc[:], f32(g.g_hi[:]), ALU.subtract).then_inc(gs_lo, 1)
            dve.wait_ge(row_done, 2)
            link(nc.vector.tensor_copy(rows[:, 0, :], core.bank(6)[0:P, :]))
            dve.wait_ge(loaded, 48)
            link(nc.vector.tensor_tensor(rows[:, 1, :], blin[:], core.bank(7)[0:P, :], ALU.add))
            for t in range(NT):
                last = nc.vector.scalar_tensor_tensor(g.acc[:, t, :], rows[:, 0, :], g.has_edge[:, t:t + 1],
                                                      g.acc[:, t, :], ALU.mult, ALU.add)
            link(last)
            link(nc.vector.tensor_tensor(g.acc[:], g.acc[:], rows[:, 1:2, :].broadcast_to([P, NT, D]), ALU.add))
            for t in range(NT):
                dve.wait_ge(done, t + 1)
                nc.vector.tensor_tensor(g.acc[:, t, :], g.acc[:, t, :], core.bank(t % 6)[0:P, :],
                                        ALU.add).then_inc(free, 1)
            dve.wait_ge(free, NT)
            layer_stats(nc, link, g.acc, ln, turn)
            for t in range(NT):
                nc.vector.scalar_tensor_tensor(g.acc[:, t, :], g.acc[:, t, :], ln.mv[:, t, 0:1], gamma[:],
                                               ALU.subtract, ALU.mult)
            link(nc.vector.memset(ln.r2[:], 0.0))
            dve.wait_ge(xb, 1)
            for t in range(NT):
                nc.vector.scalar_tensor_tensor(x[:, t, :], g.acc[:, t, :], ln.r[:, t:t + 1], x[:, t, :],
                                               ALU.mult, ALU.add)

        @block.tensor
        def _(pe):
            pe.wait_ge(diag_ready, 1)
            for i in range(2):
                for k in range(KT):
                    last = nc.tensor.matmul(core.bank(6 + i)[0:P, k * 128:(k + 1) * 128], ones[:],
                                            diag[:, i * KT + k, :], start=True, stop=True)
                last.then_inc(row_done, 1)
            pe.wait_ge(gs_lo, 1)
            for t in range(NT):
                if t >= 6:
                    pe.wait_ge(free, t - 5)
                for k in range(KT):
                    last = three_pass(nc, core.bank(t % 6)[0:P, :],
                                      [a[:, k, t * P:(t + 1) * P] for a in (g.xt_hi, g.xt_lo)],
                                      [a[:, k, :] for a in (g.g_hi, g.g_lo)], k == 0, k == KT - 1)
                last.then_inc(done, 1)


def expert_lora(core, g, w, ln):
    nc, at, sem = core.nc, core.at, core.sem
    NE, R = 4, 16
    x, xs = g.x, g.xs
    fc1_hi, fc1_lo = at("fc1_hi", [128, NE, KT, D], F32R, 92), at("fc1_lo", [128, NE, KT, D], F32R, 124)
    a_hi, a_lo = at("lora_a_hi", [128, NE, KT, 128], F32R, 156), at("lora_a_lo", [128, NE, KT, 128], F32R, 164)
    raw = [at(f"ffn_raw{i}", [128, KT, D], F32, 172 + 8 * i) for i in range(2)]
    wt, wrep = at("weights_t", [NE * R, N], F32, 172), at("weights_rep", [P, NT, NE, R], F32, 177)
    a_raw, b_raw = at("lora_a_raw", [128, NE, KT, R], F32, 188), at("lora_b_raw", [128, NE, KT, R], F32, 189)
    h_hi = [at(f"hid_hi{i}", [128, KT, CH], F32R, 188 + 8 * i) for i in range(2)]
    h_lo = [at(f"hid_lo{i}", [128, KT, CH], F32R, 192 + 8 * i) for i in range(2)]
    b_pad = at("lora_b_pad", [128, NE, KT, NE * R], F32, 4)
    f_sb = at("lora_f", [NE * R, D], F32, 204)
    lw = at("lora_weighted", [NE * R, CH], F32, 206)
    S = g.small
    gw = at("gate_cols", [128, KT, 6], F32, S)
    gw_hi, gw_lo = at("gate_hi", [128, KT, 6], F32R, S + .125), at("gate_lo", [128, KT, 6], F32R, S + .25)
    lg = at("gate_logits", [P, NT, 6], F32, S + .375)
    ex, wgt = at("gate_exp", [P, NT, 6], F32, S + .625), at("gate_weight", [P, NT, NE], F32, S + .875)
    m1, m2 = at("gate_m1", [P, NT, 1], F32, S + 1.0625), at("gate_m2", [P, NT, 1], F32, S + 1.125)

    small_in, raw_in = sem("ffn_small_in"), [sem("ffn_raw_in0"), sem("ffn_raw_in1")]
    raw_free = [sem("ffn_raw_free0"), sem("ffn_raw_free1")]
    xs_ready, hi_done = sem("ffn_xs"), sem("ffn_hi_done")
    small_hi, pads, small_lo = sem("ffn_small_hi"), sem("ffn_pads"), sem("ffn_small_lo")
    gl_done, gl_ready, ex_ready, wrep_ready, wt_done = (
        sem(f"ffn_{n}") for n in ("gl_done", "gl_ready", "ex_ready", "wrep", "wt_done"))
    start = sem("ffn_prepared")
    u_done, u_hi, u_free = sem("hid_done"), sem("hid_hi_done"), sem("hid_free")
    lora_done, lw_ready, out_done, x_added = sem("lora_done"), sem("lw_ready"), sem("ffn_out_done"), sem("ffn_x_added")
    turned = g.turned.again()
    ln.turn += 1
    turn = ln.turn
    bank = lambda u: core.bank(6 + u % 2)
    UNITS = NE * KT

    with nc.Block() as block:
        @block.sync
        def _(sp):
            sp.dma_start(gw[:], w["gates"]).then_inc(small_in, 16)
            sp.dma_start(a_raw[:], w["lora_A"]).then_inc(small_in, 16)
            sp.dma_start(b_raw[:], w["lora_B"]).then_inc(small_in, 16)
            for i in range(2 * NE):
                if i >= 2:
                    sp.wait_ge(raw_free[i % 2], i // 2)
                src = (w["fc1T"], w["fc2T"])[i // NE][i % NE].rearrange("(k p) n -> p k n", p=128)
                sp.dma_start(raw[i % 2][:], src).then_inc(raw_in[i % 2], 16)

        @block.scalar
        def _(act):
            ln.root(nc, act)
            act.wait_ge(small_in, 48)
            act.wait_ge(pads, 1)
            nc.scalar.activation(gw_hi[:], gw[:], ACT.Copy)
            for e in range(NE):
                last = nc.scalar.activation(a_hi[:, e, :, R * e:R * e + R], a_raw[:, e, :, :], ACT.Copy)
            last.then_inc(small_hi, 1)
            for e in range(NE):
                act.wait_ge(raw_in[e % 2], 16 * (e // 2 + 1))
                nc.scalar.activation(fc1_hi[:, e, :, :], raw[e % 2][:], ACT.Copy).then_inc(hi_done, 1)
            turned.scalar(core, act, g.xt_hi)
            act.wait_ge(gl_ready, 1)
            nc.scalar.activation(ex[:, :, 0:4], lg[:, :, 0:4], ACT.Exp)
            nc.scalar.activation(ex[:, :, 4:5], lg[:, :, 4:5], ACT.Exp, scale=-1.0).then_inc(ex_ready, 1)
            pp = Tick()
            act.wait_ge(start, 1)
            with act.Fori(0, NC) as c:
                pp.enter(c, UNITS)
                for e in range(NE):
                    act.wait_ge(lora_done, NE * c + e + 1)
                    for m in range(KT):
                        act.wait_ge(u_done, pp.step())
                        nc.scalar.activation(h_hi[e % 2][:, m, :], bank(m)[:, 0:CH], ACT.Relu).then_inc(u_hi, 1)
                pp.leave(NC)

        @block.vector
        def _(dve):
            link = core.link.on(dve)
            nc.vector.memset(f32(a_hi[:]), 0.0)
            nc.vector.memset(f32(a_lo[:]), 0.0)
            nc.vector.memset(b_pad[:], 0.0).then_inc(pads, 1)
            normalise(nc, link, x, xs, ln, turn)
            dve.sem_inc(xs_ready, 1)
            dve.wait_ge(small_hi, 1)
            nc.vector.tensor_tensor(gw_lo[:], gw[:], f32(gw_hi[:]), ALU.subtract)
            for e in range(NE):
                cols = slice(R * e, R * e + R)
                nc.vector.tensor_tensor(a_lo[:, e, :, cols], a_raw[:, e, :, :], f32(a_hi[:, e, :, cols]), ALU.subtract)
            for e in range(NE):
                last = nc.vector.tensor_copy(b_pad[:, e, :, R * e:R * e + R], b_raw[:, e, :, :])
            last.then_inc(small_lo, 1)
            for e in range(NE):
                dve.wait_ge(hi_done, e + 1)
                nc.vector.tensor_tensor(fc1_lo[:, e, :, :], raw[e % 2][:], f32(fc1_hi[:, e, :, :]),
                                        ALU.subtract).then_inc(raw_free[e % 2], 1)
            turned.vector(core, dve, g.xt_hi, g.xt_lo)
            dve.wait_ge(raw_free[1], 4)
            link(nc.vector.tensor_copy(f_sb[:], core.bank(1)[0:NE * R, :]))
            dve.wait_ge(gl_done, 1)
            gl = core.bank(0)[0:P, 0:NT * 8].rearrange("p (t e) -> p t e", e=8)
            link(nc.vector.tensor_copy(lg[:], gl[:, :, 0:6]))
            link(nc.vector.tensor_reduce(m1[:], lg[:, :, 0:4], AX.X, ALU.max))
            nc.vector.tensor_tensor(lg[:, :, 0:4], lg[:, :, 0:4], m1[:].broadcast_to([P, NT, 4]),
                                    ALU.subtract).then_inc(gl_ready, 1)
            dve.wait_ge(ex_ready, 1)
            link(nc.vector.tensor_reduce(m1[:], ex[:, :, 0:4], AX.X, ALU.add))
            link(nc.vector.reciprocal(m1[:], m1[:]))
            link(nc.vector.tensor_tensor(wgt[:], ex[:, :, 0:4], m1[:].broadcast_to([P, NT, 4]), ALU.mult))
            link(nc.vector.tensor_scalar(m2[:], ex[:, :, 4:5], 1.0, None, ALU.add))
            link(nc.vector.reciprocal(m2[:], m2[:]))
            link(nc.vector.tensor_scalar(m2[:], m2[:], 0.25, None, ALU.mult))
            link(nc.vector.tensor_tensor(wgt[:], wgt[:], m2[:].broadcast_to([P, NT, 4]), ALU.subtract))
            link(nc.vector.tensor_scalar(wgt[:], wgt[:], 0.0, None, ALU.max))
            link(nc.vector.tensor_reduce(m1[:], wgt[:], AX.X, ALU.add))
            link(nc.vector.tensor_scalar(m2[:], m1[:], 0.0, None, ALU.is_equal))
            link(nc.vector.tensor_tensor(m1[:], m1[:], m2[:], ALU.add))
            link(nc.vector.reciprocal(m1[:], m1[:]))
            link(nc.vector.tensor_tensor(wgt[:], wgt[:], m1[:].broadcast_to([P, NT, 4]), ALU.mult))
            nc.vector.tensor_copy(wrep[:], wgt[:].unsqueeze(3).broadcast_to([P, NT, NE, R])).then_inc(wrep_ready, 1)
            for q in range(3):
                n = min(4, NT - 4 * q) * P
                dve.wait_ge(wt_done, q + 1)
                last = nc.vector.tensor_copy(wt[:, 4 * q * P:4 * q * P + n], core.bank(2 + q)[0:NE * R, 0:n])
            last.then_inc(start, 1)
            pp = Tick()
            with dve.Fori(0, NC) as c:
                pp.enter(c, UNITS)
                for e in range(NE):
                    for m in range(KT):
                        dve.wait_ge(u_hi, pp.step())
                        nc.vector.scalar_tensor_tensor(h_lo[e % 2][:, m, :], bank(m)[:, 0:CH], 0.0,
                                                       f32(h_hi[e % 2][:, m, :]), ALU.max,
                                                       ALU.subtract).then_inc(u_free, 1)
                dve.wait_ge(lora_done, NE * c + 6)
                nc.vector.tensor_tensor(lw[:], core.bank(5)[0:NE * R, 0:CH], wt[:, bass.ds(CH * c, CH)],
                                        ALU.mult).then_inc(lw_ready, 1)
                for s in range(2):
                    dve.wait_ge(out_done, 2 * c + s + 1)
                    dst = x[:, bass.ds(2 * c + s, 1), :].rearrange("p a n -> p (a n)")
                    nc.vector.tensor_tensor(dst, dst, core.bank(s)[0:P, :], ALU.add).then_inc(x_added, 1)
                pp.leave(NC)

        @block.tensor
        def _(pe):
            pe.wait_ge(xs_ready, 1)
            turned.tensor(core, pe, xs, g.ident)
            pe.wait_ge(turned.lo, turned.before + NT)
            pe.wait_ge(small_lo, 1)
            for t in range(NT):
                for k in range(KT):
                    last = three_pass(nc, core.bank(0)[0:P, 8 * t:8 * t + 6],
                                      [a[:, k, t * P:(t + 1) * P] for a in (g.xt_hi, g.xt_lo)],
                                      [a[:, k, :] for a in (gw_hi, gw_lo)], k == 0, k == KT - 1)
            last.then_inc(gl_done, 1)
            for e in range(NE):
                pe.wait_ge(raw_in[e % 2], 32 + 16 * (e // 2 + 1))
                for k in range(KT):
                    last = nc.tensor.matmul(core.bank(1)[0:NE * R, :], b_pad[:, e, k, :], raw[e % 2][:, k, :],
                                            start=e == k == 0, stop=e == NE - 1 and k == KT - 1)
                last.then_inc(raw_free[e % 2], 1)
            pe.wait_ge(wrep_ready, 1)
            for t in range(NT):
                q, r = divmod(t, 4)
                last = nc.tensor.transpose(core.bank(2 + q)[0:NE * R, r * P:(r + 1) * P],
                                           wrep[:, t, :, :].rearrange("p e r -> p (e r)"), g.ident[0:P, 0:P])
                if r == 3 or t == NT - 1:
                    last.then_inc(wt_done, 1)
            pe.wait_ge(start, 1)
            pp = Tick()

            def hidden(c, e):
                for m in range(KT):
                    pe.wait_ge(u_free, pp.step())
                    for k in range(KT):
                        last = three_pass(nc, bank(m)[:, 0:CH],
                                          [a[:, e, k, m * 128:(m + 1) * 128] for a in (fc1_hi, fc1_lo)],
                                          [a[:, k, bass.ds(CH * c, CH)] for a in (g.xt_hi, g.xt_lo)],
                                          k == 0, k == KT - 1)
                    last.then_inc(u_done, 1)

            def lora(c, e):
                pe.wait_ge(u_free, pp.base + KT * (e + 1) + 2)
                if e == 0:
                    pe.wait_ge(lw_ready, c + 1)
                for k in range(KT):
                    last = three_pass(nc, core.bank(5)[:, 0:CH], [a[:, e, k, :] for a in (a_hi, a_lo)],
                                      [a[:, k, :] for a in (h_hi[e % 2], h_lo[e % 2])],
                                      e == k == 0, e == NE - 1 and k == KT - 1)
                last.then_inc(lora_done, 1)

            with pe.Fori(0, NC) as c:
                pp.enter(c, UNITS)
                hidden(c, 0)
                for e in range(1, NE):
                    hidden(c, e)
                    lora(c, e - 1)
                lora(c, NE - 1)
                pe.wait_ge(lw_ready, c + 2)
                for s in range(2):
                    pe.wait_ge(x_added, 2 * c + s + 1)
                    nc.tensor.matmul(core.bank(s)[0:P, :], lw[:, s * P:(s + 1) * P], f_sb[:], start=True,
                                     stop=True).then_inc(out_done, 1)
                pp.leave(NC)


def edge_mean_gnn(core, g, w, ln):
    nc, at, sem = core.nc, core.at, core.sem
    HID = 1024
    MT = HID // 128
    x, xs = g.x, g.xs
    w1_hi, w1_lo = at("w1_hi", [128, KT, HID], F32R, 92), at("w1_lo", [128, KT, HID], F32R, 108)
    e1_hi, e1_lo = at("w1e_hi", [EDGE_D, HID], F32R, 124), at("w1e_lo", [EDGE_D, HID], F32R, 128)
    w2_hi, w2_lo = at("w2_hi", [128, MT, D], F32R, 132), at("w2_lo", [128, MT, D], F32R, 148)
    raw = [at(f"gnn_raw{i}", [128, KT, D], F32, 164 + 8 * i) for i in range(2)]
    at_hi, at_lo = at("agg_t_hi", [EDGE_D, N], F32R, 164), at("agg_t_lo", [EDGE_D, N], F32R, 169)
    h_hi, h_lo = at("gh_hi", [128, MT, CH], F32R, 180), at("gh_lo", [128, MT, CH], F32R, 188)
    r = at("gh_relu", [128, 2, CH], F32, 196)
    b2 = at("gnn_b2", [P, D], F32, 4)
    b1 = at("gnn_b1", [128, MT], F32, g.small)

    small_in, raw_in = sem("gnn_small_in"), [sem("gnn_raw_in0"), sem("gnn_raw_in1")]
    raw_free, hi_done = [sem("gnn_raw_free0"), sem("gnn_raw_free1")], sem("gnn_hi_done")
    xs_ready, xres = sem("gnn_xs"), sem("gnn_xres")
    ag_done, ag_hi, prep = sem("gnn_ag_done"), sem("gnn_ag_hi"), sem("gnn_prepared")
    u_done, u_bank, u_hi, u_lo = sem("gh_done"), sem("gh_bank_free"), sem("gh_hi_done"), sem("gh_lo_done")
    out_done, x_added, s_act = sem("gnn_out_done"), sem("gnn_x_added"), sem("gnn_relu_done")
    turned = g.turned.again()
    ln.turn += 1
    turn = ln.turn
    w1v = w["W1"][0:D, :].rearrange("(k p) n -> p k n", p=128)
    w2v = w["W2"].rearrange("(k p) n -> p k n", p=128)
    loads = [(w1v[:, :, 0:D], lambda b: b[:], (w1_hi[:, :, 0:D], w1_lo[:, :, 0:D])),
             (w1v[:, :, D:], lambda b: b[:], (w1_hi[:, :, D:], w1_lo[:, :, D:])),
             (w2v[:, 0:KT, :], lambda b: b[:], (w2_hi[:, 0:KT, :], w2_lo[:, 0:KT, :])),
             (w2v[:, KT:, :], lambda b: b[:], (w2_hi[:, KT:, :], w2_lo[:, KT:, :])),
             (w["W1"][D:, :], lambda b: b[0:EDGE_D, 0:2, :].rearrange("p a n -> p (a n)"), (e1_hi[:], e1_lo[:]))]
    agg_bank = lambda q: core.bank(q)[0:EDGE_D, 0:min(4, NT - 4 * q) * P]
    agg_cols = lambda q: slice(4 * q * P, 4 * q * P + min(4, NT - 4 * q) * P)

    with nc.Block() as block:
        @block.sync
        def _(sp):
            sp.dma_start(b1[:], w["b1"]).then_inc(small_in, 16)
            sp.dma_start(b2[:], row_view(w["b2"])).then_inc(small_in, 16)
            for i, (src, dst, _) in enumerate(loads):
                if i >= 2:
                    sp.wait_ge(raw_free[i % 2], i // 2)
                sp.dma_start(dst(raw[i % 2]), src).then_inc(raw_in[i % 2], 16)

        @block.gpsimd
        def _(pool):
            pool.wait_ge(xs_ready, 1)
            pool.wait_ge(small_in, 32)
            nc.gpsimd.tensor_tensor(x[:], x[:], xs[:], ALU.add).then_inc(xres, 1)
            pool.wait_ge(xres, 1)
            for t in range(NT):
                last = nc.gpsimd.tensor_tensor(x[:, t, :], x[:, t, :], b2[:], ALU.add)
            last.then_inc(xres, 1)

        @block.scalar
        def _(act):
            ln.root(nc, act)
            for i, (_, dst, (hi, _)) in enumerate(loads):
                act.wait_ge(raw_in[i % 2], 16 * (i // 2 + 1))
                nc.scalar.activation(hi, dst(raw[i % 2]), ACT.Copy).then_inc(hi_done, 1)
            turned.scalar(core, act, g.xt_hi)
            act.wait_ge(raw_free[0], 3)
            act.wait_ge(raw_free[1], 2)
            for q in range(3):
                act.wait_ge(ag_done, q + 1)
                nc.scalar.activation(at_hi[:, agg_cols(q)], agg_bank(q), ACT.Copy).then_inc(ag_hi, 1)
            pp = Tick()
            act.wait_ge(small_in, 32)
            with act.Fori(0, NC) as c:
                pp.enter(c, MT)
                for m in range(MT):
                    v = pp.step()
                    act.wait_ge(u_done, v)
                    act.wait_ge(u_lo, v)
                    nc.scalar.activation(r[:, m % 2, :], core.bank(6 + m % 2)[:, 0:CH], ACT.Relu,
                                         bias=b1[:, m:m + 1]).then_inc(u_bank, 1)
                    act.wait_ge(u_bank, v + 2)
                    nc.scalar.activation(h_hi[:, m, :], r[:, m % 2, :], ACT.Copy).then_inc(u_hi, 1)
                pp.leave(NC)

        @block.vector
        def _(dve):
            link = core.link.on(dve)
            normalise(nc, link, x, xs, ln, turn)
            dve.sem_inc(xs_ready, 1)
            for i, (_, dst, (hi, lo)) in enumerate(loads):
                dve.wait_ge(hi_done, i + 1)
                nc.vector.tensor_tensor(lo, dst(raw[i % 2]), f32(hi), ALU.subtract).then_inc(raw_free[i % 2], 1)
            turned.vector(core, dve, g.xt_hi, g.xt_lo)
            for q in range(3):
                dve.wait_ge(ag_hi, q + 1)
                last = nc.vector.tensor_tensor(at_lo[:, agg_cols(q)], agg_bank(q), f32(at_hi[:, agg_cols(q)]),
                                               ALU.subtract)
            last.then_inc(prep, 1)
            dve.wait_ge(xres, 2)
            pp = Tick()
            with dve.Fori(0, NC) as c:
                pp.enter(c, MT)
                for m in range(MT):
                    dve.wait_ge(u_hi, pp.step())
                    nc.vector.tensor_tensor(h_lo[:, m, :], r[:, m % 2, :], f32(h_hi[:, m, :]),
                                            ALU.subtract).then_inc(u_lo, 1)
                for s in range(2):
                    dve.wait_ge(out_done, 2 * c + s + 1)
                    dst = x[:, bass.ds(2 * c + s, 1), :].rearrange("p a n -> p (a n)")
                    nc.vector.tensor_tensor(dst, dst, core.bank(s)[0:P, :], ALU.add).then_inc(x_added, 1)
                pp.leave(NC)

        @block.tensor
        def _(pe):
            pe.wait_ge(xs_ready, 1)
            turned.tensor(core, pe, xs, g.ident)
            pe.wait_ge(turned.lo, turned.before + NT)
            for t in range(NT):
                q, j = divmod(t, 4)
                last = nc.tensor.transpose(core.bank(q)[0:EDGE_D, j * P:(j + 1) * P], g.agg[:, t, :], g.ident[0:P, 0:P])
                if j == 3 or t == NT - 1:
                    last.then_inc(ag_done, 1)
            pe.wait_ge(prep, 1)
            pp = Tick()
            with pe.Fori(0, NC) as c:
                pp.enter(c, MT)
                for m in range(MT):
                    out = core.bank(6 + m % 2)[:, 0:CH]
                    cols = slice(m * 128, (m + 1) * 128)
                    pe.wait_ge(u_bank, pp.step())
                    for k in range(KT):
                        three_pass(nc, out, [a[:, k, cols] for a in (w1_hi, w1_lo)],
                                   [a[:, k, bass.ds(CH * c, CH)] for a in (g.xt_hi, g.xt_lo)], k == 0, False)
                    three_pass(nc, out, [a[:, cols] for a in (e1_hi, e1_lo)],
                               [a[:, bass.ds(CH * c, CH)] for a in (at_hi, at_lo)], False, True).then_inc(u_done, 1)
                pe.wait_ge(u_lo, pp.base + pp.n + 2)
                for s in range(2):
                    pe.wait_ge(x_added, 2 * c + s + 1)
                    for k in range(MT):
                        last = three_pass(nc, core.bank(s)[0:P, :], [a[:, k, s * P:(s + 1) * P] for a in (h_hi, h_lo)],
                                          [a[:, k, :] for a in (w2_hi, w2_lo)], k == 0, k == MT - 1)
                    last.then_inc(out_done, 1)
                pp.leave(NC)


def keys_values(core, g, w, ln):
    nc, at, sem = core.nc, core.at, core.sem
    x, xs = g.x, g.xs
    g.k_hi, g.k_lo = at("k_hi", [128, KT, N], F32R, 92), at("k_lo", [128, KT, N], F32R, 112)
    g.v_hi, g.v_lo = at("v_hi", [P, NT, D], F32R, 132), at("v_lo", [P, NT, D], F32R, 152)
    g.q_hi, g.q_lo = at("q_hi", [128, KT, N], F32R, 12), at("q_lo", [128, KT, N], F32R, 32)
    w_hi, w_lo = at("kv_w_hi", [128, KT, D], F32R, 172), at("kv_w_lo", [128, KT, D], F32R, 180)
    raw = at("kv_raw", [128, KT, D], F32, 188)
    vsum = at("v_sum", [P, 2, D], F32, 196)
    bv = at("mha_bv", [P, D], F32, 4)
    bqk = at("mha_bqk", [128, 2, KT], F32, g.small)
    small_in, raw_in, hi_done, lo_done = sem("kv_small_in"), sem("kv_raw_in"), sem("kv_hi_done"), sem("kv_lo_done")
    xs_ready, stash = sem("kv_xs"), sem("kv_stashed")
    x_ready = sem("kv_x")
    done, hi, lo, vs = sem("kv_done"), sem("kv_out_hi"), sem("kv_out_lo"), sem("kv_vsum")
    turned = g.turned.again()
    ln.turn += 1
    turn = ln.turn
    kq_units = [(m, a, b) for m in range(KT) for a, b in SPANS]
    nk, first_q = len(kq_units), len(kq_units) + NT
    total = 2 * nk + NT

    with nc.Block() as block:
        @block.sync
        def _(sp):
            sp.dma_start(bqk[:, 0, :], w["bq2"]).then_inc(small_in, 16)
            sp.dma_start(bqk[:, 1, :], w["bk2"]).then_inc(small_in, 16)
            sp.dma_start(bv[:], row_view(w["bv2"])).then_inc(small_in, 16)
            for i, src in enumerate((w["Wk2"], w["Wv2"], w["Wq2"])):
                if i:
                    sp.wait_ge(lo_done, i)
                sp.dma_start(raw[:], src.rearrange("(k p) n -> p k n", p=128)).then_inc(raw_in, 16)
            sp.dma_start(tiles(g.x3_store), x[:]).then_inc(stash, 16)
            sp.wait_ge(xs_ready, 1)
            sp.dma_start(tiles(g.xs_store), xs[:]).then_inc(stash, 16)
            sp.wait_ge(stash, 32)

        @block.scalar
        def _(act):
            ln.root(nc, act)
            act.wait_ge(raw_in, 16)
            nc.scalar.activation(w_hi[:], raw[:], ACT.Copy).then_inc(hi_done, 1)
            turned.scalar(core, act, g.xt_hi)
            act.wait_ge(small_in, 48)
            for u in range(total):
                if u == nk or u == first_q:
                    act.wait_ge(raw_in, 32 if u == nk else 48)
                    act.wait_ge(done, u)
                    nc.scalar.activation(w_hi[:], raw[:], ACT.Copy).then_inc(hi_done, 1)
                if nk <= u < first_q:
                    t = u - nk
                    act.wait_ge(vs, t + 1)
                    nc.scalar.activation(g.v_hi[:, t, :], vsum[:, t % 2, :], ACT.Copy).then_inc(hi, 1)
                    continue
                if u == first_q:
                    act.wait_ge(stash, 32)
                dst, j = (g.k_hi, 1) if u < nk else (g.q_hi, 0)
                m, a, b = kq_units[u if u < nk else u - first_q]
                act.wait_ge(done, u + 1)
                nc.scalar.activation(dst[:, m, a:b], core.bank(u % 8)[:, 0:b - a], ACT.Identity,
                                     bias=bqk[:, j, m:m + 1]).then_inc(hi, 1)

        @block.vector
        def _(dve):
            link = core.link.on(dve)
            normalise(nc, link, x, xs, ln, turn)
            dve.sem_inc(xs_ready, 1)

            def split(n):
                dve.wait_ge(hi_done, n)
                nc.vector.tensor_tensor(w_lo[:], raw[:], f32(w_hi[:]), ALU.subtract).then_inc(lo_done, 1)

            split(1)
            turned.vector(core, dve, g.xt_hi, g.xt_lo)
            dve.wait_ge(small_in, 48)
            for u in range(total):
                if u == nk or u == first_q:
                    split(2 if u == nk else 3)
                if nk <= u < first_q:
                    t = u - nk
                    dve.wait_ge(done, u + 1)
                    nc.vector.tensor_tensor(vsum[:, t % 2, :], core.bank(u % 8)[0:P, :], bv[:], ALU.add).then_inc(vs, 1)
                    dve.wait_ge(hi, u + 1)
                    nc.vector.tensor_tensor(g.v_lo[:, t, :], vsum[:, t % 2, :], f32(g.v_hi[:, t, :]),
                                            ALU.subtract).then_inc(lo, 1)
                    continue
                dh, dl, j = (g.k_hi, g.k_lo, 1) if u < nk else (g.q_hi, g.q_lo, 0)
                m, a, b = kq_units[u if u < nk else u - first_q]
                dve.wait_ge(hi, u + 1)
                nc.vector.scalar_tensor_tensor(dl[:, m, a:b], core.bank(u % 8)[:, 0:b - a], bqk[:, j, m:m + 1],
                                               f32(dh[:, m, a:b]), ALU.add, ALU.subtract).then_inc(lo, 1)

        @block.tensor
        def _(pe):
            pe.wait_ge(xs_ready, 1)
            turned.tensor(core, pe, xs, g.ident)
            pe.wait_ge(turned.lo, turned.before + NT)
            for u in range(total):
                if u in (0, nk, first_q):
                    pe.wait_ge(lo_done, 1 + (u >= nk) + (u >= first_q))
                if u >= 8:
                    pe.wait_ge(lo, u - 7)
                for k in range(KT):
                    if nk <= u < first_q:
                        t = u - nk
                        last = three_pass(nc, core.bank(u % 8)[0:P, :],
                                          [a[:, k, t * P:(t + 1) * P] for a in (g.xt_hi, g.xt_lo)],
                                          [a[:, k, :] for a in (w_hi, w_lo)], k == 0, k == KT - 1)
                    else:
                        m, lo_, hi_ = kq_units[u if u < nk else u - first_q]
                        last = three_pass(nc, core.bank(u % 8)[:, 0:hi_ - lo_],
                                          [a[:, k, m * 128:(m + 1) * 128] for a in (w_hi, w_lo)],
                                          [a[:, k, lo_:hi_] for a in (g.xt_hi, g.xt_lo)], k == 0, k == KT - 1)
                last.then_inc(done, 1)


def self_attention(core, g, w):
    nc, at, sem = core.nc, core.at, core.sem
    NH, DH = 8, 64
    scale = DH ** -0.5
    qs_hi, qs_lo = at("qs_hi", [128, KT, CH], F32R, 52), at("qs_lo", [128, KT, CH], F32R, 56)
    ctx_hi, ctx_lo = at("ctx_hi", [128, KT, CH], F32R, 60), at("ctx_lo", [128, KT, CH], F32R, 64)
    wo_hi, wo_lo = at("wo_hi", [128, KT, D], F32R, 68), at("wo_lo", [128, KT, D], F32R, 76)
    raw = at("wo_raw", [128, KT, D], F32, 84)
    pt_hi, pt_lo = at("ptm_hi", [P, NT, CH], F32R, 172), at("ptm_lo", [P, NT, CH], F32R, 182)
    prob = at("mprob", [P, 2, N], F32, 192)
    xin = at("mha_xin", [P, 2, D], F32, 4)
    bo = at("mha_bo", [P, D], F32, 8)
    S = g.small
    nmx, den, rden = (at(n, [P, 2], F32, S + i / 16) for i, n in enumerate(("nmx", "mden", "mrden")))

    small_in, raw_in, wo_h, wo_ready = sem("at_small_in"), sem("at_raw_in"), sem("at_wo_hi"), sem("at_wo_ready")
    q_in = sem("at_q_in")
    s_done, m_ready, e_ready = sem("at_s_done"), sem("at_m_ready"), sem("at_e_ready")
    r_ready, p_ready = sem("at_r_ready"), sem("at_p_ready")
    pp_done, pp_hi, pp_free = sem("at_pp_done"), sem("at_pp_hi"), sem("at_pp_free")
    xin_in, summed = sem("at_xin_in"), sem("at_summed")
    stored = sem("at_stored")
    UNITS = 2 * NH * 3 + NH + 2
    SUBS = 2 * NH
    bank = lambda u: core.bank(6 + u % 2)
    score = [core.psum[0:P, 3 * i:3 * i + 3, :].rearrange("p b n -> p (b n)") for i in range(2)]
    PIECES = [(0, 4), (4, 8), (8, 10)]

    def piece(u, q):
        j0, j1 = PIECES[q]
        return bank(u)[0:P, 0:(j1 - j0) * P].rearrange("p (j n) -> p j n", n=P)

    with nc.Block() as block:
        @block.sync
        def _(sp):
            sp.dma_start(raw[:], w["Wo"].rearrange("(k p) n -> p k n", p=128)).then_inc(raw_in, 16)
            sp.dma_start(bo[:], row_view(w["bo"])).then_inc(small_in, 16)

            def load_q(c):
                sp.dma_start(f32(qs_hi[:]), f32(g.q_hi[:, :, bass.ds(CH * c, CH)])).then_inc(q_in, 16)
                sp.dma_start(f32(qs_lo[:]), f32(g.q_lo[:, :, bass.ds(CH * c, CH)])).then_inc(q_in, 16)

            def residual_in(c):
                sp.wait_ge(stored, 16 * c + 16)
                sp.dma_start(xin[:], tiles(g.xs_store)[:, bass.ds(2 * c, 2), :]).then_inc(xin_in, 16)

            def rows_out(c):
                sp.wait_ge(summed, 2 * c + 2)
                sp.dma_start(tiles(g.pre_store)[:, bass.ds(2 * c, 2), :], xin[:]).then_inc(stored, 16)

            load_q(0)
            with sp.Fori(0, NC - 1) as c:
                residual_in(c)
                sp.wait_ge(s_done, SUBS * (c + 1))
                load_q(c + 1)
                rows_out(c)
            residual_in(NC - 1)
            rows_out(NC - 1)
            sp.wait_ge(stored, 16 * NC + 16)

        @block.gpsimd
        def _(pool):
            sub = Tick()
            with pool.Fori(0, NC) as c:
                sub.enter(c, SUBS)
                for u in range(SUBS):
                    s = u % 2
                    pool.wait_ge(r_ready, sub.step())
                    nc.gpsimd.tensor_tensor(prob[:, s, :], prob[:, s, :], rden[:, s:s + 1].broadcast_to([P, N]),
                                            ALU.mult).then_inc(p_ready, 1)
                sub.leave(NC)

        @block.scalar
        def _(act):
            act.wait_ge(raw_in, 16)
            nc.scalar.activation(wo_hi[:], raw[:], ACT.Copy).then_inc(wo_h, 1)
            sub, pp = Tick(), Tick()

            def turned_hi(u):
                for q, (j0, j1) in enumerate(PIECES):
                    act.wait_ge(pp_done, pp.step())
                    nc.scalar.activation(pt_hi[:, j0:j1, (u % 2) * P:(u % 2 + 1) * P], piece(pp.n - 1, q),
                                         ACT.Copy).then_inc(pp_hi, 1)

            def context_hi(hh):
                rows = slice(DH * (hh % 2), DH * (hh % 2) + DH)
                act.wait_ge(pp_done, pp.step())
                nc.scalar.activation(ctx_hi[rows, hh // 2, :], bank(pp.n - 1)[rows, 0:CH], ACT.Copy).then_inc(pp_hi, 1)

            with act.Fori(0, NC) as c:
                pp.enter(c, UNITS), sub.enter(c, SUBS)
                for hh in range(NH):
                    for s in range(2):
                        act.wait_ge(m_ready, sub.step())
                        nc.scalar.activation(prob[:, s, :], score[s][:, 0:N], ACT.Exp, bias=nmx[:, s:s + 1],
                                             scale=scale, accum_out=den[:, s:s + 1]).then_inc(e_ready, 1)
                    if hh > 0:
                        context_hi(hh - 1)
                    turned_hi(0), turned_hi(1)
                context_hi(NH - 1)
                pp.step(2)
                pp.leave(NC), sub.leave(NC)

        @block.vector
        def _(dve):
            link = core.link.on(dve)
            dve.wait_ge(wo_h, 1)
            nc.vector.tensor_tensor(wo_lo[:], raw[:], f32(wo_hi[:]), ALU.subtract).then_inc(wo_ready, 1)
            dve.wait_ge(small_in, 16)
            sub, pp, hi = Tick(), Tick(), Tick()

            def maximum(s):
                dve.wait_ge(s_done, sub.step())
                link(nc.vector.tensor_reduce(nmx[:, s:s + 1], score[s][:, 0:N], AX.X, ALU.max))
                nc.vector.tensor_scalar(nmx[:, s:s + 1], nmx[:, s:s + 1], -scale, None, ALU.mult).then_inc(m_ready, 1)

            def inverse(s):
                dve.wait_ge(e_ready, sub.base + sub.n + 1 + s)
                nc.vector.reciprocal(rden[:, s:s + 1], den[:, s:s + 1]).then_inc(r_ready, 1)

            def turned_lo(u):
                for q, (j0, j1) in enumerate(PIECES):
                    pp.step()
                    dve.wait_ge(pp_hi, hi.step())
                    cols = slice((u % 2) * P, (u % 2 + 1) * P)
                    nc.vector.tensor_tensor(pt_lo[:, j0:j1, cols], piece(pp.n - 1, q), f32(pt_hi[:, j0:j1, cols]),
                                            ALU.subtract).then_inc(pp_free, 1)

            def context_lo(hh):
                rows = slice(DH * (hh % 2), DH * (hh % 2) + DH)
                pp.step()
                dve.wait_ge(pp_hi, hi.step())
                nc.vector.tensor_tensor(ctx_lo[rows, hh // 2, :], bank(pp.n - 1)[rows, 0:CH],
                                        f32(ctx_hi[rows, hh // 2, :]), ALU.subtract).then_inc(pp_free, 1)

            with dve.Fori(0, NC) as c:
                pp.enter(c, UNITS), sub.enter(c, SUBS), hi.enter(c, UNITS - 2), link.enter(c, SUBS + 2)
                for hh in range(NH):
                    maximum(0), maximum(1)
                    inverse(0), inverse(1)
                    if hh > 0:
                        context_lo(hh - 1)
                    turned_lo(0), turned_lo(1)
                context_lo(NH - 1)
                dve.wait_ge(xin_in, 16 * c + 16)
                for s in range(2):
                    v = pp.step()
                    link(nc.vector.tensor_tensor(xin[:, s, :], xin[:, s, :], bo[:], ALU.add))
                    dve.wait_ge(pp_done, v)
                    nc.vector.tensor_tensor(xin[:, s, :], xin[:, s, :], bank(pp.n - 1)[0:P, :],
                                            ALU.add).then_inc(pp_free, 1)
                    dve.wait_ge(pp_free, v + 2)
                    dve.sem_inc(summed, 1)
                for x in (pp, sub, hi, link):
                    x.leave(NC)

        @block.tensor
        def _(pe):
            pe.wait_ge(wo_ready, 1)
            pp, sub = Tick(), Tick()

            def scores(hh, s):
                rows = slice(DH * (hh % 2), DH * (hh % 2) + DH)
                pe.wait_ge(e_ready, sub.step())
                for a, b in SPANS:
                    last = three_pass(nc, score[s][:, a:b],
                                      [x[rows, hh // 2, s * P:(s + 1) * P] for x in (qs_hi, qs_lo)],
                                      [x[rows, hh // 2, a:b] for x in (g.k_hi, g.k_lo)], True, True)
                last.then_inc(s_done, 1)

            def turn(s):
                pe.wait_ge(p_ready, sub.base + sub.n - 1 + s)
                for q, (j0, j1) in enumerate(PIECES):
                    pe.wait_ge(pp_free, pp.step())
                    for j in range(j0, j1):
                        last = nc.tensor.transpose(piece(pp.n - 1, q)[:, j - j0, :], prob[:, s, j * P:(j + 1) * P],
                                                   g.ident[0:P, 0:P])
                    last.then_inc(pp_done, 1)

            def context(hh):
                pe.wait_ge(pp_free, pp.step() + 1)
                for j in range(NT):
                    last = three_pass(nc, bank(pp.n - 1)[:, 0:CH],
                                      [x[:, j, 128 * (hh // 2):128 * (hh // 2) + 128] for x in (g.v_hi, g.v_lo)],
                                      [x[:, j, :] for x in (pt_hi, pt_lo)], j == 0, j == NT - 1)
                last.then_inc(pp_done, 1)

            with pe.Fori(0, NC) as c:
                pp.enter(c, UNITS), sub.enter(c, SUBS)
                pe.wait_ge(q_in, 32 * c + 32)
                for hh in range(NH):
                    scores(hh, 0), scores(hh, 1)
                    if hh > 0:
                        context(hh - 1)
                    turn(0), turn(1)
                context(NH - 1)
                pe.wait_ge(pp_free, pp.base + pp.n + 2)
                for s in range(2):
                    v = pp.step()
                    pe.wait_ge(pp_free, v)
                    for k in range(KT):
                        last = three_pass(nc, bank(pp.n - 1)[0:P, :], [x[:, k, s * P:(s + 1) * P] for x in (ctx_hi, ctx_lo)],
                                          [x[:, k, :] for x in (wo_hi, wo_lo)], k == 0, k == KT - 1)
                    last.then_inc(pp_done, 1)
                pp.leave(NC), sub.leave(NC)


def expert_mixture(core, g, w, ln):
    nc, at, sem = core.nc, core.at, core.sem
    NE, HID = 8, 256
    MT = HID // 128
    t_, pre = at("moe_t", [P, NT, D], F32, 12), at("moe_pre", [P, NT, D], F32, 32)
    raw1, raw2 = at("moe_raw1", [128, KT, HID], F32, 92), at("moe_raw2", [128, MT, D], F32, 96)
    w1 = [[at(f"moe_w1_{x}{i}", [128, KT, HID], F32R, 100 + 8 * i + 4 * j) for j, x in enumerate(("hi", "lo"))]
          for i in range(2)]
    w2 = [[at(f"moe_w2_{x}{i}", [128, MT, D], F32R, 116 + 8 * i + 4 * j) for j, x in enumerate(("hi", "lo"))]
          for i in range(2)]
    r = at("moe_gelu", [128, MT, CH], F32, 132)
    h_hi, h_lo = at("moe_h_hi", [128, MT, CH], F32R, 134), at("moe_h_lo", [128, MT, CH], F32R, 136)
    g1, beta1, g2, beta2 = (at(n, [P, D], F32, 140 + 2 * i) for i, n in enumerate(("g1", "beta1", "g2", "beta2")))
    b2 = at("moe_b2", [NE, D], F32, 148)
    bg, b1 = at("moe_bg", [P, NE], F32, 150), at("moe_b1", [128, NE * MT], F32, 150.125)
    wg = at("moe_wg", [128, KT, NE], F32, 150.25)
    wg_hi, wg_lo = at("moe_wg_hi", [128, KT, NE], F32R, 150.375), at("moe_wg_lo", [128, KT, NE], F32R, 150.5)
    x3 = at("moe_x3", [P, NT, D], F32, 152)
    hot_t = at("moe_hot_t", [NE, N], F32, 172)
    S = 177
    lg, hot, rank = at("moe_lg", [P, NT, NE], F32, S), at("moe_hot", [P, NT * NE], F32, S + .5), at("moe_rank", [P, NE], F32, S + 1)
    best = at("moe_best", [P, NT, 1], F32, S + 1.125)
    hot3 = hot[:].rearrange("p (t e) -> p t e", e=NE)

    pre_in, small_in = sem("moe_pre_in"), sem("moe_small_in")
    raw1_in, raw2_in = sem("moe_raw1_in"), sem("moe_raw2_in")
    x3_ready, wg_hi_done, wg_ready = sem("moe_x3"), sem("moe_wg_hi_done"), sem("moe_wg_ready")
    t_ready, lg_done, hot_ready = sem("moe_t_ready"), sem("moe_lg_done"), sem("moe_hot_ready")
    ht_done, ht_ready, b2_done, b2_added = sem("moe_ht_done"), sem("moe_ht_ready"), sem("moe_b2_done"), sem("moe_b2_added")
    w_hi, w_lo = sem("moe_w_hi"), sem("moe_w_lo")
    u_done, u_bank, u_hi, u_lo = sem("moe_u_done"), sem("moe_bank_free"), sem("moe_hi"), sem("moe_lo")
    out_done, added = sem("moe_out_done"), sem("moe_added")
    final, stored = sem("final_ready"), sem("out_stored")
    turned = g.turned.again()
    ln.turn += 2
    turn = ln.turn - 1
    w1_rows = w["W1e"].rearrange("e (k p) n -> e p k n", p=128)
    w2_rows = w["W2e"].rearrange("e (k p) n -> e p k n", p=128)

    def experts(eng, body, counts):
        with eng.Fori(0, NE // 2 - 1) as pair:
            for tick, per in counts:
                tick.enter(pair, 2 * per)
            for par in range(2):
                body(2 * pair + par, par, True)
            for tick, per in counts:
                tick.leave(NE // 2 - 1)
        for par in range(2):
            body(NE - 2 + par, par, par == 0)

    with nc.Block() as block:
        @block.sync
        def _(sp):
            sp.dma_start(pre[:], tiles(g.pre_store)).then_inc(pre_in, 16)
            for dst, src in ((g1[:], row_view(w["g1"])), (beta1[:], row_view(w["beta1"])), (g2[:], row_view(w["g2"])),
                             (beta2[:], row_view(w["beta2"])), (bg[:], row_view(w["bg"])), (b2[:], w["b2e"]), (b1[:], w["b1e"]),
                             (wg[:], w["Wg"].rearrange("(k p) n -> p k n", p=128)), (x3[:], tiles(g.x3_store))):
                sp.dma_start(dst, src).then_inc(small_in, 16)
            sp.dma_start(raw1[:], w1_rows[0]).then_inc(raw1_in, 16)
            sp.dma_start(raw2[:], w2_rows[0]).then_inc(raw2_in, 16)
            with sp.Fori(1, NE) as e:
                sp.wait_ge(w_lo, 2 * e - 1)
                sp.dma_start(raw1[:], w1_rows[bass.ds(e, 1)].rearrange("a p k n -> (a p) k n")).then_inc(raw1_in, 16)
                sp.wait_ge(w_lo, 2 * e)
                sp.dma_start(raw2[:], w2_rows[bass.ds(e, 1)].rearrange("a p k n -> (a p) k n")).then_inc(raw2_in, 16)
            for t in range(NT):
                sp.wait_ge(final, t + 1)
                sp.dma_start(w["out"][t * P:(t + 1) * P, :], t_[:, t, :]).then_inc(stored, 16)
            sp.wait_ge(stored, 16 * NT)

        @block.gpsimd
        def _(pool):
            pool.wait_ge(small_in, 144)
            for t in range(NT):
                last = nc.gpsimd.tensor_tensor(x3[:, t, :], x3[:, t, :], beta2[:], ALU.add)
            last.then_inc(x3_ready, 1)

        @block.scalar
        def _(act):
            ln.root_at(nc, act, turn)
            act.wait_ge(small_in, 144)
            nc.scalar.activation(wg_hi[:], wg[:], ACT.Copy).then_inc(wg_hi_done, 1)
            turned.scalar(core, act, g.xt_hi)

            def split(e, par):
                act.wait_ge(raw1_in, 16 * e + 16)
                nc.scalar.activation(w1[par][0][:], raw1[:], ACT.Copy).then_inc(w_hi, 1)
                act.wait_ge(raw2_in, 16 * e + 16)
                nc.scalar.activation(w2[par][0][:], raw2[:], ACT.Copy).then_inc(w_hi, 1)

            split(0, 0)
            units, its = Tick(), Tick()

            def hidden(e):
                for m in range(MT):
                    v = units.step()
                    act.wait_ge(u_done, v)
                    act.wait_ge(u_lo, v)
                    nc.scalar.activation(r[:, m, :], core.bank(6 + m)[:, 0:CH], ACT.Gelu,
                                         bias=b1[:, bass.ds(MT * e + m, 1)]).then_inc(u_bank, 1)
                act.wait_ge(out_done, 2 * its.step())
                act.wait_ge(u_bank, 2 + v)
                for m in range(MT):
                    nc.scalar.activation(h_hi[:, m, :], r[:, m, :], ACT.Copy).then_inc(u_hi, 1)

            def expert(e, par, more):
                if more:
                    act.wait_ge(out_done, 2 * its.base + 2 * its.n + 2)
                    split(e + 1, 1 - par)
                with act.Fori(0, NC) as c:
                    units.enter(c, MT), its.enter(c, 1)
                    hidden(e)
                    units.leave(NC), its.leave(NC)

            experts(act, expert, ((units, MT * NC), (its, NC)))
            ln.root_at(nc, act, turn + 1)

        @block.vector
        def _(dve):
            link = core.link.on(dve)
            dve.wait_ge(pre_in, 16)
            dve.wait_ge(small_in, 144)
            affine(nc, link, pre, t_, ln, turn, g1, [beta1[:]] * NT, None)
            dve.sem_inc(t_ready, 1)
            dve.wait_ge(wg_hi_done, 1)
            nc.vector.tensor_tensor(wg_lo[:], wg[:], f32(wg_hi[:]), ALU.subtract).then_inc(wg_ready, 1)
            turned.vector(core, dve, g.xt_hi, g.xt_lo)
            for e in range(NE):
                last = nc.vector.memset(rank[:, e:e + 1], float(NE - e))
            link(last)
            dve.wait_ge(lg_done, 1)
            gl = core.bank(0)[0:P, 0:NT * NE].rearrange("p (t e) -> p t e", e=NE)
            link(nc.vector.tensor_tensor(lg[:], gl, bc(bg[:], NT), ALU.add))
            link(nc.vector.tensor_reduce(best[:], lg[:], AX.X, ALU.max))
            link(nc.vector.tensor_tensor(lg[:], lg[:], best[:].broadcast_to([P, NT, NE]), ALU.is_equal))
            link(nc.vector.tensor_tensor(lg[:], lg[:], bc(rank[:], NT), ALU.mult))
            link(nc.vector.tensor_reduce(best[:], lg[:], AX.X, ALU.max))
            nc.vector.tensor_tensor(hot3, lg[:], best[:].broadcast_to([P, NT, NE]), ALU.is_equal).then_inc(hot_ready, 1)
            for q in range(3):
                n = min(4, NT - 4 * q) * P
                dve.wait_ge(ht_done, q + 1)
                last = nc.vector.tensor_copy(hot_t[:, 4 * q * P:4 * q * P + n], core.bank(1 + q)[0:NE, 0:n])
            last.then_inc(ht_ready, 1)
            for t in range(NT):
                dve.wait_ge(b2_done, t + 1)
                nc.vector.tensor_tensor(t_[:, t, :], t_[:, t, :], core.bank(4 + t % 2)[0:P, :],
                                        ALU.add).then_inc(b2_added, 1)

            halves, units, subs = Tick(), Tick(), Tick()

            def split(par):
                for dst, src in ((w1[par], raw1), (w2[par], raw2)):
                    dve.wait_ge(w_hi, halves.step())
                    nc.vector.tensor_tensor(dst[1][:], src[:], f32(dst[0][:]), ALU.subtract).then_inc(w_lo, 1)

            split(0)

            def rests():
                for m in range(MT):
                    dve.wait_ge(u_hi, units.step())
                    nc.vector.tensor_tensor(h_lo[:, m, :], r[:, m, :], f32(h_hi[:, m, :]), ALU.subtract).then_inc(u_lo, 1)

            def add_out(c, e):
                for s in range(2):
                    dve.wait_ge(out_done, subs.step() + 2)
                    dst = t_[:, bass.ds(2 * c + s, 1), :].rearrange("p a n -> p (a n)")
                    nc.vector.scalar_tensor_tensor(dst, core.bank(s)[0:P, :], hot[:, bass.ds(NE * (2 * c + s) + e, 1)],
                                                   dst, ALU.mult, ALU.add).then_inc(added, 1)

            def expert(e, par, more):
                if more:
                    split(1 - par)
                rests()
                with dve.Fori(1, NC) as c:
                    units.enter(c - 1, MT), subs.enter(c - 1, 2)
                    rests()
                    add_out(c - 1, e)
                    units.leave(NC - 1), subs.leave(NC - 1)
                add_out(NC - 1, e)

            experts(dve, expert, ((halves, 2), (units, MT * NC), (subs, 2 * NC)))
            dve.wait_ge(added, 2 * NC * NE + 2)
            dve.wait_ge(x3_ready, 1)
            affine(nc, link, t_, t_, ln, turn + 1, g2, [x3[:, t, :] for t in range(NT)], final)

        @block.tensor
        def _(pe):
            pe.wait_ge(t_ready, 1)
            turned.tensor(core, pe, t_, g.ident)
            pe.wait_ge(turned.lo, turned.before + NT)
            pe.wait_ge(wg_ready, 1)
            for t in range(NT):
                for k in range(KT):
                    last = three_pass(nc, core.bank(0)[0:P, NE * t:NE * t + NE],
                                      [a[:, k, t * P:(t + 1) * P] for a in (g.xt_hi, g.xt_lo)],
                                      [a[:, k, :] for a in (wg_hi, wg_lo)], k == 0, k == KT - 1)
            last.then_inc(lg_done, 1)
            pe.wait_ge(hot_ready, 1)
            for t in range(NT):
                q, j = divmod(t, 4)
                last = nc.tensor.transpose(core.bank(1 + q)[0:NE, j * P:(j + 1) * P], hot3[:, t, :], g.ident[0:P, 0:P])
                if j == 3 or t == NT - 1:
                    last.then_inc(ht_done, 1)
            pe.wait_ge(ht_ready, 1)
            for t in range(NT):
                if t >= 2:
                    pe.wait_ge(b2_added, t - 1)
                nc.tensor.matmul(core.bank(4 + t % 2)[0:P, :], hot_t[:, t * P:(t + 1) * P], b2[:], start=True,
                                 stop=True).then_inc(b2_done, 1)
            units, subs = Tick(), Tick()

            def hidden(c, par):
                for m in range(MT):
                    pe.wait_ge(u_bank, units.step())
                    for k in range(KT):
                        last = three_pass(nc, core.bank(6 + m)[:, 0:CH],
                                          [a[:, k, m * 128:(m + 1) * 128] for a in w1[par]],
                                          [a[:, k, bass.ds(CH * c, CH)] for a in (g.xt_hi, g.xt_lo)],
                                          k == 0, k == KT - 1)
                    last.then_inc(u_done, 1)

            def outputs(c, par, ahead):
                pe.wait_ge(u_lo, units.base + units.n - ahead + 2)
                for s in range(2):
                    pe.wait_ge(added, subs.step())
                    for k in range(MT):
                        last = three_pass(nc, core.bank(s)[0:P, :], [a[:, k, s * P:(s + 1) * P] for a in (h_hi, h_lo)],
                                          [a[:, k, :] for a in w2[par]], k == 0, k == MT - 1)
                    last.then_inc(out_done, 1)

            def expert(e, par, more):
                pe.wait_ge(w_lo, 2 * e + 2)
                hidden(0, par)
                with pe.Fori(1, NC) as c:
                    units.enter(c - 1, MT), subs.enter(c - 1, 2)
                    hidden(c, par)
                    outputs(c - 1, par, MT)
                    units.leave(NC - 1), subs.leave(NC - 1)
                outputs(NC - 1, par, 0)

            experts(pe, expert, ((units, MT * NC), (subs, 2 * NC)))


class Shared:
    pass


def program(nc, w):
    with ExitStack() as stack:
        core = Core(nc, stack)
        at = core.at
        g = Shared()
        g.ident, g.lohi = at("ident", [128, 128], F32, 0), at("lohi", [128, 2 * NT], I32, 0.5)
        g.node_ids = at("node_ids", [128, N], F16, 1)
        g.small = 1
        ln, g.turned = NormState(core, 2.5), Turned(core)
        g.gcol, g.headflag = at("gcol", [128, KT, 2], F32, 3.5), at("headflag", [128, HEADS], F32, 3.5625)
        g.has_edge = at("has_edge", [P, NT], F32, 3.625)
        g.agg = at("edge_mean", [P, NT, EDGE_D], F32, 8)
        g.x, g.xs = at("x_first", [P, NT, D], F32, 160), at("xs_first", [P, NT, D], F32, 180)
        g.xn_hi, g.xn_lo = at("xn_hi", [P, NT, D], F32R, 12), at("xn_lo", [P, NT, D], F32R, 32)
        g.xt_hi, g.xt_lo = at("xt_hi", [128, KT, N], F32R, 52), at("xt_lo", [128, KT, N], F32R, 72)
        g.acc, g.gs_acc = at("acc", [P, NT, D], F32, 92), at("gs_acc", [128, KT, D], F32, 144)
        g.attr_sums = at("attr_sums", [P, NT, PARTS], F32, 112)
        g.counts = nc.dram_tensor("edge_counts", [N, N], U16, kind="Internal").ap()
        g.x3_store, g.xs_store, g.pre_store = (
            nc.dram_tensor(n, [N, D], F32, kind="Internal").ap() for n in ("x3_store", "xs_store", "pre_store"))

        edge_ranges(core, g, w["dst_pairs"], w["src_cols"], w["dst_cols"], w["x"], w["attr"])
        count_edges(core, g)
        first_features(core, g, ln)
        graph_attention(core, g, w)
        g.x, g.xs = at("x_res", [P, NT, D], F32, 12), at("xs_res", [P, NT, D], F32, 32)
        graph_output(core, g, w, ln)
        expert_lora(core, g, w, ln)
        edge_mean_gnn(core, g, w, ln)
        keys_values(core, g, w, ln)
        self_attention(core, g, w)
        expert_mixture(core, g, w, ln)


def lay_out(i):
    def turned(a):
        return a.swapaxes(-1, -2)

    def cols(a, *lead):
        return np.moveaxis(a.reshape(*a.shape[:-1], -1, 128), -1, 0)

    gates = np.concatenate([i["L0_ffn_gate_w"], i["L0_ffn_thr_w"], np.zeros((1, D), np.float32)])
    out = {
        "x": i["x"],
        "dst_pairs": i["dst"].reshape(EP, 2 * P), "src_cols": i["src"].reshape(2 * EP, P).T,
        "dst_cols": i["dst"].reshape(2 * EP, P).T,
        "attr": i["edge_attr_64"].reshape(2 * EP, P, EDGE_D).transpose(1, 0, 2),
        "WqT": turned(i["L0_gnn_Wq"]), "WkT": turned(i["L0_gnn_Wk"]), "WvT": turned(i["L0_gnn_Wv"]),
        "WskipT": turned(i["L0_gnn_Wskip"]), "Wlin": i["L0_gnn_Wlin"],
        "bq": cols(i["L0_gnn_bq"]), "bk": cols(i["L0_gnn_bk"]), "bv": cols(i["L0_gnn_bv"]),
        "bskip": cols(i["L0_gnn_bskip"]),
        "blin": i["L0_gnn_blin"], "gamma": i["L0_gnn_gamma"], "beta": i["L0_gnn_beta"],
        "gates": gates.reshape(6, KT, 128).transpose(2, 1, 0),
        "lora_A": i["L0_ffn_lora_A"].reshape(4, KT, 128, 16).transpose(2, 0, 1, 3),
        "lora_B": turned(i["L0_ffn_lora_B"]).reshape(4, KT, 128, 16).transpose(2, 0, 1, 3),
        "fc1T": turned(i["L0_ffn_fc1_w"]), "fc2T": turned(i["L0_ffn_fc2_w"]),
        "W1": i["L1_gnn_W1"], "b1": cols(i["L1_gnn_b1"]), "W2": i["L1_gnn_W2"], "b2": i["L1_gnn_b2"],
        "Wq2": i["L1_ffn_Wq"], "Wk2": i["L1_ffn_Wk"], "Wv2": i["L1_ffn_Wv"], "Wo": i["L1_ffn_Wo"],
        "bq2": cols(i["L1_ffn_bq"]), "bk2": cols(i["L1_ffn_bk"]), "bv2": i["L1_ffn_bv"], "bo": i["L1_ffn_bo"],
        "g1": i["L1_ffn_g1"], "beta1": i["L1_ffn_beta1"], "g2": i["L1_ffn_g2"], "beta2": i["L1_ffn_beta2"],
        "Wg": i["L1_ffn_Wg"], "bg": i["L1_ffn_bg"],
        "W1e": i["L1_ffn_W1"], "b1e": cols(i["L1_ffn_b1"].reshape(-1)), "W2e": i["L1_ffn_W2"], "b2e": i["L1_ffn_b2"],
    }
    return {name: np.ascontiguousarray(a) for name, a in out.items()}


def kernel(**inputs):
    import concourse.bacc as bacc
    from concourse.bass_utils import run_bass_kernel_spmd

    arrays = lay_out({name: np.asarray(a) for name, a in inputs.items()})
    nc = bacc.Bacc("TRN2", target_bir_lowering=False, num_devices=1)
    handles = {name: nc.dram_tensor(f"in_{name}", a.shape, mybir.dt.from_np(a.dtype), kind="ExternalInput").ap()
               for name, a in arrays.items()}
    handles["out"] = nc.dram_tensor("out", [N, D], F32, kind="ExternalOutput").ap()
    program(nc, handles)
    result = run_bass_kernel_spmd(nc, [{f"in_{name}": a for name, a in arrays.items()}], core_ids=[0])
    return result.results[0]["out"]
```

```python
from contextlib import ExitStack

import numpy as np
import concourse.bass as bass
from concourse import mybir

F32 = mybir.dt.float32
F32R = mybir.dt.float32r
BF16 = mybir.dt.bfloat16
F16 = mybir.dt.float16
U16 = mybir.dt.uint16
I32 = mybir.dt.int32
ALU = mybir.AluOpType
ACT = mybir.ActivationFunctionType
AX = mybir.AxisListType

N, D = 1250, 512
P = 125
NT = N // P
CH = 2 * P
NC = N // CH
KT = D // 128
EDGES = 21250
EP = EDGES // (2 * P)
EDGE_D = 64
PARTS = 3 * EDGE_D + 2
BANK = 512
SPANS = [(0, 512), (512, 1024), (1024, N)]
HEADS = 4
EPS = 1e-5
OFF = -1e30


class Tick:

    def __init__(self, first=0):
        self.base, self.n, self.kept = first, 0, []

    def step(self, k=1):
        self.n += k
        return self.base + self.n

    def enter(self, turn, per):
        self.kept.append((self.base, self.n, per))
        self.base, self.n = self.base + self.n + turn * per, 0

    def leave(self, turns):
        base, n, per = self.kept.pop()
        if self.n != per:
            raise AssertionError(f"a turn counts {self.n}, not {per}")
        self.base, self.n = base, n + turns * per


class Link(Tick):

    def __init__(self, eng, sem):
        super().__init__()
        self.eng, self.sem = eng, sem

    def on(self, eng):
        self.eng = eng
        return self

    def __call__(self, ins):
        ins.then_inc(self.sem, 1)
        self.eng.wait_ge(self.sem, self.step())


def bc(ap, t):
    return ap.rearrange("p (a n) -> p a n", a=1).broadcast_to([ap.shape[0], t, ap.shape[1]])


CREDITS = {"hot_free": 2, "count_copied": 2, "count_stored0": 16, "count_stored1": 16,
           "pp_free": 2, "pp_done": 1, "hm_v_free": 1, "hm_v_done1": 1, "hm_p3_done": 1, "hm_u_free": 2,
           "WqT_lo": 1, "WkT_lo": 1, "WvT_lo": 1, "Wlin_lo": 1, "WskipT_lo": 1, "qk_stored": 16, "vl_stored": 16, "s_free": 1, "tp_free": 3, "tp_done": 6,
           "cnt_free0": 1, "cnt_free1": 1, "hid_free": 2, "lora_done": 2, "lw_ready": 1, "ffn_x_added": 2,
           "gh_bank_free": 2, "gh_lo_done": 2, "gnn_x_added": 2,
           "at_e_ready": 3, "at_tp_free": 3, "at_c_free": 1, "at_summed": 1, "at_stored": 16,
           "moe_bank_free": 2, "moe_lo": 2, "moe_out_done": 2, "moe_added": 2}


class Core:

    def __init__(self, nc, stack):
        self.nc, self.stack = nc, stack
        self.bottom = -(-nc.sbuf_base // 128) * 128
        self.psum = stack.enter_context(nc.psum_tensor("psum", [128, 8, BANK], F32))
        self.link = Link(None, stack.enter_context(nc.semaphore("dve_link")))
        self.parts = []
        self.credits = {name: stack.enter_context(nc.semaphore(name)) for name in CREDITS}

    def at(self, name, shape, dtype, kb):
        return self.nc.alloc_sbuf_tensor_at(name, shape, dtype, offset=self.bottom + int(kb * 1024))

    def sem(self, name):
        if name in self.credits:
            return self.credits[name]
        self.parts.append(self.nc.alloc_semaphore(name=name))
        return self.parts[-1]

    def next_part(self):
        self.nc.clear_and_free_semaphores(self.parts)
        self.nc.all_engine_barrier()
        self.parts = []

    def bank(self, b):
        return self.psum[:, b, :]


def three_pass(nc, out, lhs, rhs, start, stop):
    (lh, ll), (rh, rl) = lhs, rhs
    nc.tensor.matmul(out, lh, rh, start=start, stop=False)
    nc.tensor.matmul(out, lh, rl, start=False, stop=False)
    return nc.tensor.matmul(out, ll, rh, start=False, stop=stop)


def layer_stats(nc, link, x, s, turn):
    for t in range(NT):
        link(nc.vector.bn_stats(s.stats[:, t, :], x[:, t, :]))
    for t in range(NT):
        link(nc.vector.bn_aggr(s.mv[:, t, :], s.stats[:, t, :]))
    nc.vector.tensor_scalar(s.ve[:], s.mv[:, :, 1], EPS, None, ALU.add).then_inc(s.var_ready, 1)
    link.eng.wait_ge(s.std_ready, turn)
    r, r2 = s.r, s.r2
    link(nc.vector.reciprocal(r[:], s.sd[:]))
    link(nc.vector.tensor_tensor(r2[:], r[:], r[:], ALU.mult))
    link(nc.vector.tensor_tensor(r2[:], r2[:], s.ve[:], ALU.mult))
    link(nc.vector.tensor_scalar(r2[:], r2[:], -0.5, 1.5, ALU.mult, ALU.add))
    link(nc.vector.tensor_tensor(r[:], r[:], r2[:], ALU.mult))


def normalise(nc, link, x, out, s, turn):
    layer_stats(nc, link, x, s, turn)
    for t in range(NT):
        link(nc.vector.tensor_scalar(out[:, t, :], x[:, t, :], s.mv[:, t, 0:1], s.r[:, t:t + 1],
                                     ALU.subtract, ALU.mult))


def affine(nc, link, x, out, s, turn, gain, shift, ready):
    layer_stats(nc, link, x, s, turn)
    for t in range(NT):
        nc.vector.scalar_tensor_tensor(x[:, t, :], x[:, t, :], s.mv[:, t, 0:1], gain[:], ALU.subtract, ALU.mult)
    link(nc.vector.memset(s.r2[:], 0.0))
    for t in range(NT):
        last = nc.vector.scalar_tensor_tensor(out[:, t, :], x[:, t, :], s.r[:, t:t + 1], shift[t], ALU.mult, ALU.add)
        if ready is None:
            link(last)
        else:
            last.then_inc(ready, 1)


class NormState:

    def __init__(self, core, kb):
        at = core.at
        self.stats = at("ln_stats", [P, NT, 6], F32, kb)
        self.mv = at("ln_mean_var", [P, NT, 2], F32, kb + 0.25)
        self.ve = at("ln_var_eps", [P, NT], F32, kb + 0.375)
        self.sd = at("ln_std", [P, NT], F32, kb + 0.5)
        self.r = at("ln_rstd", [P, NT], F32, kb + 0.625)
        self.r2 = at("ln_newton", [P, NT], F32, kb + 0.75)
        self.var_ready, self.std_ready = core.sem("ln_var_ready"), core.sem("ln_std_ready")
        self.turn = 0

    def root(self, nc, eng):
        self.root_at(nc, eng, self.turn)

    def root_at(self, nc, eng, turn):
        eng.wait_ge(self.var_ready, turn)
        nc.scalar.activation(self.sd[:], self.ve[:], ACT.Sqrt).then_inc(self.std_ready, 1)


def edge_ranges(core, g, dst_pairs, src_cols, dst_cols, x_in, attr_in):
    nc, at, sem = core.nc, core.at, core.sem
    base = 140
    g.src_i = at("src_i", [P, 2 * EP], I32, base)
    g.dst_i = at("dst_i", [P, 2 * EP], I32, base + 1)
    dst_p = at("dst_pairs", [EP, 2 * P], I32, base + 2)
    g.src_f = at("src_f", [P, 2 * EP], F32, base + 3)
    g.dst_f = at("dst_f", [P, 2 * EP], F32, base + 4)
    small = at("range_small", [128, 8], F32, base + 5)
    tile_first = at("tile_first", [128, NT], F32, base + 5.25)
    hit = at("hit", [128, NT], F32, base + 5.5)
    cand = at("cand", [128, 2 * NT], F32, base + 5.75)
    best = at("best", [128, 2 * NT], F32, base + 6)
    lohi_f = at("lohi_f", [128, 2 * NT], F32, base + 6.25)
    s_load, s_iota, s_cand, s_best = sem("edges_loaded"), sem("range_iota"), sem("range_cand"), sem("range_best")
    s_pool = sem("range_pool")
    g.node_i = at("node_ids_i", [128, N], I32, base + 7)
    g.ids_ready, g.x_loaded = sem("ids_ready"), sem("x_loaded")
    attr = at("edge_attr", [P, 2 * EP, EDGE_D], F32, 84)
    g.parts = at("edge_parts", [P, 2 * EP, PARTS], BF16, 12)
    HALF = EP
    halves = [slice(i * HALF, (i + 1) * HALF) for i in range(2)]
    attr_loaded = [sem("attr_loaded0"), sem("attr_loaded1")]
    part_ready, rest_ready = sem("part_ready"), sem("rest_ready")

    with nc.Block() as block:
        @block.sync
        def _(sp):
            for name, n in CREDITS.items():
                sp.sem_inc(core.credits[name], n)
            sp.dma_start(dst_p[:], dst_pairs).then_inc(s_load, 16)
            sp.dma_start(g.dst_i[:], dst_cols).then_inc(s_load, 16)
            sp.dma_start(g.src_i[:], src_cols).then_inc(s_load, 16)
            for i, h in enumerate(halves):
                sp.dma_start(attr[:, h, :], attr_in[:, h, :]).then_inc(attr_loaded[i], 16)
            sp.dma_start(g.x[:], x_in.rearrange("(t p) d -> p t d", p=P)).then_inc(g.x_loaded, 16)

        @block.gpsimd
        def _(pool):
            nc.gpsimd.memset(g.ident[:], 0.0).then_inc(s_pool, 1)
            nc.gpsimd.memset(cand[:], 0.0).then_inc(s_iota, 1)
            nc.gpsimd.iota(tile_first[:], pattern=[[P, NT]], base=0, channel_multiplier=0,
                           allow_small_or_imprecise_dtypes=True).then_inc(s_iota, 1)
            nc.gpsimd.iota(small[:, 0:1], pattern=[[0, 1]], base=1, channel_multiplier=1,
                           allow_small_or_imprecise_dtypes=True).then_inc(s_iota, 1)
            nc.gpsimd.iota(g.node_ids[:], pattern=[[1, N]], base=0, channel_multiplier=0,
                           allow_small_or_imprecise_dtypes=True).then_inc(g.ids_ready, 1)
            pool.wait_ge(s_pool, 1)
            nc.gpsimd.affine_select(out=g.ident[:], in_=g.ident[:], compare_op=ALU.not_equal, fill=1.0,
                                    base=0, pattern=[[-1, 128]], channel_multiplier=1).then_inc(s_pool, 1)
            pool.wait_ge(s_cand, 1)
            nc.gpsimd.partition_all_reduce(best[:], cand[:], 128, bass.bass_isa.ReduceOp.max).then_inc(s_best, 1)

        @block.scalar
        def _(act):
            for n in range(3):
                for i, h in enumerate(halves):
                    if n == 0:
                        act.wait_ge(attr_loaded[i], 16)
                    else:
                        act.wait_ge(rest_ready, 2 * (n - 1) + i + 1)
                    nc.scalar.activation(g.parts[:, h, n * EDGE_D:(n + 1) * EDGE_D], attr[:, h, :],
                                         ACT.Copy).then_inc(part_ready, 1)

        @block.vector
        def _(dve):
            link = core.link.on(dve)
            nc.vector.memset(g.parts[:, :, 3 * EDGE_D:], 1.0)
            dve.wait_ge(s_load, 48)
            dve.wait_ge(s_iota, 3)
            nc.vector.tensor_copy(g.dst_f[:], g.dst_i[:])
            nc.vector.tensor_copy(g.src_f[:], g.src_i[:])
            link(nc.vector.tensor_reduce(small[0:EP, 1:2], dst_p[:], AX.X, ALU.max))
            link(nc.vector.tensor_reduce(small[0:EP, 2:3], dst_p[:], AX.X, ALU.min))
            link(nc.vector.tensor_scalar(small[0:EP, 3:4], small[0:EP, 0:1], -1.0, EP + 1.0, ALU.mult, ALU.add))
            link(nc.vector.tensor_scalar(hit[0:EP, :], tile_first[0:EP, :], small[0:EP, 1:2], None, ALU.is_le))
            link(nc.vector.tensor_scalar(cand[0:EP, 0:NT], tile_first[0:EP, :], float(P), small[0:EP, 2:3],
                                         ALU.add, ALU.is_gt))
            link(nc.vector.tensor_tensor(hit[0:EP, :], hit[0:EP, :], cand[0:EP, 0:NT], ALU.mult))
            link(nc.vector.tensor_scalar(cand[0:EP, 0:NT], hit[0:EP, :], small[0:EP, 0:1], None, ALU.mult))
            nc.vector.tensor_scalar(cand[0:EP, NT:], hit[0:EP, :], small[0:EP, 3:4], None,
                                    ALU.mult).then_inc(s_cand, 1)
            dve.wait_ge(s_best, 1)
            hi, lo = lohi_f[:, NT:], lohi_f[:, 0:NT]
            link(nc.vector.tensor_scalar(hi, best[:, 0:NT], 1.0, None, ALU.max))
            link(nc.vector.tensor_scalar(lo, best[:, NT:], -1.0, float(EP), ALU.mult, ALU.add))
            link(nc.vector.tensor_scalar(cand[:, 0:NT], hi, -1.0, None, ALU.add))
            link(nc.vector.tensor_tensor(lo, lo, cand[:, 0:NT], ALU.min))
            link(nc.vector.tensor_copy(g.lohi[:], lohi_f[:]))
            for n in range(2):
                for i, h in enumerate(halves):
                    dve.wait_ge(part_ready, 2 * n + i + 1)
                    nc.vector.tensor_tensor(attr[:, h, :], attr[:, h, :], g.parts[:, h, n * EDGE_D:(n + 1) * EDGE_D],
                                            ALU.subtract).then_inc(rest_ready, 1)


def pair_range(eng, g, t):
    lo = eng.value_load(g.lohi[0:1, bass.ds(t, 1)], min_val=0, max_val=EP - 1)
    hi = eng.value_load(g.lohi[0:1, bass.ds(t + NT, 1)], min_val=1, max_val=EP)
    return lo, hi


def count_edges(core, g):
    nc, at, sem = core.nc, core.at, core.sem
    base = 84
    hot_src = at("hot_src", [P, 2, N], BF16, base)
    hot_dst = at("hot_dst", [P, 2, 128], BF16, base + 6)
    zero = at("zero_bf", [128, BANK], BF16, base + 7)
    sums = g.attr_sums
    out = at("counts_out", [P, 2, N], U16, base + 9)
    ready, free = sem("hot_ready"), sem("hot_free")
    tile_done = sem("count_tile_done")
    copied, zeroed = sem("count_copied"), sem("zeroed")
    stored = [sem("count_stored0"), sem("count_stored1")]
    rows = g.counts.rearrange("(t p) s -> t p s", p=P)

    with nc.Block() as block:
        @block.vector
        def _(dve):
            nc.vector.memset(zero[:], 0.0).then_inc(zeroed, 1)
            dve.wait_ge(g.ids_ready, 1)
            turn = dve.alloc_register("hot_turn_dve")
            dve.reg_mov(turn, 1)
            with dve.Fori(0, NT) as t:
                lo, hi = pair_range(dve, g, t)
                with dve.Fori(lo, hi) as j:
                    for a in range(2):
                        dve.wait_ge(free, turn)
                        dve.reg_add(turn, turn, 1)
                        nc.vector.tensor_scalar(hot_src[:, a, :], g.node_ids[0:P, :], g.src_f[:, bass.ds(2 * j + a, 1)],
                                                None, ALU.is_equal)
                        nc.vector.tensor_scalar(hot_dst[:, a, 0:P], g.node_ids[0:P, bass.ds(t * P, P)],
                                                g.dst_f[:, bass.ds(2 * j + a, 1)], None,
                                                ALU.is_equal).then_inc(ready, 1)

        @block.tensor
        def _(pe):
            pe.wait_ge(zeroed, 1)
            turn = pe.alloc_register("hot_turn_pe")
            pe.reg_mov(turn, 1)
            with pe.Fori(0, NT // 2) as t2:
                for par in range(2):
                    lo, hi = pair_range(pe, g, 2 * t2 + par)
                    acc = core.psum[0:P, 3 * par:3 * par + 3, :].rearrange("p b n -> p (b n)")
                    pe.wait_ge(copied, 2 * t2 + par + 1)
                    att = core.bank(6 + par)[0:P, 0:PARTS]
                    for a, b in SPANS:
                        nc.tensor.matmul(acc[:, a:b], zero[:, 0:P], zero[:, 0:b - a], start=True, stop=False)
                    nc.tensor.matmul(att, zero[:, 0:P], zero[:, 0:PARTS], start=True, stop=False)
                    with pe.Fori(lo, hi) as j:
                        for s in range(2):
                            pe.wait_ge(ready, turn)
                            pe.reg_add(turn, turn, 1)
                            for a, b in SPANS:
                                nc.tensor.matmul(acc[:, a:b], hot_dst[:, s, 0:P], hot_src[:, s, a:b],
                                                 start=False, stop=False)
                            last = nc.tensor.matmul(att, hot_dst[:, s, 0:P],
                                                    g.parts[:, bass.ds(2 * j + s, 1), :].rearrange("p a n -> p (a n)"),
                                                    start=False, stop=False)
                            last.then_inc(free, 1)
                    for a, b in SPANS:
                        nc.tensor.matmul(acc[:, a:b], zero[:, 0:P], zero[:, 0:b - a], start=False, stop=True)
                    last = nc.tensor.matmul(att, zero[:, 0:P], zero[:, 0:PARTS], start=False, stop=True)
                    last.then_inc(tile_done, 1)

        @block.scalar
        def _(act):
            with act.Fori(0, NT // 2) as t2:
                for par in range(2):
                    acc = core.psum[0:P, 3 * par:3 * par + 3, :].rearrange("p b n -> p (b n)")
                    act.wait_ge(tile_done, 2 * t2 + par + 1)
                    act.wait_ge(stored[par], 16 * t2 + 16)
                    nc.scalar.activation(sums[:, bass.ds(2 * t2 + par, 1), :].rearrange("p a n -> p (a n)"),
                                         core.bank(6 + par)[0:P, 0:PARTS], ACT.Copy)
                    nc.scalar.activation(out[:, par, :], acc[:, 0:N], ACT.Copy).then_inc(copied, 1)
            
        @block.sync
        def _(sp):
            with sp.Fori(0, NT // 2) as t2:
                for par in range(2):
                    sp.wait_ge(copied, 2 * t2 + par + 3)
                    sp.dma_start(rows[bass.ds(2 * t2 + par, 1), :, :].rearrange("a p s -> (a p) s"),
                                 out[:, par, :]).then_inc(stored[par], 16)
            for par in range(2):
                sp.wait_ge(stored[par], 16 * (NT // 2) + 16)


def f32(ap):
    return ap.bitcast(F32)


class Turned:

    def __init__(self, core):
        self.done, self.hi, self.lo = (core.sem(f"turned{x}") for x in ("", "_hi", "_lo"))
        self.before = -NT

    def again(self):
        self.before += NT
        return self

    def bank(self, core, t):
        return core.bank(t % 8)[:, 0:KT * P].rearrange("p (k n) -> p k n", k=KT)

    def tensor(self, core, pe, xs, ident):
        for t in range(NT):
            if t >= 8:
                pe.wait_ge(self.lo, self.before + t - 7)
            for k in range(KT):
                last = core.nc.tensor.transpose(self.bank(core, t)[:, k, :], xs[:, t, k * 128:(k + 1) * 128],
                                                ident[0:P, 0:P])
            last.then_inc(self.done, 1)

    def scalar(self, core, act, hi):
        for t in range(NT):
            act.wait_ge(self.done, self.before + t + 1)
            core.nc.scalar.activation(hi[:, :, t * P:(t + 1) * P], self.bank(core, t),
                                      ACT.Copy).then_inc(self.hi, 1)

    def vector(self, core, dve, hi, lo):
        for t in range(NT):
            dve.wait_ge(self.hi, self.before + t + 1)
            core.nc.vector.tensor_tensor(lo[:, :, t * P:(t + 1) * P], self.bank(core, t),
                                         f32(hi[:, :, t * P:(t + 1) * P]), ALU.subtract).then_inc(self.lo, 1)


def first_features(core, g, ln):
    nc, at, sem = core.nc, core.at, core.sem
    turned = g.turned.again()
    u_hi, u_lo = at("u_hi", [128, HEADS * KT], F32R, g.small), at("u_lo", [128, HEADS * KT], F32R, g.small + .125)
    bqk, bqbk = at("bqk_cols", [128, HEADS * KT], F32, g.small + .25), at("bqbk", [P, HEADS], F32, g.small + .375)
    ones = at("ones_cd", [128, P], F32, g.small + .5)
    u_hi_done, u_ready, cd_done = sem("f0_u_hi"), sem("f0_u_ready"), sem("f0_cd_done")
    xs_ready, nm_hi = sem("f0_xs"), sem("f0_nm_hi")
    ln.turn += 1
    with nc.Block() as block:
        @block.vector
        def _(dve):
            link = core.link.on(dve)
            dve.wait_ge(g.x_loaded, 16)
            normalise(nc, link, g.x, g.xs, ln, ln.turn)
            link(nc.vector.memset(g.acc[:], 0.0))
            sums, cnt = g.attr_sums, g.attr_sums[:, :, 3 * EDGE_D:3 * EDGE_D + 1]
            link(nc.vector.tensor_tensor(g.agg[:], sums[:, :, 0:EDGE_D], sums[:, :, EDGE_D:2 * EDGE_D], ALU.add))
            link(nc.vector.tensor_tensor(g.agg[:], g.agg[:], sums[:, :, 2 * EDGE_D:3 * EDGE_D], ALU.add))
            link(nc.vector.tensor_scalar(cnt, cnt, 1.0, None, ALU.max))
            link(nc.vector.reciprocal(cnt, cnt))
            link(nc.vector.tensor_tensor(g.agg[:], g.agg[:], cnt.broadcast_to([P, NT, EDGE_D]), ALU.mult))
            link(nc.vector.tensor_tensor(bqk[:], g.bq[:], g.bk[:], ALU.mult))
            nc.vector.memset(ones[:], 1.0).then_inc(xs_ready, 1)
            dve.wait_ge(nm_hi, 1)
            nc.vector.tensor_tensor(g.xn_lo[:], g.xs[:], f32(g.xn_hi[:]), ALU.subtract)
            dve.wait_ge(u_hi_done, 1)
            nc.vector.tensor_tensor(u_lo[:], g.ucols[:], f32(u_hi[:]), ALU.subtract).then_inc(u_ready, 1)
            turned.vector(core, dve, g.xt_hi, g.xt_lo)
            dve.wait_ge(cd_done, 1)
            link(nc.vector.tensor_reduce(bqbk[:], core.bank(1)[0:P, 0:HEADS * KT].rearrange("p (h k) -> p h k", k=KT),
                                         AX.X, ALU.add))
            nc.vector.tensor_tensor(g.cd[:].rearrange("p (t h) -> p t h", h=HEADS),
                                    core.bank(0)[0:P, 0:NT * HEADS].rearrange("p (t h) -> p t h", h=HEADS),
                                    bc(bqbk[:], NT), ALU.add)

        @block.scalar
        def _(act):
            nc.scalar.activation(u_hi[:], g.ucols[:], ACT.Copy).then_inc(u_hi_done, 1)
            ln.root(nc, act)
            act.wait_ge(xs_ready, 1)
            nc.scalar.activation(g.xn_hi[:], g.xs[:], ACT.Copy).then_inc(nm_hi, 1)
            turned.scalar(core, act, g.xt_hi)

        @block.tensor
        def _(pe):
            pe.wait_ge(xs_ready, 1)
            turned.tensor(core, pe, g.xs, g.ident)
            pe.wait_ge(u_ready, 1)
            pe.wait_ge(turned.lo, turned.before + NT)
            for t in range(NT):
                for k in range(KT):
                    three_pass(nc, core.bank(0)[0:P, HEADS * t:HEADS * t + HEADS],
                               [a[:, k, t * P:(t + 1) * P] for a in (g.xt_hi, g.xt_lo)],
                               [a[:].rearrange("p (h k) -> p k h", k=KT)[:, k, :] for a in (u_hi, u_lo)],
                               k == 0, k == KT - 1)
            nc.tensor.matmul(core.bank(1)[0:P, 0:HEADS * KT], ones[:], bqk[:], start=True, stop=True).then_inc(cd_done, 1)


def head_matrices(core, g, w):
    nc, at, sem = core.nc, core.at, core.sem
    names = ("WqT", "WkT", "WvT", "Wlin", "WskipT")
    Q, K, V, LIN, SKIP = range(5)
    raw = [at(f"raw_{n}", [128, KT, D], F32, kb) for n, kb in zip(names, (120, 128, 136, 144, 196))]
    halves = [[at(f"{n}_{x}", [128, KT, D], F32R, 20 + 16 * i + 8 * j) for j, x in enumerate(("hi", "lo"))]
              for i, n in enumerate(names)]
    out = [at("qk_out0", [128, KT, D], F32, 12), at("vl_out0", [128, KT, D], F32, 100)]
    zero = at("zero_head", [128, D], BF16, 180)
    bvs = at("bvs_cols", [128, 2, HEADS * KT], F32, g.small)
    raw_in = [sem(f"{n}_in") for n in names]
    split_hi, split_lo_ = sem("hm_hi"), [sem(f"{n}_lo") for n in names]
    v_done, v_free, zeroed = [sem("hm_v_done0"), sem("hm_v_done1")], sem("hm_v_free"), sem("hm_zeroed")
    lin_ready, p3_done = sem("hm_lin_ready"), sem("hm_p3_done")
    u_done, u_free = sem("hm_u_done"), sem("hm_u_free")
    stored = [sem("qk_stored"), sem("vl_stored")]
    flag, gs_ready, gs_stored = sem("hm_flag"), sem("hm_gs_ready"), sem("hm_gs_stored")
    bank = lambda u: core.bank(4 + u % 2)
    stores = (g.qk_store, g.vl_store)

    def wview(ap, h):
        return ap.rearrange("(h k p) n -> h p k n", p=128, k=KT)[bass.ds(h, 1)].rearrange("a p k n -> (a p) k n")

    with nc.Block() as block:
        @block.sync
        def _(sp):
            for dst, name in ((g.bq[:], "bq"), (g.bk[:], "bk"), (bvs[:, 0, :], "bv"), (bvs[:, 1, :], "bskip")):
                sp.dma_start(dst, w[name]).then_inc(g.cols_in, 16)
            with sp.Fori(0, HEADS) as h:
                for i in (Q, K, V, LIN, SKIP):
                    if i in (Q, K):
                        sp.wait_ge(v_free, h + 1)
                    elif i == LIN:
                        sp.wait_ge(v_done[1], h + 1)
                        sp.wait_ge(split_lo_[i], h + 1)
                    else:
                        sp.wait_ge(split_lo_[i], h + 1)
                    sp.dma_start(raw[i][:], wview(w[names[i]], h)).then_inc(raw_in[i], 16)
            sp.wait_ge(gs_ready, 1)
            sp.dma_start(g.gs_store, g.gs_acc[:]).then_inc(gs_stored, 16)
            sp.wait_ge(gs_stored, 16)

        @block.scalar
        def _(act):
            def hi(i, h):
                act.wait_ge(raw_in[i], 16 * h + 16)
                if i == LIN:
                    act.wait_ge(lin_ready, h + 1)
                    act.wait_ge(p3_done, h + 1)
                nc.scalar.activation(halves[i][0][:], raw[i][:], ACT.Copy).then_inc(split_hi, 1)

            units = Tick()
            with act.Fori(0, HEADS) as h:
                units.enter(h, 2 * KT)
                hi(Q, h), hi(K, h), hi(V, h), hi(LIN, h)
                for i in range(2):
                    if i == 1:
                        hi(SKIP, h)
                    act.wait_ge(stored[i], 16 * h + 16)
                    for m in range(KT):
                        act.wait_ge(u_done, units.step())
                        nc.scalar.activation(out[i][:, m, :], bank(m), ACT.Copy).then_inc(u_free, 1)
                    act.wait_ge(u_free, 2 + units.base + units.n)
                    act.dma_start(stores[i][bass.ds(h, 1)].rearrange("a p k n -> (a p) k n"),
                                  out[i][:]).then_inc(stored[i], 16)
                units.leave(HEADS)
            for i in range(2):
                act.wait_ge(stored[i], 16 * HEADS + 16)

        @block.vector
        def _(dve):
            nc.vector.memset(zero[:], 0.0).then_inc(zeroed, 1)
            nc.vector.memset(g.headflag[:], 0.0).then_inc(flag, 1)
            dve.wait_ge(flag, 1)
            nc.vector.memset(g.headflag[:, 0:1], 1.0).then_inc(flag, 1)
            dve.wait_ge(flag, 2)
            his = Tick()

            def lo(i):
                dve.wait_ge(split_hi, his.step())
                nc.vector.tensor_tensor(halves[i][1][:], raw[i][:], f32(halves[i][0][:]),
                                        ALU.subtract).then_inc(split_lo_[i], 1)

            with dve.Fori(0, HEADS) as h:
                his.enter(h, 5)
                dve.wait_ge(raw_in[LIN], 16 * h + 16)
                for k in range(KT):
                    blk = raw[LIN][:, k, k * 128:(k + 1) * 128]
                    last = nc.vector.scalar_tensor_tensor(blk, g.ident[:], g.headflag[:, bass.ds(h, 1)], blk,
                                                          ALU.mult, ALU.add)
                last.then_inc(lin_ready, 1)
                lo(Q), lo(K), lo(V), lo(LIN)
                dve.wait_ge(v_done[0], h + 1)
                nc.vector.tensor_copy(g.tcols[:, bass.ds(KT * h, KT)], core.bank(6)[:, 0:KT])
                nc.vector.tensor_copy(g.ucols[:, bass.ds(KT * h, KT)], core.bank(6)[:, KT:2 * KT]).then_inc(v_free, 1)
                lo(SKIP)
                his.leave(HEADS)
            dve.wait_ge(p3_done, HEADS + 2)
            nc.vector.tensor_copy(g.gcol[:], core.bank(7)[:, 0:2 * KT].rearrange("p (k i) -> p k i", i=2))
            nc.vector.tensor_copy(g.gs_acc[:], core.psum[:, 0:KT, :]).then_inc(gs_ready, 1)

        @block.tensor
        def _(pe):
            units = Tick()
            pe.wait_ge(zeroed, 1)
            for b in (0, 1, 2, 3, 7):
                nc.tensor.matmul(core.bank(b), zero[:, 0:128], zero[:], start=True, stop=False)

            def product(i, j, out_of, before=None):
                for m in range(KT):
                    dst = out_of(m)
                    for k in range(KT):
                        last = three_pass(nc, dst, [x[:, k, m * 128:(m + 1) * 128] for x in halves[i]],
                                          [x[:, k, :] for x in halves[j]], before is None and k == 0,
                                          before is None and k == KT - 1)
                    if before is None:
                        last.then_inc(u_done, 1)
                return last

            def unit(m):
                pe.wait_ge(u_free, units.step())
                return bank(m)

            pe.wait_ge(g.cols_in, 64)
            with pe.Fori(0, HEADS) as h:
                units.enter(h, 2 * KT)
                pe.wait_ge(v_free, h + 1)
                pe.wait_ge(raw_in[Q], 16 * h + 16)
                pe.wait_ge(raw_in[K], 16 * h + 16)
                for c, (i, bias) in enumerate(((K, g.bq), (Q, g.bk))):
                    for m in range(KT):
                        for k in range(KT):
                            last = nc.tensor.matmul(core.bank(6)[:, c * KT + m:c * KT + m + 1],
                                                    raw[i][:, k, m * 128:(m + 1) * 128],
                                                    bias[:, bass.ds(KT * h + k, 1)], start=k == 0, stop=k == KT - 1)
                last.then_inc(v_done[0], 1)
                pe.wait_ge(split_lo_[Q], h + 2)
                pe.wait_ge(split_lo_[K], h + 2)
                product(Q, K, unit)
                pe.wait_ge(lin_ready, h + 1)
                for m in range(KT):
                    for k in range(KT):
                        last = nc.tensor.matmul(core.bank(7)[:, 2 * m:2 * m + 2], raw[LIN][:, k, m * 128:(m + 1) * 128],
                                                bvs[:, :, bass.ds(KT * h + k, 1)].rearrange("p i a -> p (i a)"),
                                                start=False, stop=False)
                last.then_inc(v_done[1], 1)
                pe.wait_ge(split_lo_[V], h + 2)
                pe.wait_ge(split_lo_[LIN], h + 2)
                product(V, LIN, unit)
                pe.wait_ge(split_lo_[SKIP], h + 2)
                product(SKIP, LIN, core.bank, before=True).then_inc(p3_done, 1)
                units.leave(HEADS)
            for b in (0, 1, 2, 3, 7):
                last = nc.tensor.matmul(core.bank(b), zero[:, 0:128], zero[:], start=False, stop=True)
            last.then_inc(p3_done, 1)


def graph_attention(core, g, w):
    nc, at, sem = core.nc, core.at, core.sem
    scale = 1.0 / np.sqrt(float(D)).item()
    m_hi, m_lo = at("qk_hi", [128, KT, D], F32R, 112), at("qk_lo", [128, KT, D], F32R, 120)
    g_hi, g_lo = at("vl_hi", [128, KT, D], F32R, 128), at("vl_lo", [128, KT, D], F32R, 136)
    g.g_hi, g.g_lo = g_hi, g_lo
    raw1 = at("raw1", [128, KT, D], F32, 152)
    R = 160
    t_hi, t_lo = at("t_hi", [128, KT, CH], F32R, R), at("t_lo", [128, KT, CH], F32R, R + 4)
    yt_hi, yt_lo = at("yt_hi", [128, KT, CH], F32R, 144), at("yt_lo", [128, KT, CH], F32R, 148)
    pt_hi, pt_lo = at("pt_hi", [P, NT, CH], F32R, R + 8), at("pt_lo", [P, NT, CH], F32R, R + 18)
    prob = at("prob", [P, 2, N], F32, R + 28)
    cnt = at("cnt", [P, 2, N], U16, R + 38)
    maskb = at("maskb", [P, N], BF16, R + 43)
    S = g.small
    mx, mxc, nb = (at(n, [P, 2], F32, S + i / 32) for i, n in enumerate(("mx", "mxc", "nb")))
    den, rden = (at(n, [P, 2], F32, S + .125 + i / 32) for i, n in enumerate(("den", "rden")))

    raw_in, raw_free, split_hi = sem("heads_in"), sem("heads_free"), sem("heads_hi")
    pp_done, pp_free, pp_hi = sem("pp_done"), sem("pp_free"), sem("pp_hi")
    s_done, s_free, m_ready, e_ready = sem("s_done"), sem("s_free"), sem("m_ready"), sem("e_ready")
    p_ready, tcol_ready = sem("p_ready"), sem("tcol_ready")
    tcol = at("t_col", [128, KT], F32, g.small + .5)
    tp_done, tp_hi, tp_free = sem("tp_done"), sem("tp_hi"), sem("tp_free")
    cl, c_free = [sem("cnt_loaded0"), sem("cnt_loaded1")], [sem("cnt_free0"), sem("cnt_free1")]

    UNITS = 10 * NC
    bank = lambda u: core.bank(6 + u % 2)
    score = core.psum[0:P, 0:3, :].rearrange("p b n -> p (b n)")
    rows = g.counts.rearrange("(t p) s -> t p s", p=P)
    PIECES = [(0, 4), (4, 8), (8, 10)]

    def piece(q):
        j0, j1 = PIECES[q]
        return core.bank(3 + q)[0:P, 0:(j1 - j0) * P].rearrange("p (j n) -> p j n", n=P)

    def pipeline(eng, chunk, last_outputs, vl_split, counts):
        chunk(0, 0, None, False)
        vl_split(0)
        with eng.Fori(0, HEADS - 1) as h:
            for tick, per in counts:
                tick.enter(h, NC * per)
            with eng.Fori(1, NC - 1) as c:
                for tick, per in counts:
                    tick.enter(c - 1, per)
                chunk(h, c, c - 1, False)
                for tick, per in counts:
                    tick.leave(NC - 2)
            chunk(h, NC - 1, NC - 2, True)
            chunk(h + 1, 0, NC - 1, False)
            vl_split(h + 1)
            for tick, per in counts:
                tick.leave(HEADS - 1)
        with eng.Fori(1, NC) as c:
            for tick, per in counts:
                tick.enter(c - 1, per)
            chunk(HEADS - 1, c, c - 1, False)
            for tick, per in counts:
                tick.leave(NC - 1)
        last_outputs()

    with nc.Block() as block:
        @block.sync
        def _(sp):
            def matrix_in(store, h):
                src = store[bass.ds(h, 1)].rearrange("a p k n -> (a p) k n")
                sp.dma_start(raw1[:], src).then_inc(raw_in, 16)

            def counts_in(h, c):
                for s in range(2):
                    sp.wait_ge(c_free[s], NC * h + c + 1)
                    sp.dma_start(cnt[:, s, :], rows[bass.ds(2 * c + s, 1), :, :].rearrange("a p s -> (a p) s")
                                 ).then_inc(cl[s], 16)

            matrix_in(g.qk_store, 0)
            sp.wait_ge(raw_free, 1)
            matrix_in(g.vl_store, 0)
            counts_in(0, 0)
            with sp.Fori(0, HEADS - 1) as h:
                sp.wait_ge(raw_free, 2 * h + 2)
                matrix_in(g.qk_store, h + 1)
                with sp.Fori(1, NC) as c:
                    counts_in(h, c)
                sp.wait_ge(raw_free, 2 * h + 3)
                matrix_in(g.vl_store, h + 1)
                counts_in(h + 1, 0)
            with sp.Fori(1, NC) as c:
                counts_in(HEADS - 1, c)

        @block.scalar
        def _(act):
            pp, tp, sub = Tick(), Tick(), Tick()

            def split_in(value, dst):
                act.wait_ge(raw_in, 16 * value)
                nc.scalar.activation(dst[:], raw1[:], ACT.Copy).then_inc(split_hi, 1)

            def unit_to(dst, rows_=128, n=D, bias=None):
                act.wait_ge(pp_done, 1 + pp.step())
                src = bank((pp.n - 1))[0:rows_, 0:n]
                if bias is None:
                    ins = nc.scalar.activation(dst, src, ACT.Copy)
                else:
                    ins = nc.scalar.activation(dst, src, ACT.Identity, bias=bias)
                ins.then_inc(pp_hi, 1)

            def t_units(h, c):
                if isinstance(c, int) and c == 0:
                    nc.scalar.activation(tcol[:], g.tcols[:, bass.ds(KT * h, KT)], ACT.Copy).then_inc(tcol_ready, 1)
                    act.wait_ge(tcol_ready, h + 1)
                for m in range(KT):
                    unit_to(t_hi[:, m, :], n=CH, bias=tcol[:, m:m + 1])

            def exponentials(s):
                act.wait_ge(m_ready, sub.step())
                nc.scalar.activation(prob[:, s, :], prob[:, s, :], ACT.Exp, bias=nb[:, s:s + 1],
                                     scale=scale).then_inc(e_ready, 1)

            def y_unit(m):
                unit_to(yt_hi[:, m, :], n=CH)

            def turn_hi(s):
                for q, (j0, j1) in enumerate(PIECES):
                    act.wait_ge(tp_done, 6 + tp.step())
                    nc.scalar.activation(pt_hi[:, j0:j1, s * P:(s + 1) * P], piece(q), ACT.Copy).then_inc(tp_hi, 1)

            def chunk(h, c, before, split):
                units = [lambda m=m: y_unit(m) for m in range(KT)] if before is not None else [lambda: None] * KT
                t_units(h, c)
                units[0]()
                exponentials(0)
                units[1](), units[2]()
                exponentials(1)
                units[3]()
                turn_hi(0)
                if split:
                    split_in(2 * h + 3, m_hi)
                if before is not None:
                    pp.step(2)
                turn_hi(1)

            def last_outputs():
                for m in range(KT):
                    y_unit(m)
                pp.step(2)

            split_in(1, m_hi)
            pipeline(act, chunk, last_outputs, lambda h: split_in(2 * h + 2, g_hi), ((pp, 10), (tp, 6), (sub, 2)))

        @block.vector
        def _(dve):
            link = core.link.on(dve)
            pp, tp, sub, hi = Tick(), Tick(), Tick(), Tick()

            def split_lo(value, dst_hi, dst_lo):
                dve.wait_ge(split_hi, value)
                nc.vector.tensor_tensor(dst_lo[:], raw1[:], f32(dst_hi[:]), ALU.subtract).then_inc(raw_free, 1)

            def unit():
                v = pp.step()
                return v, bank(pp.n - 1)

            def unit_lo(dst_hi, dst_lo, n=D, bias=None):
                _, b = unit()
                dve.wait_ge(pp_hi, hi.step())
                if bias is None:
                    ins = nc.vector.tensor_tensor(dst_lo, b[:, 0:n], f32(dst_hi), ALU.subtract)
                else:
                    ins = nc.vector.scalar_tensor_tensor(dst_lo, b[:, 0:n], bias, f32(dst_hi), ALU.add, ALU.subtract)
                ins.then_inc(pp_free, 1)

            def t_units(h):
                for m in range(KT):
                    unit_lo(t_hi[:, m, :], t_lo[:, m, :], CH, g.tcols[:, bass.ds(KT * h + m, 1)])

            def y_unit(m):
                unit_lo(yt_hi[:, m, :], yt_lo[:, m, :], CH)

            def mask(s, it):
                dve.wait_ge(cl[s], 16 * it + 16)
                link(nc.vector.tensor_scalar(maskb[:], cnt[:, s, :], 0.0, OFF, ALU.is_equal, ALU.mult))

            def maximum(s, const):
                v = sub.step()
                dve.wait_ge(tp_done, 3 * v)
                dve.wait_ge(s_done, v)
                nc.vector.memset(mxc[:, s:s + 1], 0.0)
                nc.vector.tensor_tensor_reduce(out=prob[:, s, :], in0=score[:, 0:N], in1=maskb[:], scale=1.0,
                                               scalar=-3e38, op0=ALU.add, op1=ALU.max,
                                               accum_out=mx[:, s:s + 1]).then_inc(s_free, 1)
                dve.wait_ge(s_free, v + 1)
                link(nc.vector.tensor_tensor(mxc[:, s:s + 1], mx[:, s:s + 1], const, ALU.add))
                nc.vector.tensor_scalar(nb[:, s:s + 1], mxc[:, s:s + 1], const, -scale,
                                        ALU.subtract, ALU.mult).then_inc(m_ready, 1)

            def normalise_sum(s, it, tile):
                dve.wait_ge(e_ready, sub.base + sub.n)
                nc.vector.tensor_tensor_reduce(out=prob[:, s, :], in0=prob[:, s, :], in1=cnt[:, s, :], scale=1.0,
                                               scalar=0.0, op0=ALU.mult, op1=ALU.add,
                                               accum_out=den[:, s:s + 1]).then_inc(c_free[s], 1)
                dve.wait_ge(c_free[s], it + 2)
                link(nc.vector.tensor_scalar(g.has_edge[:, bass.ds(tile, 1)], den[:, s:s + 1], 0.5, None, ALU.is_ge))
                link(nc.vector.tensor_scalar(den[:, s:s + 1], den[:, s:s + 1], 0.5, None, ALU.max))
                link(nc.vector.reciprocal(rden[:, s:s + 1], den[:, s:s + 1]))
                nc.vector.tensor_scalar(prob[:, s, :], prob[:, s, :], rden[:, s:s + 1], None,
                                        ALU.mult).then_inc(p_ready, 1)

            def turn_lo(s):
                for q, (j0, j1) in enumerate(PIECES):
                    dve.wait_ge(tp_hi, tp.step())
                    nc.vector.tensor_tensor(pt_lo[:, j0:j1, s * P:(s + 1) * P], piece(q),
                                            f32(pt_hi[:, j0:j1, s * P:(s + 1) * P]), ALU.subtract).then_inc(tp_free, 1)

            def add_out(c):
                for s in range(2):
                    v, b = unit()
                    dve.wait_ge(pp_done, 1 + v)
                    dst = g.acc[:, bass.ds(2 * c + s, 1), :].rearrange("p a n -> p (a n)")
                    nc.vector.tensor_tensor(dst, dst, b[0:P, :], ALU.add).then_inc(pp_free, 1)

            def chunk(h, c, before, split):
                def y(m):
                    if before is not None:
                        y_unit(m)

                it = NC * h + c
                const = [g.cd[:, bass.ds(HEADS * (2 * c + s) + h, 1)] for s in range(2)]
                t_units(h)
                mask(0, it)
                y(0)
                maximum(0, const[0])
                y(1)
                normalise_sum(0, it, 2 * c)
                y(2)
                mask(1, it)
                maximum(1, const[1])
                y(3)
                normalise_sum(1, it, 2 * c + 1)
                turn_lo(0)
                if split:
                    split_lo(2 * h + 3, m_hi, m_lo)
                if before is not None:
                    add_out(before)
                turn_lo(1)

            def last_outputs():
                for m in range(KT):
                    y_unit(m)
                add_out(NC - 1)

            split_lo(1, m_hi, m_lo)
            pipeline(dve, chunk, last_outputs, lambda h: split_lo(2 * h + 2, g_hi, g_lo),
                     ((pp, 10), (tp, 6), (sub, 2), (hi, 8), (link, 10)))

        @block.tensor
        def _(pe):
            pp, tp, sub = Tick(), Tick(), Tick()

            def unit():
                v = pp.step()
                pe.wait_ge(pp_free, v)
                return bank(pp.n - 1)

            def t_units(c):
                for m in range(KT):
                    out = unit()
                    for k in range(KT):
                        last = three_pass(nc, out[:, 0:CH], [x[:, k, m * 128:(m + 1) * 128] for x in (m_hi, m_lo)],
                                          [x[:, k, bass.ds(CH * c, CH)] for x in (g.xt_hi, g.xt_lo)],
                                          k == 0, k == KT - 1)
                    last.then_inc(pp_done, 1)

            def scores(s, t_end):
                if s == 0:
                    pe.wait_ge(pp_free, t_end + 2)
                pe.wait_ge(s_free, sub.step())
                for a, b in SPANS:
                    for k in range(KT):
                        last = three_pass(nc, score[:, a:b], [x[:, k, s * P:(s + 1) * P] for x in (t_hi, t_lo)],
                                          [x[:, k, a:b] for x in (g.xt_hi, g.xt_lo)], k == 0, k == KT - 1)
                last.then_inc(s_done, 1)

            def turn(s):
                v = tp.step()
                pe.wait_ge(p_ready, v)
                pe.wait_ge(tp_free, 3 * v)
                for q, (j0, j1) in enumerate(PIECES):
                    for j in range(j0, j1):
                        last = nc.tensor.transpose(piece(q)[:, j - j0, :], prob[:, s, j * P:(j + 1) * P],
                                                   g.ident[0:P, 0:P])
                    last.then_inc(tp_done, 1)

            def y_unit(m):
                if m == 0:
                    pe.wait_ge(tp_free, 3 * (tp.base + tp.n) + 3)
                out = unit()
                for j in range(NT):
                    last = three_pass(nc, out[:, 0:CH], [x[:, j, m * 128:(m + 1) * 128] for x in (g.xn_hi, g.xn_lo)],
                                      [x[:, j, :] for x in (pt_hi, pt_lo)], j == 0, j == NT - 1)
                last.then_inc(pp_done, 1)

            def out_units():
                pe.wait_ge(pp_free, pp.base + pp.n + 2)
                for s in range(2):
                    out = unit()
                    for k in range(KT):
                        last = three_pass(nc, out[0:P, :], [x[:, k, s * P:(s + 1) * P] for x in (yt_hi, yt_lo)],
                                          [x[:, k, :] for x in (g_hi, g_lo)], k == 0, k == KT - 1)
                    last.then_inc(pp_done, 1)

            def chunk(h, c, before, split):
                def y(m):
                    if before is not None:
                        y_unit(m)

                if isinstance(c, int) and c == 0:
                    pe.wait_ge(raw_free, 2 * h + 1)
                t_units(c)
                t_end = pp.base + pp.n
                y(0)
                scores(0, t_end)
                y(1), y(2)
                scores(1, t_end)
                y(3)
                turn(0)
                if before is not None:
                    pe.wait_ge(raw_free, 2 * h + (0 if isinstance(c, int) and c == 0 else 2))
                    out_units()
                turn(1)

            def last_outputs():
                for m in range(KT):
                    y_unit(m)
                out_units()

            pipeline(pe, chunk, last_outputs, lambda h: None, ((pp, 10), (tp, 2), (sub, 2)))


def row_view(ap, rows=P):
    return ap.rearrange("(a n) -> a n", a=1).broadcast_to([rows, ap.shape[0]])


def tiles(ap):
    return ap.rearrange("(t p) d -> p t d", p=P)


def graph_output(core, g, w, ln):
    nc, at, sem = core.nc, core.at, core.sem
    ones = at("ones_f", [128, P], F32, 170)
    diag = at("diag", [128, 2 * KT, 128], F32, 4)
    rows = at("bias_rows", [P, 2, D], F32, 160)
    gamma, beta, blin = (at(n, [P, D], F32, 164 + 2 * i) for i, n in enumerate(("gamma", "beta", "blin")))
    x = g.x
    loaded, x_in, gs_in = sem("go_rows_loaded"), sem("go_x_loaded"), sem("go_gs_in")
    gs_hi, gs_lo, diag_ready = sem("go_gs_hi"), sem("go_gs_lo"), sem("go_diag")
    row_done, row_free, done, free = sem("go_row_done"), sem("go_row_free"), sem("go_done"), sem("go_free")
    xb = sem("go_x_beta")
    ln.turn += 1
    turn = ln.turn
    with nc.Block() as block:
        @block.sync
        def _(sp):
            for dst, src in ((blin, w["blin"]), (gamma, w["gamma"]), (beta, w["beta"])):
                sp.dma_start(dst[:], row_view(src)).then_inc(loaded, 16)
            sp.dma_start(g.gs_acc[:], g.gs_store).then_inc(gs_in, 16)
            sp.dma_start(x[:], tiles(w["x"])).then_inc(x_in, 16)

        @block.gpsimd
        def _(pool):
            pool.wait_ge(loaded, 48)
            pool.wait_ge(x_in, 16)
            for t in range(NT):
                last = nc.gpsimd.tensor_tensor(x[:, t, :], x[:, t, :], beta[:], ALU.add)
            last.then_inc(xb, 1)

        @block.scalar
        def _(act):
            act.wait_ge(gs_in, 16)
            nc.scalar.activation(g.g_hi[:], g.gs_acc[:], ACT.Copy).then_inc(gs_hi, 1)
            ln.root(nc, act)

        @block.vector
        def _(dve):
            link = core.link.on(dve)
            nc.vector.memset(ones[:], 1.0)
            for i in range(2):
                for k in range(KT):
                    last = nc.vector.tensor_scalar(diag[:, i * KT + k, :], g.ident[:], g.gcol[:, k, i:i + 1], None,
                                                   ALU.mult)
            last.then_inc(diag_ready, 1)
            dve.wait_ge(gs_hi, 1)
            nc.vector.tensor_tensor(g.g_lo[:], g.gs_acc[:], f32(g.g_hi[:]), ALU.subtract).then_inc(gs_lo, 1)
            dve.wait_ge(row_done, 2)
            link(nc.vector.tensor_copy(rows[:, 0, :], core.bank(6)[0:P, :]))
            dve.wait_ge(loaded, 48)
            link(nc.vector.tensor_tensor(rows[:, 1, :], blin[:], core.bank(7)[0:P, :], ALU.add))
            for t in range(NT):
                last = nc.vector.scalar_tensor_tensor(g.acc[:, t, :], rows[:, 0, :], g.has_edge[:, t:t + 1],
                                                      g.acc[:, t, :], ALU.mult, ALU.add)
            link(last)
            link(nc.vector.tensor_tensor(g.acc[:], g.acc[:], rows[:, 1:2, :].broadcast_to([P, NT, D]), ALU.add))
            for t in range(NT):
                dve.wait_ge(done, t + 1)
                nc.vector.tensor_tensor(g.acc[:, t, :], g.acc[:, t, :], core.bank(t % 6)[0:P, :],
                                        ALU.add).then_inc(free, 1)
            dve.wait_ge(free, NT)
            layer_stats(nc, link, g.acc, ln, turn)
            for t in range(NT):
                nc.vector.scalar_tensor_tensor(g.acc[:, t, :], g.acc[:, t, :], ln.mv[:, t, 0:1], gamma[:],
                                               ALU.subtract, ALU.mult)
            link(nc.vector.memset(ln.r2[:], 0.0))
            dve.wait_ge(xb, 1)
            for t in range(NT):
                nc.vector.scalar_tensor_tensor(x[:, t, :], g.acc[:, t, :], ln.r[:, t:t + 1], x[:, t, :],
                                               ALU.mult, ALU.add)

        @block.tensor
        def _(pe):
            pe.wait_ge(diag_ready, 1)
            for i in range(2):
                for k in range(KT):
                    last = nc.tensor.matmul(core.bank(6 + i)[0:P, k * 128:(k + 1) * 128], ones[:],
                                            diag[:, i * KT + k, :], start=True, stop=True)
                last.then_inc(row_done, 1)
            pe.wait_ge(gs_lo, 1)
            for t in range(NT):
                if t >= 6:
                    pe.wait_ge(free, t - 5)
                for k in range(KT):
                    last = three_pass(nc, core.bank(t % 6)[0:P, :],
                                      [a[:, k, t * P:(t + 1) * P] for a in (g.xt_hi, g.xt_lo)],
                                      [a[:, k, :] for a in (g.g_hi, g.g_lo)], k == 0, k == KT - 1)
                last.then_inc(done, 1)


def expert_lora(core, g, w, ln):
    nc, at, sem = core.nc, core.at, core.sem
    NE, R = 4, 16
    x, xs = g.x, g.xs
    fc1_hi, fc1_lo = at("fc1_hi", [128, NE, KT, D], F32R, 92), at("fc1_lo", [128, NE, KT, D], F32R, 124)
    a_hi, a_lo = at("lora_a_hi", [128, NE, KT, 128], F32R, 156), at("lora_a_lo", [128, NE, KT, 128], F32R, 164)
    raw = [at(f"ffn_raw{i}", [128, KT, D], F32, 172 + 8 * i) for i in range(2)]
    wt, wrep = at("weights_t", [NE * R, N], F32, 172), at("weights_rep", [P, NT, NE, R], F32, 177)
    a_raw, b_raw = at("lora_a_raw", [128, NE, KT, R], F32, 188), at("lora_b_raw", [128, NE, KT, R], F32, 189)
    h_hi = [at(f"hid_hi{i}", [128, KT, CH], F32R, 188 + 8 * i) for i in range(2)]
    h_lo = [at(f"hid_lo{i}", [128, KT, CH], F32R, 192 + 8 * i) for i in range(2)]
    b_pad = at("lora_b_pad", [128, NE, KT, NE * R], F32, 4)
    f_sb = at("lora_f", [NE * R, D], F32, 204)
    lw = at("lora_weighted", [NE * R, CH], F32, 206)
    S = g.small
    gw = at("gate_cols", [128, KT, 6], F32, S)
    gw_hi, gw_lo = at("gate_hi", [128, KT, 6], F32R, S + .125), at("gate_lo", [128, KT, 6], F32R, S + .25)
    lg = at("gate_logits", [P, NT, 6], F32, S + .375)
    ex, wgt = at("gate_exp", [P, NT, 6], F32, S + .625), at("gate_weight", [P, NT, NE], F32, S + .875)
    m1, m2 = at("gate_m1", [P, NT, 1], F32, S + 1.0625), at("gate_m2", [P, NT, 1], F32, S + 1.125)

    small_in, raw_in = sem("ffn_small_in"), [sem("ffn_raw_in0"), sem("ffn_raw_in1")]
    raw_free = [sem("ffn_raw_free0"), sem("ffn_raw_free1")]
    xs_ready, hi_done = sem("ffn_xs"), sem("ffn_hi_done")
    small_hi, pads, small_lo = sem("ffn_small_hi"), sem("ffn_pads"), sem("ffn_small_lo")
    gl_done, gl_ready, ex_ready, wrep_ready, wt_done = (
        sem(f"ffn_{n}") for n in ("gl_done", "gl_ready", "ex_ready", "wrep", "wt_done"))
    start = sem("ffn_prepared")
    u_done, u_hi, u_free = sem("hid_done"), sem("hid_hi_done"), sem("hid_free")
    lora_done, lw_ready, out_done, x_added = sem("lora_done"), sem("lw_ready"), sem("ffn_out_done"), sem("ffn_x_added")
    turned = g.turned.again()
    ln.turn += 1
    turn = ln.turn
    bank = lambda u: core.bank(6 + u % 2)
    UNITS = NE * KT

    with nc.Block() as block:
        @block.sync
        def _(sp):
            sp.dma_start(gw[:], w["gates"]).then_inc(small_in, 16)
            sp.dma_start(a_raw[:], w["lora_A"]).then_inc(small_in, 16)
            sp.dma_start(b_raw[:], w["lora_B"]).then_inc(small_in, 16)
            for i in range(2 * NE):
                if i >= 2:
                    sp.wait_ge(raw_free[i % 2], i // 2)
                src = (w["fc1T"], w["fc2T"])[i // NE][i % NE].rearrange("(k p) n -> p k n", p=128)
                sp.dma_start(raw[i % 2][:], src).then_inc(raw_in[i % 2], 16)

        @block.scalar
        def _(act):
            ln.root(nc, act)
            act.wait_ge(small_in, 48)
            act.wait_ge(pads, 1)
            nc.scalar.activation(gw_hi[:], gw[:], ACT.Copy)
            for e in range(NE):
                last = nc.scalar.activation(a_hi[:, e, :, R * e:R * e + R], a_raw[:, e, :, :], ACT.Copy)
            last.then_inc(small_hi, 1)
            for e in range(NE):
                act.wait_ge(raw_in[e % 2], 16 * (e // 2 + 1))
                nc.scalar.activation(fc1_hi[:, e, :, :], raw[e % 2][:], ACT.Copy).then_inc(hi_done, 1)
            turned.scalar(core, act, g.xt_hi)
            act.wait_ge(gl_ready, 1)
            nc.scalar.activation(ex[:, :, 0:4], lg[:, :, 0:4], ACT.Exp)
            nc.scalar.activation(ex[:, :, 4:5], lg[:, :, 4:5], ACT.Exp, scale=-1.0).then_inc(ex_ready, 1)
            pp = Tick()
            act.wait_ge(start, 1)
            with act.Fori(0, NC) as c:
                pp.enter(c, UNITS)
                for e in range(NE):
                    act.wait_ge(lora_done, NE * c + e + 1)
                    for m in range(KT):
                        act.wait_ge(u_done, pp.step())
                        nc.scalar.activation(h_hi[e % 2][:, m, :], bank(m)[:, 0:CH], ACT.Relu).then_inc(u_hi, 1)
                pp.leave(NC)

        @block.vector
        def _(dve):
            link = core.link.on(dve)
            nc.vector.memset(f32(a_hi[:]), 0.0)
            nc.vector.memset(f32(a_lo[:]), 0.0)
            nc.vector.memset(b_pad[:], 0.0).then_inc(pads, 1)
            normalise(nc, link, x, xs, ln, turn)
            dve.sem_inc(xs_ready, 1)
            dve.wait_ge(small_hi, 1)
            nc.vector.tensor_tensor(gw_lo[:], gw[:], f32(gw_hi[:]), ALU.subtract)
            for e in range(NE):
                cols = slice(R * e, R * e + R)
                nc.vector.tensor_tensor(a_lo[:, e, :, cols], a_raw[:, e, :, :], f32(a_hi[:, e, :, cols]), ALU.subtract)
            for e in range(NE):
                last = nc.vector.tensor_copy(b_pad[:, e, :, R * e:R * e + R], b_raw[:, e, :, :])
            last.then_inc(small_lo, 1)
            for e in range(NE):
                dve.wait_ge(hi_done, e + 1)
                nc.vector.tensor_tensor(fc1_lo[:, e, :, :], raw[e % 2][:], f32(fc1_hi[:, e, :, :]),
                                        ALU.subtract).then_inc(raw_free[e % 2], 1)
            turned.vector(core, dve, g.xt_hi, g.xt_lo)
            dve.wait_ge(raw_free[1], 4)
            link(nc.vector.tensor_copy(f_sb[:], core.bank(1)[0:NE * R, :]))
            dve.wait_ge(gl_done, 1)
            gl = core.bank(0)[0:P, 0:NT * 8].rearrange("p (t e) -> p t e", e=8)
            link(nc.vector.tensor_copy(lg[:], gl[:, :, 0:6]))
            link(nc.vector.tensor_reduce(m1[:], lg[:, :, 0:4], AX.X, ALU.max))
            nc.vector.tensor_tensor(lg[:, :, 0:4], lg[:, :, 0:4], m1[:].broadcast_to([P, NT, 4]),
                                    ALU.subtract).then_inc(gl_ready, 1)
            dve.wait_ge(ex_ready, 1)
            link(nc.vector.tensor_reduce(m1[:], ex[:, :, 0:4], AX.X, ALU.add))
            link(nc.vector.reciprocal(m1[:], m1[:]))
            link(nc.vector.tensor_tensor(wgt[:], ex[:, :, 0:4], m1[:].broadcast_to([P, NT, 4]), ALU.mult))
            link(nc.vector.tensor_scalar(m2[:], ex[:, :, 4:5], 1.0, None, ALU.add))
            link(nc.vector.reciprocal(m2[:], m2[:]))
            link(nc.vector.tensor_scalar(m2[:], m2[:], 0.25, None, ALU.mult))
            link(nc.vector.tensor_tensor(wgt[:], wgt[:], m2[:].broadcast_to([P, NT, 4]), ALU.subtract))
            link(nc.vector.tensor_scalar(wgt[:], wgt[:], 0.0, None, ALU.max))
            link(nc.vector.tensor_reduce(m1[:], wgt[:], AX.X, ALU.add))
            link(nc.vector.tensor_scalar(m2[:], m1[:], 0.0, None, ALU.is_equal))
            link(nc.vector.tensor_tensor(m1[:], m1[:], m2[:], ALU.add))
            link(nc.vector.reciprocal(m1[:], m1[:]))
            link(nc.vector.tensor_tensor(wgt[:], wgt[:], m1[:].broadcast_to([P, NT, 4]), ALU.mult))
            nc.vector.tensor_copy(wrep[:], wgt[:].unsqueeze(3).broadcast_to([P, NT, NE, R])).then_inc(wrep_ready, 1)
            for q in range(3):
                n = min(4, NT - 4 * q) * P
                dve.wait_ge(wt_done, q + 1)
                last = nc.vector.tensor_copy(wt[:, 4 * q * P:4 * q * P + n], core.bank(2 + q)[0:NE * R, 0:n])
            last.then_inc(start, 1)
            pp = Tick()
            with dve.Fori(0, NC) as c:
                pp.enter(c, UNITS)
                for e in range(NE):
                    for m in range(KT):
                        dve.wait_ge(u_hi, pp.step())
                        nc.vector.scalar_tensor_tensor(h_lo[e % 2][:, m, :], bank(m)[:, 0:CH], 0.0,
                                                       f32(h_hi[e % 2][:, m, :]), ALU.max,
                                                       ALU.subtract).then_inc(u_free, 1)
                dve.wait_ge(lora_done, NE * c + 6)
                nc.vector.tensor_tensor(lw[:], core.bank(5)[0:NE * R, 0:CH], wt[:, bass.ds(CH * c, CH)],
                                        ALU.mult).then_inc(lw_ready, 1)
                for s in range(2):
                    dve.wait_ge(out_done, 2 * c + s + 1)
                    dst = x[:, bass.ds(2 * c + s, 1), :].rearrange("p a n -> p (a n)")
                    nc.vector.tensor_tensor(dst, dst, core.bank(s)[0:P, :], ALU.add).then_inc(x_added, 1)
                pp.leave(NC)

        @block.tensor
        def _(pe):
            pe.wait_ge(xs_ready, 1)
            turned.tensor(core, pe, xs, g.ident)
            pe.wait_ge(turned.lo, turned.before + NT)
            pe.wait_ge(small_lo, 1)
            for t in range(NT):
                for k in range(KT):
                    last = three_pass(nc, core.bank(0)[0:P, 8 * t:8 * t + 6],
                                      [a[:, k, t * P:(t + 1) * P] for a in (g.xt_hi, g.xt_lo)],
                                      [a[:, k, :] for a in (gw_hi, gw_lo)], k == 0, k == KT - 1)
            last.then_inc(gl_done, 1)
            for e in range(NE):
                pe.wait_ge(raw_in[e % 2], 32 + 16 * (e // 2 + 1))
                for k in range(KT):
                    last = nc.tensor.matmul(core.bank(1)[0:NE * R, :], b_pad[:, e, k, :], raw[e % 2][:, k, :],
                                            start=e == k == 0, stop=e == NE - 1 and k == KT - 1)
                last.then_inc(raw_free[e % 2], 1)
            pe.wait_ge(wrep_ready, 1)
            for t in range(NT):
                q, r = divmod(t, 4)
                last = nc.tensor.transpose(core.bank(2 + q)[0:NE * R, r * P:(r + 1) * P],
                                           wrep[:, t, :, :].rearrange("p e r -> p (e r)"), g.ident[0:P, 0:P])
                if r == 3 or t == NT - 1:
                    last.then_inc(wt_done, 1)
            pe.wait_ge(start, 1)
            pp = Tick()

            def hidden(c, e):
                for m in range(KT):
                    pe.wait_ge(u_free, pp.step())
                    for k in range(KT):
                        last = three_pass(nc, bank(m)[:, 0:CH],
                                          [a[:, e, k, m * 128:(m + 1) * 128] for a in (fc1_hi, fc1_lo)],
                                          [a[:, k, bass.ds(CH * c, CH)] for a in (g.xt_hi, g.xt_lo)],
                                          k == 0, k == KT - 1)
                    last.then_inc(u_done, 1)

            def lora(c, e):
                pe.wait_ge(u_free, pp.base + KT * (e + 1) + 2)
                if e == 0:
                    pe.wait_ge(lw_ready, c + 1)
                for k in range(KT):
                    last = three_pass(nc, core.bank(5)[:, 0:CH], [a[:, e, k, :] for a in (a_hi, a_lo)],
                                      [a[:, k, :] for a in (h_hi[e % 2], h_lo[e % 2])],
                                      e == k == 0, e == NE - 1 and k == KT - 1)
                last.then_inc(lora_done, 1)

            with pe.Fori(0, NC) as c:
                pp.enter(c, UNITS)
                hidden(c, 0)
                for e in range(1, NE):
                    hidden(c, e)
                    lora(c, e - 1)
                lora(c, NE - 1)
                pe.wait_ge(lw_ready, c + 2)
                for s in range(2):
                    pe.wait_ge(x_added, 2 * c + s + 1)
                    nc.tensor.matmul(core.bank(s)[0:P, :], lw[:, s * P:(s + 1) * P], f_sb[:], start=True,
                                     stop=True).then_inc(out_done, 1)
                pp.leave(NC)


def edge_mean_gnn(core, g, w, ln):
    nc, at, sem = core.nc, core.at, core.sem
    HID = 1024
    MT = HID // 128
    x, xs = g.x, g.xs
    w1_hi, w1_lo = at("w1_hi", [128, KT, HID], F32R, 92), at("w1_lo", [128, KT, HID], F32R, 108)
    e1_hi, e1_lo = at("w1e_hi", [EDGE_D, HID], F32R, 124), at("w1e_lo", [EDGE_D, HID], F32R, 128)
    w2_hi, w2_lo = at("w2_hi", [128, MT, D], F32R, 132), at("w2_lo", [128, MT, D], F32R, 148)
    raw = [at(f"gnn_raw{i}", [128, KT, D], F32, 164 + 8 * i) for i in range(2)]
    at_hi, at_lo = at("agg_t_hi", [EDGE_D, N], F32R, 164), at("agg_t_lo", [EDGE_D, N], F32R, 169)
    h_hi, h_lo = at("gh_hi", [128, MT, CH], F32R, 180), at("gh_lo", [128, MT, CH], F32R, 188)
    r = at("gh_relu", [128, 2, CH], F32, 196)
    b2 = at("gnn_b2", [P, D], F32, 4)
    b1 = at("gnn_b1", [128, MT], F32, g.small)

    small_in, raw_in = sem("gnn_small_in"), [sem("gnn_raw_in0"), sem("gnn_raw_in1")]
    raw_free, hi_done = [sem("gnn_raw_free0"), sem("gnn_raw_free1")], sem("gnn_hi_done")
    xs_ready, xres = sem("gnn_xs"), sem("gnn_xres")
    ag_done, ag_hi, prep = sem("gnn_ag_done"), sem("gnn_ag_hi"), sem("gnn_prepared")
    u_done, u_bank, u_hi, u_lo = sem("gh_done"), sem("gh_bank_free"), sem("gh_hi_done"), sem("gh_lo_done")
    out_done, x_added, s_act = sem("gnn_out_done"), sem("gnn_x_added"), sem("gnn_relu_done")
    turned = g.turned.again()
    ln.turn += 1
    turn = ln.turn
    w1v = w["W1"][0:D, :].rearrange("(k p) n -> p k n", p=128)
    w2v = w["W2"].rearrange("(k p) n -> p k n", p=128)
    loads = [(w1v[:, :, 0:D], lambda b: b[:], (w1_hi[:, :, 0:D], w1_lo[:, :, 0:D])),
             (w1v[:, :, D:], lambda b: b[:], (w1_hi[:, :, D:], w1_lo[:, :, D:])),
             (w2v[:, 0:KT, :], lambda b: b[:], (w2_hi[:, 0:KT, :], w2_lo[:, 0:KT, :])),
             (w2v[:, KT:, :], lambda b: b[:], (w2_hi[:, KT:, :], w2_lo[:, KT:, :])),
             (w["W1"][D:, :], lambda b: b[0:EDGE_D, 0:2, :].rearrange("p a n -> p (a n)"), (e1_hi[:], e1_lo[:]))]
    agg_bank = lambda q: core.bank(q)[0:EDGE_D, 0:min(4, NT - 4 * q) * P]
    agg_cols = lambda q: slice(4 * q * P, 4 * q * P + min(4, NT - 4 * q) * P)

    with nc.Block() as block:
        @block.sync
        def _(sp):
            sp.dma_start(b1[:], w["b1"]).then_inc(small_in, 16)
            sp.dma_start(b2[:], row_view(w["b2"])).then_inc(small_in, 16)
            for i, (src, dst, _) in enumerate(loads):
                if i >= 2:
                    sp.wait_ge(raw_free[i % 2], i // 2)
                sp.dma_start(dst(raw[i % 2]), src).then_inc(raw_in[i % 2], 16)

        @block.gpsimd
        def _(pool):
            pool.wait_ge(xs_ready, 1)
            pool.wait_ge(small_in, 32)
            nc.gpsimd.tensor_tensor(x[:], x[:], xs[:], ALU.add).then_inc(xres, 1)
            pool.wait_ge(xres, 1)
            for t in range(NT):
                last = nc.gpsimd.tensor_tensor(x[:, t, :], x[:, t, :], b2[:], ALU.add)
            last.then_inc(xres, 1)

        @block.scalar
        def _(act):
            ln.root(nc, act)
            for i, (_, dst, (hi, _)) in enumerate(loads):
                act.wait_ge(raw_in[i % 2], 16 * (i // 2 + 1))
                nc.scalar.activation(hi, dst(raw[i % 2]), ACT.Copy).then_inc(hi_done, 1)
            turned.scalar(core, act, g.xt_hi)
            act.wait_ge(raw_free[0], 3)
            act.wait_ge(raw_free[1], 2)
            for q in range(3):
                act.wait_ge(ag_done, q + 1)
                nc.scalar.activation(at_hi[:, agg_cols(q)], agg_bank(q), ACT.Copy).then_inc(ag_hi, 1)
            pp = Tick()
            act.wait_ge(small_in, 32)
            with act.Fori(0, NC) as c:
                pp.enter(c, MT)
                for m in range(MT):
                    v = pp.step()
                    act.wait_ge(u_done, v)
                    act.wait_ge(u_lo, v)
                    nc.scalar.activation(r[:, m % 2, :], core.bank(6 + m % 2)[:, 0:CH], ACT.Relu,
                                         bias=b1[:, m:m + 1]).then_inc(u_bank, 1)
                    act.wait_ge(u_bank, v + 2)
                    nc.scalar.activation(h_hi[:, m, :], r[:, m % 2, :], ACT.Copy).then_inc(u_hi, 1)
                pp.leave(NC)

        @block.vector
        def _(dve):
            link = core.link.on(dve)
            normalise(nc, link, x, xs, ln, turn)
            dve.sem_inc(xs_ready, 1)
            for i, (_, dst, (hi, lo)) in enumerate(loads):
                dve.wait_ge(hi_done, i + 1)
                nc.vector.tensor_tensor(lo, dst(raw[i % 2]), f32(hi), ALU.subtract).then_inc(raw_free[i % 2], 1)
            turned.vector(core, dve, g.xt_hi, g.xt_lo)
            for q in range(3):
                dve.wait_ge(ag_hi, q + 1)
                last = nc.vector.tensor_tensor(at_lo[:, agg_cols(q)], agg_bank(q), f32(at_hi[:, agg_cols(q)]),
                                               ALU.subtract)
            last.then_inc(prep, 1)
            dve.wait_ge(xres, 2)
            pp = Tick()
            with dve.Fori(0, NC) as c:
                pp.enter(c, MT)
                for m in range(MT):
                    dve.wait_ge(u_hi, pp.step())
                    nc.vector.tensor_tensor(h_lo[:, m, :], r[:, m % 2, :], f32(h_hi[:, m, :]),
                                            ALU.subtract).then_inc(u_lo, 1)
                for s in range(2):
                    dve.wait_ge(out_done, 2 * c + s + 1)
                    dst = x[:, bass.ds(2 * c + s, 1), :].rearrange("p a n -> p (a n)")
                    nc.vector.tensor_tensor(dst, dst, core.bank(s)[0:P, :], ALU.add).then_inc(x_added, 1)
                pp.leave(NC)

        @block.tensor
        def _(pe):
            pe.wait_ge(xs_ready, 1)
            turned.tensor(core, pe, xs, g.ident)
            pe.wait_ge(turned.lo, turned.before + NT)
            for t in range(NT):
                q, j = divmod(t, 4)
                last = nc.tensor.transpose(core.bank(q)[0:EDGE_D, j * P:(j + 1) * P], g.agg[:, t, :], g.ident[0:P, 0:P])
                if j == 3 or t == NT - 1:
                    last.then_inc(ag_done, 1)
            pe.wait_ge(prep, 1)
            pp = Tick()
            with pe.Fori(0, NC) as c:
                pp.enter(c, MT)
                for m in range(MT):
                    out = core.bank(6 + m % 2)[:, 0:CH]
                    cols = slice(m * 128, (m + 1) * 128)
                    pe.wait_ge(u_bank, pp.step())
                    for k in range(KT):
                        three_pass(nc, out, [a[:, k, cols] for a in (w1_hi, w1_lo)],
                                   [a[:, k, bass.ds(CH * c, CH)] for a in (g.xt_hi, g.xt_lo)], k == 0, False)
                    three_pass(nc, out, [a[:, cols] for a in (e1_hi, e1_lo)],
                               [a[:, bass.ds(CH * c, CH)] for a in (at_hi, at_lo)], False, True).then_inc(u_done, 1)
                pe.wait_ge(u_lo, pp.base + pp.n + 2)
                for s in range(2):
                    pe.wait_ge(x_added, 2 * c + s + 1)
                    for k in range(MT):
                        last = three_pass(nc, core.bank(s)[0:P, :], [a[:, k, s * P:(s + 1) * P] for a in (h_hi, h_lo)],
                                          [a[:, k, :] for a in (w2_hi, w2_lo)], k == 0, k == MT - 1)
                    last.then_inc(out_done, 1)
                pp.leave(NC)


def keys_values(core, g, w, ln):
    nc, at, sem = core.nc, core.at, core.sem
    x, xs = g.x, g.xs
    g.k_hi, g.k_lo = at("k_hi", [128, KT, N], F32R, 92), at("k_lo", [128, KT, N], F32R, 112)
    g.v_hi, g.v_lo = at("v_hi", [P, NT, D], F32R, 132), at("v_lo", [P, NT, D], F32R, 152)
    q_hi, q_lo = at("q_hi", [128, KT, N], F32R, 132), at("q_lo", [128, KT, N], F32R, 152)
    w_hi, w_lo = at("kv_w_hi", [128, KT, D], F32R, 172), at("kv_w_lo", [128, KT, D], F32R, 180)
    raw = at("kv_raw", [128, KT, D], F32, 188)
    vsum = at("v_sum", [P, 2, D], F32, 196)
    bv = at("mha_bv", [P, D], F32, 4)
    bqk = at("mha_bqk", [128, 2, KT], F32, g.small)
    small_in, raw_in, hi_done, lo_done = sem("kv_small_in"), sem("kv_raw_in"), sem("kv_hi_done"), sem("kv_lo_done")
    xs_ready, stash = sem("kv_xs"), sem("kv_stashed")
    x_ready = sem("kv_x")
    done, hi, lo, vs = sem("kv_done"), sem("kv_out_hi"), sem("kv_out_lo"), sem("kv_vsum")
    turned = g.turned.again()
    ln.turn += 1
    turn = ln.turn
    kq_units = [(m, a, b) for m in range(KT) for a, b in SPANS]
    first_k, first_v = len(kq_units), 2 * len(kq_units)
    total = first_v + NT
    q_stored = sem("kv_q_stored")

    def features(u):
        halves, j = ((q_hi, q_lo), 0) if u < first_k else ((g.k_hi, g.k_lo), 1)
        m, a, b = kq_units[u % first_k]
        return *halves, j, m, a, b

    with nc.Block() as block:
        @block.sync
        def _(sp):
            sp.dma_start(bqk[:, 0, :], w["bq2"]).then_inc(small_in, 16)
            sp.dma_start(bqk[:, 1, :], w["bk2"]).then_inc(small_in, 16)
            sp.dma_start(bv[:], row_view(w["bv2"])).then_inc(small_in, 16)
            for i, src in enumerate((w["Wq2"], w["Wk2"], w["Wv2"])):
                if i:
                    sp.wait_ge(lo_done, i)
                sp.dma_start(raw[:], src.rearrange("(k p) n -> p k n", p=128)).then_inc(raw_in, 16)
            sp.dma_start(tiles(g.x3_store), x[:]).then_inc(stash, 16)
            sp.wait_ge(xs_ready, 1)
            sp.dma_start(tiles(g.xs_store), xs[:]).then_inc(stash, 16)
            sp.wait_ge(lo, first_k)
            for dst, src in zip(g.q_store, (q_hi, q_lo)):
                sp.dma_start(dst, f32(src[:])).then_inc(q_stored, 16)
            sp.wait_ge(stash, 32)

        @block.scalar
        def _(act):
            ln.root(nc, act)
            act.wait_ge(raw_in, 16)
            nc.scalar.activation(w_hi[:], raw[:], ACT.Copy).then_inc(hi_done, 1)
            turned.scalar(core, act, g.xt_hi)
            act.wait_ge(small_in, 48)
            for u in range(total):
                if u in (first_k, first_v):
                    act.wait_ge(raw_in, 32 if u == first_k else 48)
                    act.wait_ge(done, u)
                    nc.scalar.activation(w_hi[:], raw[:], ACT.Copy).then_inc(hi_done, 1)
                if u == first_v:
                    act.wait_ge(q_stored, 32)
                if u >= first_v:
                    t = u - first_v
                    act.wait_ge(vs, t + 1)
                    nc.scalar.activation(g.v_hi[:, t, :], vsum[:, t % 2, :], ACT.Copy).then_inc(hi, 1)
                    continue
                dst, _, j, m, a, b = features(u)
                act.wait_ge(done, u + 1)
                nc.scalar.activation(dst[:, m, a:b], core.bank(u % 8)[:, 0:b - a], ACT.Identity,
                                     bias=bqk[:, j, m:m + 1]).then_inc(hi, 1)

        @block.vector
        def _(dve):
            link = core.link.on(dve)
            normalise(nc, link, x, xs, ln, turn)
            dve.sem_inc(xs_ready, 1)

            def split(n):
                dve.wait_ge(hi_done, n)
                nc.vector.tensor_tensor(w_lo[:], raw[:], f32(w_hi[:]), ALU.subtract).then_inc(lo_done, 1)

            split(1)
            turned.vector(core, dve, g.xt_hi, g.xt_lo)
            dve.wait_ge(small_in, 48)
            for u in range(total):
                if u in (first_k, first_v):
                    split(2 if u == first_k else 3)
                if u >= first_v:
                    t = u - first_v
                    dve.wait_ge(done, u + 1)
                    nc.vector.tensor_tensor(vsum[:, t % 2, :], core.bank(u % 8)[0:P, :], bv[:], ALU.add).then_inc(vs, 1)
                    dve.wait_ge(hi, u + 1)
                    nc.vector.tensor_tensor(g.v_lo[:, t, :], vsum[:, t % 2, :], f32(g.v_hi[:, t, :]),
                                            ALU.subtract).then_inc(lo, 1)
                    continue
                dh, dl, j, m, a, b = features(u)
                dve.wait_ge(hi, u + 1)
                nc.vector.scalar_tensor_tensor(dl[:, m, a:b], core.bank(u % 8)[:, 0:b - a], bqk[:, j, m:m + 1],
                                               f32(dh[:, m, a:b]), ALU.add, ALU.subtract).then_inc(lo, 1)

        @block.tensor
        def _(pe):
            pe.wait_ge(xs_ready, 1)
            turned.tensor(core, pe, xs, g.ident)
            pe.wait_ge(turned.lo, turned.before + NT)
            for u in range(total):
                if u in (0, first_k, first_v):
                    pe.wait_ge(lo_done, 1 + (u >= first_k) + (u >= first_v))
                if u >= 8:
                    pe.wait_ge(lo, u - 7)
                for k in range(KT):
                    if u >= first_v:
                        t = u - first_v
                        last = three_pass(nc, core.bank(u % 8)[0:P, :],
                                          [a[:, k, t * P:(t + 1) * P] for a in (g.xt_hi, g.xt_lo)],
                                          [a[:, k, :] for a in (w_hi, w_lo)], k == 0, k == KT - 1)
                    else:
                        m, lo_, hi_ = features(u)[-3:]
                        last = three_pass(nc, core.bank(u % 8)[:, 0:hi_ - lo_],
                                          [a[:, k, m * 128:(m + 1) * 128] for a in (w_hi, w_lo)],
                                          [a[:, k, lo_:hi_] for a in (g.xt_hi, g.xt_lo)], k == 0, k == KT - 1)
                last.then_inc(done, 1)


def self_attention(core, g, w):
    nc, at, sem = core.nc, core.at, core.sem
    NH, DH = 8, 64
    scale = DH ** -0.5
    qs_hi, qs_lo = at("qs_hi", [128, KT, CH], F32R, 52), at("qs_lo", [128, KT, CH], F32R, 56)
    ctx_hi, ctx_lo = at("ctx_hi", [128, KT, CH], F32R, 60), at("ctx_lo", [128, KT, CH], F32R, 64)
    wo_hi, wo_lo = at("wo_hi", [128, KT, D], F32R, 68), at("wo_lo", [128, KT, D], F32R, 76)
    raw = at("wo_raw", [128, KT, D], F32, 84)
    pt = [(at("ptm_hi0", [P, NT, CH], F32R, 172), at("ptm_lo0", [P, NT, CH], F32R, 182)),
          (at("ptm_hi1", [P, NT, CH], F32R, 12), at("ptm_lo1", [P, NT, CH], F32R, 22))]
    prob = at("mprob", [P, 4, N], F32, 32)
    xin = at("mha_xin", [P, 2, D], F32, 4)
    bo = at("mha_bo", [P, D], F32, 8)
    S = g.small
    mx, dens = at("mmax", [P, 2, 4], F32, S), at("mden", [P, 2, 4], F32, S + .0625)
    nmx, den, rden = (at(n, [P, 4], F32, S + .125 + i / 16) for i, n in enumerate(("nmx", "mdsum", "mrden")))

    small_in, raw_in, wo_h, wo_ready = sem("at_small_in"), sem("at_raw_in"), sem("at_wo_hi"), sem("at_wo_ready")
    q_in = sem("at_q_in")
    s_done, m_ready, e_ready = sem("at_s_done"), sem("at_m_ready"), sem("at_e_ready")
    r_ready, p_ready = sem("at_r_ready"), sem("at_p_ready")
    tp_done, tp_hi, tp_free = sem("at_tp_done"), sem("at_tp_hi"), sem("at_tp_free")
    c_done, c_hi, c_free = sem("at_c_done"), sem("at_c_hi"), sem("at_c_free")
    o_done, xin_in, summed, stored = sem("at_o_done"), sem("at_xin_in"), sem("at_summed"), sem("at_stored")
    SUBS = 2 * NH
    score = core.psum[0:P, 0:3, :].rearrange("p b n -> p (b n)")
    ctx_bank = core.bank(6)
    PIECES = [(0, 4), (4, 8), (8, 10)]
    OUT = 5

    def piece(q):
        j0, j1 = PIECES[q]
        return core.bank(3 + q)[0:P, 0:(j1 - j0) * P].rearrange("p (j n) -> p j n", n=P)

    def place(n):
        hh, s = n // 2, n % 2
        return slice(DH * (hh % 2), DH * (hh % 2) + DH), hh // 2, slice(s * P, (s + 1) * P)

    def chunks(eng, chunk, counts):
        chunk(0, range(SUBS), lambda j: j >= 0)
        with eng.Fori(1, NC) as c:
            for tick, per in counts:
                tick.enter(c - 1, per)
            chunk(c, range(SUBS), lambda j: True)
            for tick, per in counts:
                tick.leave(NC - 1)
        chunk(NC, range(OUT + 2), lambda j: j < 0)

    def pt_part(n, half, j0, j1):
        return pt[n // 2 % 2][half][:, j0:j1, n % 2 * P:(n % 2 + 1) * P]

    with nc.Block() as block:
        @block.sync
        def _(sp):
            sp.dma_start(raw[:], w["Wo"].rearrange("(k p) n -> p k n", p=128)).then_inc(raw_in, 16)
            sp.dma_start(bo[:], row_view(w["bo"])).then_inc(small_in, 16)

            def load_q(c):
                sp.dma_start(f32(qs_hi[:]), g.q_store[0][:, :, bass.ds(CH * c, CH)]).then_inc(q_in, 16)
                sp.dma_start(f32(qs_lo[:]), g.q_store[1][:, :, bass.ds(CH * c, CH)]).then_inc(q_in, 16)

            def residual_in(c):
                sp.wait_ge(stored, 16 * c + 16)
                sp.dma_start(xin[:], tiles(g.xs_store)[:, bass.ds(2 * c, 2), :]).then_inc(xin_in, 16)

            def rows_out(c):
                sp.wait_ge(summed, 2 * c + 3)
                sp.dma_start(tiles(g.pre_store)[:, bass.ds(2 * c, 2), :], xin[:]).then_inc(stored, 16)

            load_q(0)
            residual_in(0)
            with sp.Fori(0, NC - 1) as c:
                sp.wait_ge(s_done, 3 * SUBS * (c + 1))
                load_q(c + 1)
                rows_out(c)
                residual_in(c + 1)
            rows_out(NC - 1)
            sp.wait_ge(stored, 16 * NC + 16)

        @block.gpsimd
        def _(pool):
            sub = Tick()
            with pool.Fori(0, NC) as c:
                sub.enter(c, SUBS)
                for n in range(SUBS):
                    pool.wait_ge(r_ready, sub.step())
                    nc.gpsimd.tensor_tensor(prob[:, n % 4, :], prob[:, n % 4, :], rden[:, n % 4:n % 4 + 1].broadcast_to([P, N]),
                                            ALU.mult).then_inc(p_ready, 1)
                sub.leave(NC)

        @block.scalar
        def _(act):
            act.wait_ge(raw_in, 16)
            nc.scalar.activation(wo_hi[:], raw[:], ACT.Copy).then_inc(wo_h, 1)
            sub, tp, ctx = Tick(), Tick(), Tick()

            def exponentials(n):
                s = n % 2
                act.wait_ge(m_ready, sub.step())
                for q, (a, b) in enumerate(SPANS):
                    nc.scalar.activation(prob[:, n % 4, a:b], score[:, a:b], ACT.Exp, bias=nmx[:, s:s + 1],
                                         scale=scale, accum_out=dens[:, s, q:q + 1]).then_inc(e_ready, 1)

            def turned_hi(n):
                for q, (j0, j1) in enumerate(PIECES):
                    act.wait_ge(tp_done, tp.step())
                    nc.scalar.activation(pt_part(n, 0, j0, j1), piece(q), ACT.Copy).then_inc(tp_hi, 1)

            def context_hi(hh):
                rows, k, _ = place(2 * hh)
                act.wait_ge(c_done, ctx.step())
                nc.scalar.activation(ctx_hi[rows, k, :], ctx_bank[rows, 0:CH], ACT.Copy).then_inc(c_hi, 1)

            def chunk(c, steps, live):
                for n in steps:
                    if live(n):
                        exponentials(n)
                    if n % 2 == 0 and live(n - 6):
                        context_hi((n - 6) % SUBS // 2)
                    if live(n - 2):
                        turned_hi((n - 2) % SUBS)

            chunks(act, chunk, ((sub, SUBS), (tp, 3 * SUBS), (ctx, NH)))

        @block.vector
        def _(dve):
            link = core.link.on(dve)
            dve.wait_ge(wo_h, 1)
            nc.vector.tensor_tensor(wo_lo[:], raw[:], f32(wo_hi[:]), ALU.subtract).then_inc(wo_ready, 1)
            dve.wait_ge(small_in, 16)
            spans, tp, ctx, exps = Tick(), Tick(), Tick(), Tick()

            def inverse(n):
                s = n % 2
                dve.wait_ge(e_ready, 3 + exps.step(3))
                link(nc.vector.tensor_reduce(den[:, s:s + 1], dens[:, s, 0:3], AX.X, ALU.add))
                nc.vector.reciprocal(rden[:, n % 4:n % 4 + 1], den[:, s:s + 1]).then_inc(r_ready, 1)

            def maximum(n):
                s = n % 2
                for q, (a, b) in enumerate(SPANS):
                    dve.wait_ge(s_done, spans.step())
                    last = nc.vector.tensor_reduce(mx[:, s, q:q + 1], score[:, a:b], AX.X, ALU.max)
                link(last)
                link(nc.vector.tensor_reduce(nmx[:, s:s + 1], mx[:, s, 0:3], AX.X, ALU.max))
                nc.vector.tensor_scalar(nmx[:, s:s + 1], nmx[:, s:s + 1], -scale, None, ALU.mult).then_inc(m_ready, 1)

            def turned_lo(n):
                for q, (j0, j1) in enumerate(PIECES):
                    dve.wait_ge(tp_hi, tp.step())
                    nc.vector.tensor_tensor(pt_part(n, 1, j0, j1), piece(q), f32(pt_part(n, 0, j0, j1)),
                                            ALU.subtract).then_inc(tp_free, 1)

            def context_lo(hh):
                rows, k, _ = place(2 * hh)
                dve.wait_ge(c_hi, ctx.step())
                nc.vector.tensor_tensor(ctx_lo[rows, k, :], ctx_bank[rows, 0:CH], f32(ctx_hi[rows, k, :]),
                                        ALU.subtract).then_inc(c_free, 1)

            def chunk(c, steps, live):
                for n in steps:
                    if live(n - 1):
                        inverse((n - 1) % SUBS)
                    if n % 2 and live(n - 7):
                        context_lo((n - 7) % SUBS // 2)
                    if live(n):
                        maximum(n)
                    if live(n - 3):
                        turned_lo((n - 3) % SUBS)
                    if n == OUT - 2 and live(-1):
                        dve.wait_ge(xin_in, 16 * c)
                        for s in range(2):
                            link(nc.vector.tensor_tensor(xin[:, s, :], xin[:, s, :], bo[:], ALU.add))
                    if n in (OUT, OUT + 1) and live(-1):
                        s = n - OUT
                        dve.wait_ge(o_done, 2 * (c - 1) + s + 1)
                        nc.vector.tensor_tensor(xin[:, s, :], xin[:, s, :], core.bank(7)[0:P, :],
                                                ALU.add).then_inc(summed, 1)

            chunks(dve, chunk, ((spans, 3 * SUBS), (exps, 3 * SUBS), (tp, 3 * SUBS), (ctx, NH), (link, 3 * SUBS + 2)))

        @block.tensor
        def _(pe):
            pe.wait_ge(wo_ready, 1)
            spans, sub, tp, ctx = Tick(), Tick(), Tick(), Tick()

            def scores(n):
                rows, k, cols = place(n)
                for a, b in SPANS:
                    pe.wait_ge(e_ready, spans.step())
                    three_pass(nc, score[:, a:b], [x[rows, k, cols] for x in (qs_hi, qs_lo)],
                               [x[rows, k, a:b] for x in (g.k_hi, g.k_lo)], True, True).then_inc(s_done, 1)

            def turn(n):
                for q, (j0, j1) in enumerate(PIECES):
                    if q == 0:
                        pe.wait_ge(p_ready, sub.step())
                    pe.wait_ge(tp_free, tp.step())
                    for j in range(j0, j1):
                        last = nc.tensor.transpose(piece(q)[:, j - j0, :], prob[:, n % 4, j * P:(j + 1) * P],
                                                   g.ident[0:P, 0:P])
                    last.then_inc(tp_done, 1)

            def context(hh, half):
                if half == 0:
                    v = ctx.step()
                    pe.wait_ge(c_free, v)
                    pe.wait_ge(tp_free, 6 * v + 3)
                for j in range(half * NT // 2, (half + 1) * NT // 2):
                    last = three_pass(nc, ctx_bank[:, 0:CH],
                                      [x[:, j, 128 * (hh // 2):128 * (hh // 2) + 128] for x in (g.v_hi, g.v_lo)],
                                      [x[:, j, :] for x in pt[hh % 2]], j == 0, j == NT - 1)
                if half == 1:
                    last.then_inc(c_done, 1)

            def output(c, s):
                if s == 0:
                    pe.wait_ge(c_free, ctx.base + ctx.n + 1)
                pe.wait_ge(summed, 2 * c + s + 1)
                for k in range(KT):
                    last = three_pass(nc, core.bank(7)[0:P, :],
                                      [x[:, k, s * P:(s + 1) * P] for x in (ctx_hi, ctx_lo)],
                                      [x[:, k, :] for x in (wo_hi, wo_lo)], k == 0, k == KT - 1)
                last.then_inc(o_done, 1)

            def chunk(c, steps, live):
                if live(0):
                    pe.wait_ge(q_in, 32 * (c + 1))
                for n in steps:
                    if live(n):
                        scores(n)
                    if n in (OUT, OUT + 1) and live(-1):
                        output(c - 1, n - OUT)
                    if live(n - 5):
                        context((n - 5) % SUBS // 2, (n - 5) % 2)
                    if live(n - 2):
                        turn((n - 2) % SUBS)

            chunks(pe, chunk, ((spans, 3 * SUBS), (sub, SUBS), (tp, 3 * SUBS), (ctx, NH)))


def expert_mixture(core, g, w, ln):
    nc, at, sem = core.nc, core.at, core.sem
    NE, HID = 8, 256
    MT = HID // 128
    t_, pre = at("moe_t", [P, NT, D], F32, 12), at("moe_pre", [P, NT, D], F32, 32)
    raw1, raw2 = at("moe_raw1", [128, KT, HID], F32, 92), at("moe_raw2", [128, MT, D], F32, 96)
    w1 = [[at(f"moe_w1_{x}{i}", [128, KT, HID], F32R, 100 + 8 * i + 4 * j) for j, x in enumerate(("hi", "lo"))]
          for i in range(2)]
    w2 = [[at(f"moe_w2_{x}{i}", [128, MT, D], F32R, 116 + 8 * i + 4 * j) for j, x in enumerate(("hi", "lo"))]
          for i in range(2)]
    r = at("moe_gelu", [128, MT, CH], F32, 132)
    h_hi, h_lo = at("moe_h_hi", [128, MT, CH], F32R, 134), at("moe_h_lo", [128, MT, CH], F32R, 136)
    g1, beta1, g2, beta2 = (at(n, [P, D], F32, 140 + 2 * i) for i, n in enumerate(("g1", "beta1", "g2", "beta2")))
    b2 = at("moe_b2", [NE, D], F32, 148)
    bg, b1 = at("moe_bg", [P, NE], F32, 150), at("moe_b1", [128, NE * MT], F32, 150.125)
    wg = at("moe_wg", [128, KT, NE], F32, 150.25)
    wg_hi, wg_lo = at("moe_wg_hi", [128, KT, NE], F32R, 150.375), at("moe_wg_lo", [128, KT, NE], F32R, 150.5)
    x3 = at("moe_x3", [P, NT, D], F32, 152)
    hot_t = at("moe_hot_t", [NE, N], F32, 172)
    S = 177
    lg, hot, rank = at("moe_lg", [P, NT, NE], F32, S), at("moe_hot", [P, NT * NE], F32, S + .5), at("moe_rank", [P, NE], F32, S + 1)
    best = at("moe_best", [P, NT, 1], F32, S + 1.125)
    hot3 = hot[:].rearrange("p (t e) -> p t e", e=NE)

    pre_in, small_in = sem("moe_pre_in"), sem("moe_small_in")
    raw1_in, raw2_in = sem("moe_raw1_in"), sem("moe_raw2_in")
    x3_ready, wg_hi_done, wg_ready = sem("moe_x3"), sem("moe_wg_hi_done"), sem("moe_wg_ready")
    t_ready, lg_done, hot_ready = sem("moe_t_ready"), sem("moe_lg_done"), sem("moe_hot_ready")
    ht_done, ht_ready, b2_done, b2_added = sem("moe_ht_done"), sem("moe_ht_ready"), sem("moe_b2_done"), sem("moe_b2_added")
    w_hi, w_lo = sem("moe_w_hi"), sem("moe_w_lo")
    u_done, u_bank, u_hi, u_lo = sem("moe_u_done"), sem("moe_bank_free"), sem("moe_hi"), sem("moe_lo")
    out_done, added = sem("moe_out_done"), sem("moe_added")
    final, stored = sem("final_ready"), sem("out_stored")
    turned = g.turned.again()
    ln.turn += 2
    turn = ln.turn - 1
    w1_rows = w["W1e"].rearrange("e (k p) n -> e p k n", p=128)
    w2_rows = w["W2e"].rearrange("e (k p) n -> e p k n", p=128)

    def experts(eng, body, counts):
        with eng.Fori(0, NE // 2 - 1) as pair:
            for tick, per in counts:
                tick.enter(pair, 2 * per)
            for par in range(2):
                body(2 * pair + par, par, True)
            for tick, per in counts:
                tick.leave(NE // 2 - 1)
        for par in range(2):
            body(NE - 2 + par, par, par == 0)

    with nc.Block() as block:
        @block.sync
        def _(sp):
            sp.dma_start(pre[:], tiles(g.pre_store)).then_inc(pre_in, 16)
            for dst, src in ((g1[:], row_view(w["g1"])), (beta1[:], row_view(w["beta1"])), (g2[:], row_view(w["g2"])),
                             (beta2[:], row_view(w["beta2"])), (bg[:], row_view(w["bg"])), (b2[:], w["b2e"]), (b1[:], w["b1e"]),
                             (wg[:], w["Wg"].rearrange("(k p) n -> p k n", p=128)), (x3[:], tiles(g.x3_store))):
                sp.dma_start(dst, src).then_inc(small_in, 16)
            sp.dma_start(raw1[:], w1_rows[0]).then_inc(raw1_in, 16)
            sp.dma_start(raw2[:], w2_rows[0]).then_inc(raw2_in, 16)
            with sp.Fori(1, NE) as e:
                sp.wait_ge(w_lo, 2 * e - 1)
                sp.dma_start(raw1[:], w1_rows[bass.ds(e, 1)].rearrange("a p k n -> (a p) k n")).then_inc(raw1_in, 16)
                sp.wait_ge(w_lo, 2 * e)
                sp.dma_start(raw2[:], w2_rows[bass.ds(e, 1)].rearrange("a p k n -> (a p) k n")).then_inc(raw2_in, 16)
            for t in range(NT):
                sp.wait_ge(final, t + 1)
                sp.dma_start(w["out"][t * P:(t + 1) * P, :], t_[:, t, :]).then_inc(stored, 16)
            sp.wait_ge(stored, 16 * NT)

        @block.gpsimd
        def _(pool):
            pool.wait_ge(small_in, 144)
            for t in range(NT):
                last = nc.gpsimd.tensor_tensor(x3[:, t, :], x3[:, t, :], beta2[:], ALU.add)
            last.then_inc(x3_ready, 1)

        @block.scalar
        def _(act):
            ln.root_at(nc, act, turn)
            act.wait_ge(small_in, 144)
            nc.scalar.activation(wg_hi[:], wg[:], ACT.Copy).then_inc(wg_hi_done, 1)
            turned.scalar(core, act, g.xt_hi)

            def split(e, par):
                act.wait_ge(raw1_in, 16 * e + 16)
                nc.scalar.activation(w1[par][0][:], raw1[:], ACT.Copy).then_inc(w_hi, 1)
                act.wait_ge(raw2_in, 16 * e + 16)
                nc.scalar.activation(w2[par][0][:], raw2[:], ACT.Copy).then_inc(w_hi, 1)

            split(0, 0)
            units, its = Tick(), Tick()

            def hidden(e):
                for m in range(MT):
                    v = units.step()
                    act.wait_ge(u_done, v)
                    act.wait_ge(u_lo, v)
                    nc.scalar.activation(r[:, m, :], core.bank(6 + m)[:, 0:CH], ACT.Gelu,
                                         bias=b1[:, bass.ds(MT * e + m, 1)]).then_inc(u_bank, 1)
                act.wait_ge(out_done, 2 * its.step())
                act.wait_ge(u_bank, 2 + v)
                for m in range(MT):
                    nc.scalar.activation(h_hi[:, m, :], r[:, m, :], ACT.Copy).then_inc(u_hi, 1)

            def expert(e, par, more):
                if more:
                    act.wait_ge(out_done, 2 * its.base + 2 * its.n + 2)
                    split(e + 1, 1 - par)
                with act.Fori(0, NC) as c:
                    units.enter(c, MT), its.enter(c, 1)
                    hidden(e)
                    units.leave(NC), its.leave(NC)

            experts(act, expert, ((units, MT * NC), (its, NC)))
            ln.root_at(nc, act, turn + 1)

        @block.vector
        def _(dve):
            link = core.link.on(dve)
            dve.wait_ge(pre_in, 16)
            dve.wait_ge(small_in, 144)
            affine(nc, link, pre, t_, ln, turn, g1, [beta1[:]] * NT, None)
            dve.sem_inc(t_ready, 1)
            dve.wait_ge(wg_hi_done, 1)
            nc.vector.tensor_tensor(wg_lo[:], wg[:], f32(wg_hi[:]), ALU.subtract).then_inc(wg_ready, 1)
            turned.vector(core, dve, g.xt_hi, g.xt_lo)
            for e in range(NE):
                last = nc.vector.memset(rank[:, e:e + 1], float(NE - e))
            link(last)
            dve.wait_ge(lg_done, 1)
            gl = core.bank(0)[0:P, 0:NT * NE].rearrange("p (t e) -> p t e", e=NE)
            link(nc.vector.tensor_tensor(lg[:], gl, bc(bg[:], NT), ALU.add))
            link(nc.vector.tensor_reduce(best[:], lg[:], AX.X, ALU.max))
            link(nc.vector.tensor_tensor(lg[:], lg[:], best[:].broadcast_to([P, NT, NE]), ALU.is_equal))
            link(nc.vector.tensor_tensor(lg[:], lg[:], bc(rank[:], NT), ALU.mult))
            link(nc.vector.tensor_reduce(best[:], lg[:], AX.X, ALU.max))
            nc.vector.tensor_tensor(hot3, lg[:], best[:].broadcast_to([P, NT, NE]), ALU.is_equal).then_inc(hot_ready, 1)
            for q in range(3):
                n = min(4, NT - 4 * q) * P
                dve.wait_ge(ht_done, q + 1)
                last = nc.vector.tensor_copy(hot_t[:, 4 * q * P:4 * q * P + n], core.bank(1 + q)[0:NE, 0:n])
            last.then_inc(ht_ready, 1)
            for t in range(NT):
                dve.wait_ge(b2_done, t + 1)
                nc.vector.tensor_tensor(t_[:, t, :], t_[:, t, :], core.bank(4 + t % 2)[0:P, :],
                                        ALU.add).then_inc(b2_added, 1)

            halves, units, subs = Tick(), Tick(), Tick()

            def split(par):
                for dst, src in ((w1[par], raw1), (w2[par], raw2)):
                    dve.wait_ge(w_hi, halves.step())
                    nc.vector.tensor_tensor(dst[1][:], src[:], f32(dst[0][:]), ALU.subtract).then_inc(w_lo, 1)

            split(0)

            def rests():
                for m in range(MT):
                    dve.wait_ge(u_hi, units.step())
                    nc.vector.tensor_tensor(h_lo[:, m, :], r[:, m, :], f32(h_hi[:, m, :]), ALU.subtract).then_inc(u_lo, 1)

            def add_out(c, e):
                for s in range(2):
                    dve.wait_ge(out_done, subs.step() + 2)
                    dst = t_[:, bass.ds(2 * c + s, 1), :].rearrange("p a n -> p (a n)")
                    nc.vector.scalar_tensor_tensor(dst, core.bank(s)[0:P, :], hot[:, bass.ds(NE * (2 * c + s) + e, 1)],
                                                   dst, ALU.mult, ALU.add).then_inc(added, 1)

            def expert(e, par, more):
                if more:
                    split(1 - par)
                rests()
                with dve.Fori(1, NC) as c:
                    units.enter(c - 1, MT), subs.enter(c - 1, 2)
                    rests()
                    add_out(c - 1, e)
                    units.leave(NC - 1), subs.leave(NC - 1)
                add_out(NC - 1, e)

            experts(dve, expert, ((halves, 2), (units, MT * NC), (subs, 2 * NC)))
            dve.wait_ge(added, 2 * NC * NE + 2)
            dve.wait_ge(x3_ready, 1)
            affine(nc, link, t_, t_, ln, turn + 1, g2, [x3[:, t, :] for t in range(NT)], final)

        @block.tensor
        def _(pe):
            pe.wait_ge(t_ready, 1)
            turned.tensor(core, pe, t_, g.ident)
            pe.wait_ge(turned.lo, turned.before + NT)
            pe.wait_ge(wg_ready, 1)
            for t in range(NT):
                for k in range(KT):
                    last = three_pass(nc, core.bank(0)[0:P, NE * t:NE * t + NE],
                                      [a[:, k, t * P:(t + 1) * P] for a in (g.xt_hi, g.xt_lo)],
                                      [a[:, k, :] for a in (wg_hi, wg_lo)], k == 0, k == KT - 1)
            last.then_inc(lg_done, 1)
            pe.wait_ge(hot_ready, 1)
            for t in range(NT):
                q, j = divmod(t, 4)
                last = nc.tensor.transpose(core.bank(1 + q)[0:NE, j * P:(j + 1) * P], hot3[:, t, :], g.ident[0:P, 0:P])
                if j == 3 or t == NT - 1:
                    last.then_inc(ht_done, 1)
            pe.wait_ge(ht_ready, 1)
            for t in range(NT):
                if t >= 2:
                    pe.wait_ge(b2_added, t - 1)
                nc.tensor.matmul(core.bank(4 + t % 2)[0:P, :], hot_t[:, t * P:(t + 1) * P], b2[:], start=True,
                                 stop=True).then_inc(b2_done, 1)
            units, subs = Tick(), Tick()

            def hidden(c, par):
                for m in range(MT):
                    pe.wait_ge(u_bank, units.step())
                    for k in range(KT):
                        last = three_pass(nc, core.bank(6 + m)[:, 0:CH],
                                          [a[:, k, m * 128:(m + 1) * 128] for a in w1[par]],
                                          [a[:, k, bass.ds(CH * c, CH)] for a in (g.xt_hi, g.xt_lo)],
                                          k == 0, k == KT - 1)
                    last.then_inc(u_done, 1)

            def outputs(c, par, ahead):
                pe.wait_ge(u_lo, units.base + units.n - ahead + 2)
                for s in range(2):
                    pe.wait_ge(added, subs.step())
                    for k in range(MT):
                        last = three_pass(nc, core.bank(s)[0:P, :], [a[:, k, s * P:(s + 1) * P] for a in (h_hi, h_lo)],
                                          [a[:, k, :] for a in w2[par]], k == 0, k == MT - 1)
                    last.then_inc(out_done, 1)

            def expert(e, par, more):
                pe.wait_ge(w_lo, 2 * e + 2)
                hidden(0, par)
                with pe.Fori(1, NC) as c:
                    units.enter(c - 1, MT), subs.enter(c - 1, 2)
                    hidden(c, par)
                    outputs(c - 1, par, MT)
                    units.leave(NC - 1), subs.leave(NC - 1)
                outputs(NC - 1, par, 0)

            experts(pe, expert, ((units, MT * NC), (subs, 2 * NC)))


class Shared:
    pass


def program(nc, w):
    with ExitStack() as stack:
        core = Core(nc, stack)
        at = core.at
        g = Shared()
        g.ident, g.lohi = at("ident", [128, 128], F32, 0), at("lohi", [128, 2 * NT], I32, 0.5)
        g.node_ids = at("node_ids", [128, N], F16, 1)
        g.small = 1
        ln, g.turned = NormState(core, 2.5), Turned(core)
        core.parts = []
        g.gcol, g.headflag = at("gcol", [128, KT, 2], F32, 3.5), at("headflag", [128, HEADS], F32, 3.5625)
        g.has_edge = at("has_edge", [P, NT], F32, 3.625)
        g.bq, g.bk = at("bq_cols", [128, HEADS * KT], F32, 4), at("bk_cols", [128, HEADS * KT], F32, 4.125)
        g.tcols, g.ucols = at("t_cols", [128, HEADS * KT], F32, 4.25), at("u_cols", [128, HEADS * KT], F32, 4.375)
        g.cd, g.cols_in = at("score_consts", [P, NT * HEADS], F32, 4.5), core.sem("bias_cols_in")
        g.agg = at("edge_mean", [P, NT, EDGE_D], F32, 8)
        g.x, g.xs = at("x_first", [P, NT, D], F32, 160), at("xs_first", [P, NT, D], F32, 180)
        g.xn_hi, g.xn_lo = at("xn_hi", [P, NT, D], F32R, 12), at("xn_lo", [P, NT, D], F32R, 32)
        g.xt_hi, g.xt_lo = at("xt_hi", [128, KT, N], F32R, 52), at("xt_lo", [128, KT, N], F32R, 72)
        g.acc, g.gs_acc = at("acc", [P, NT, D], F32, 92), at("gs_acc", [128, KT, D], F32, 144)
        g.attr_sums = at("attr_sums", [P, NT, PARTS], F32, 112)
        g.counts = nc.dram_tensor("edge_counts", [N, N], U16, kind="Internal").ap()
        g.x3_store, g.xs_store, g.pre_store = (
            nc.dram_tensor(n, [N, D], F32, kind="Internal").ap() for n in ("x3_store", "xs_store", "pre_store"))

        g.qk_store, g.vl_store = (
            nc.dram_tensor(n, [HEADS, 128, KT, D], F32, kind="Internal").ap() for n in ("qk_store", "vl_store"))
        g.gs_store = nc.dram_tensor("skip_store", [128, KT, D], F32, kind="Internal").ap()
        g.q_store = [nc.dram_tensor(n, [128, KT, N], F32, kind="Internal").ap() for n in ("q_hi_store", "q_lo_store")]

        edge_ranges(core, g, w["dst_pairs"], w["src_cols"], w["dst_cols"], w["x"], w["attr"])
        count_edges(core, g)
        head_matrices(core, g, w)
        first_features(core, g, ln)
        graph_attention(core, g, w)
        core.next_part()
        g.x, g.xs = at("x_res", [P, NT, D], F32, 12), at("xs_res", [P, NT, D], F32, 32)
        graph_output(core, g, w, ln)
        expert_lora(core, g, w, ln)
        edge_mean_gnn(core, g, w, ln)
        keys_values(core, g, w, ln)
        self_attention(core, g, w)
        expert_mixture(core, g, w, ln)


def lay_out(i):
    def turned(a):
        return a.swapaxes(-1, -2)

    def cols(a, *lead):
        return np.moveaxis(a.reshape(*a.shape[:-1], -1, 128), -1, 0)

    gates = np.concatenate([i["L0_ffn_gate_w"], i["L0_ffn_thr_w"], np.zeros((1, D), np.float32)])
    out = {
        "x": i["x"],
        "dst_pairs": i["dst"].reshape(EP, 2 * P), "src_cols": i["src"].reshape(2 * EP, P).T,
        "dst_cols": i["dst"].reshape(2 * EP, P).T,
        "attr": i["edge_attr_64"].reshape(2 * EP, P, EDGE_D).transpose(1, 0, 2),
        "WqT": turned(i["L0_gnn_Wq"]), "WkT": turned(i["L0_gnn_Wk"]), "WvT": turned(i["L0_gnn_Wv"]),
        "WskipT": turned(i["L0_gnn_Wskip"]), "Wlin": i["L0_gnn_Wlin"],
        "bq": cols(i["L0_gnn_bq"]), "bk": cols(i["L0_gnn_bk"]), "bv": cols(i["L0_gnn_bv"]),
        "bskip": cols(i["L0_gnn_bskip"]),
        "blin": i["L0_gnn_blin"], "gamma": i["L0_gnn_gamma"], "beta": i["L0_gnn_beta"],
        "gates": gates.reshape(6, KT, 128).transpose(2, 1, 0),
        "lora_A": i["L0_ffn_lora_A"].reshape(4, KT, 128, 16).transpose(2, 0, 1, 3),
        "lora_B": turned(i["L0_ffn_lora_B"]).reshape(4, KT, 128, 16).transpose(2, 0, 1, 3),
        "fc1T": turned(i["L0_ffn_fc1_w"]), "fc2T": turned(i["L0_ffn_fc2_w"]),
        "W1": i["L1_gnn_W1"], "b1": cols(i["L1_gnn_b1"]), "W2": i["L1_gnn_W2"], "b2": i["L1_gnn_b2"],
        "Wq2": i["L1_ffn_Wq"], "Wk2": i["L1_ffn_Wk"], "Wv2": i["L1_ffn_Wv"], "Wo": i["L1_ffn_Wo"],
        "bq2": cols(i["L1_ffn_bq"]), "bk2": cols(i["L1_ffn_bk"]), "bv2": i["L1_ffn_bv"], "bo": i["L1_ffn_bo"],
        "g1": i["L1_ffn_g1"], "beta1": i["L1_ffn_beta1"], "g2": i["L1_ffn_g2"], "beta2": i["L1_ffn_beta2"],
        "Wg": i["L1_ffn_Wg"], "bg": i["L1_ffn_bg"],
        "W1e": i["L1_ffn_W1"], "b1e": cols(i["L1_ffn_b1"].reshape(-1)), "W2e": i["L1_ffn_W2"], "b2e": i["L1_ffn_b2"],
    }
    return {name: np.ascontiguousarray(a) for name, a in out.items()}


def kernel(**inputs):
    import concourse.bacc as bacc
    from concourse.bass_utils import run_bass_kernel_spmd

    arrays = lay_out({name: np.asarray(a) for name, a in inputs.items()})
    nc = bacc.Bacc("TRN2", target_bir_lowering=False, num_devices=1)
    handles = {name: nc.dram_tensor(f"in_{name}", a.shape, mybir.dt.from_np(a.dtype), kind="ExternalInput").ap()
               for name, a in arrays.items()}
    handles["out"] = nc.dram_tensor("out", [N, D], F32, kind="ExternalOutput").ap()
    program(nc, handles)
    result = run_bass_kernel_spmd(nc, [{f"in_{name}": a for name, a in arrays.items()}], core_ids=[0])
    return result.results[0]["out"]
```

```python
from contextlib import ExitStack

import numpy as np
import concourse.bass as bass
from concourse import mybir

F32 = mybir.dt.float32
F32R = mybir.dt.float32r
BF16 = mybir.dt.bfloat16
F16 = mybir.dt.float16
U16 = mybir.dt.uint16
I32 = mybir.dt.int32
ALU = mybir.AluOpType
ACT = mybir.ActivationFunctionType
AX = mybir.AxisListType

N, D = 1250, 512
P = 125
NT = N // P
CH = 2 * P
NC = N // CH
KT = D // 128
EDGES = 21250
GROUP = 4
GROUPS = -(-EDGES // (GROUP * P))
ET = GROUPS * GROUP
EDGE_D = 64
PARTS = 3 * EDGE_D + 2
BANK = 512
SPANS = [(0, 512), (512, 1024), (1024, N)]
HEADS = 4
EPS = 1e-5
OFF = -1e30
NO_EDGE = -1e29


class Tick:

    def __init__(self, first=0):
        self.base, self.n, self.kept = first, 0, []

    def step(self, k=1):
        self.n += k
        return self.base + self.n

    def enter(self, turn, per):
        self.kept.append((self.base, self.n, per))
        self.base, self.n = self.base + self.n + turn * per, 0

    def leave(self, turns):
        base, n, per = self.kept.pop()
        if self.n != per:
            raise AssertionError(f"a turn counts {self.n}, not {per}")
        self.base, self.n = base, n + turns * per


class Link(Tick):

    def __init__(self, eng, sem):
        super().__init__()
        self.eng, self.sem = eng, sem

    def on(self, eng):
        self.eng = eng
        return self

    def __call__(self, ins):
        ins.then_inc(self.sem, 1)
        self.eng.wait_ge(self.sem, self.step())


def bc(ap, t):
    return ap.rearrange("p (a n) -> p a n", a=1).broadcast_to([ap.shape[0], t, ap.shape[1]])


CREDITS = {"hot_free": 4, "count_copied": 2, "count_stored0": 16, "count_stored1": 16,
           "pp_free": 2, "pp_done": 1, "hm_v_free": 1, "hm_v_done1": 1, "hm_p3_done": 1, "hm_u_free": 2,
           "WqT_lo": 1, "WkT_lo": 1, "WvT_lo": 1, "Wlin_lo": 1, "WskipT_lo": 1, "qk_stored": 16, "vl_stored": 16, "s_free": 1, "tp_free": 3, "tp_done": 6,
           "cnt_free0": 1, "cnt_free1": 1, "hid_free": 2, "lora_done": 2, "lw_ready": 1, "ffn_x_added": 2,
           "gh_bank_free": 2, "gh_lo_done": 2, "gnn_x_added": 2,
           "at_e_ready": 3, "at_tp_free": 3, "at_c_free": 1, "at_summed": 1, "at_stored": 16,
           "moe_bank_free": 2, "moe_lo": 2, "moe_out_done": 2, "moe_added": 2}


class Core:

    def __init__(self, nc, stack):
        self.nc, self.stack = nc, stack
        self.bottom = -(-nc.sbuf_base // 128) * 128
        self.psum = stack.enter_context(nc.psum_tensor("psum", [128, 8, BANK], F32))
        self.link = Link(None, stack.enter_context(nc.semaphore("dve_link")))
        self.parts = []
        self.credits = {name: stack.enter_context(nc.semaphore(name)) for name in CREDITS}

    def at(self, name, shape, dtype, kb):
        return self.nc.alloc_sbuf_tensor_at(name, shape, dtype, offset=self.bottom + int(kb * 1024))

    def sem(self, name):
        if name in self.credits:
            return self.credits[name]
        self.parts.append(self.nc.alloc_semaphore(name=name))
        return self.parts[-1]

    def next_part(self):
        self.nc.clear_and_free_semaphores(self.parts)
        self.nc.all_engine_barrier()
        self.parts = []

    def bank(self, b):
        return self.psum[:, b, :]


def three_pass(nc, out, lhs, rhs, start, stop):
    (lh, ll), (rh, rl) = lhs, rhs
    nc.tensor.matmul(out, lh, rh, start=start, stop=False)
    nc.tensor.matmul(out, lh, rl, start=False, stop=False)
    return nc.tensor.matmul(out, ll, rh, start=False, stop=stop)


def layer_stats(nc, link, x, s, turn):
    for t in range(NT):
        last = nc.vector.bn_stats(s.stats[:, t, :], x[:, t, :])
    link(last)
    for t in range(NT):
        last = nc.vector.bn_aggr(s.mv[:, t, :], s.stats[:, t, :])
    link(last)
    nc.vector.tensor_scalar(s.ve[:], s.mv[:, :, 1], EPS, None, ALU.add).then_inc(s.var_ready, 1)
    link.eng.wait_ge(s.std_ready, turn)
    r, r2 = s.r, s.r2
    link(nc.vector.reciprocal(r[:], s.sd[:]))
    link(nc.vector.tensor_tensor(r2[:], r[:], r[:], ALU.mult))
    link(nc.vector.tensor_tensor(r2[:], r2[:], s.ve[:], ALU.mult))
    link(nc.vector.tensor_scalar(r2[:], r2[:], -0.5, 1.5, ALU.mult, ALU.add))
    link(nc.vector.tensor_tensor(r[:], r[:], r2[:], ALU.mult))


def normalise(nc, link, x, out, s, turn, ready):
    layer_stats(nc, link, x, s, turn)
    for t in range(NT):
        nc.vector.tensor_scalar(out[:, t, :], x[:, t, :], s.mv[:, t, 0:1], s.r[:, t:t + 1],
                                ALU.subtract, ALU.mult).then_inc(ready, 1)


def affine(nc, link, x, out, s, turn, gain, shift, ready):
    layer_stats(nc, link, x, s, turn)
    for t in range(NT):
        nc.vector.scalar_tensor_tensor(x[:, t, :], x[:, t, :], s.mv[:, t, 0:1], gain[:], ALU.subtract, ALU.mult)
    link(nc.vector.memset(s.r2[:], 0.0))
    for t in range(NT):
        last = nc.vector.scalar_tensor_tensor(out[:, t, :], x[:, t, :], s.r[:, t:t + 1], shift[t], ALU.mult, ALU.add)
        if ready is not None:
            last.then_inc(ready, 1)
    if ready is None:
        link(last)


class NormState:

    def __init__(self, core, kb):
        at = core.at
        self.stats = at("ln_stats", [P, NT, 6], F32, kb)
        self.mv = at("ln_mean_var", [P, NT, 2], F32, kb + 0.25)
        self.ve = at("ln_var_eps", [P, NT], F32, kb + 0.375)
        self.sd = at("ln_std", [P, NT], F32, kb + 0.5)
        self.r = at("ln_rstd", [P, NT], F32, kb + 0.625)
        self.r2 = at("ln_newton", [P, NT], F32, kb + 0.75)
        self.var_ready, self.std_ready = core.sem("ln_var_ready"), core.sem("ln_std_ready")
        self.turn = 0

    def root(self, nc, eng):
        self.root_at(nc, eng, self.turn)

    def root_at(self, nc, eng, turn):
        eng.wait_ge(self.var_ready, turn)
        nc.scalar.activation(self.sd[:], self.ve[:], ACT.Sqrt).then_inc(self.std_ready, 1)


def edge_ranges(core, g, dst_groups, src_cols, dst_cols, x_in, attr_in):
    nc, at, sem = core.nc, core.at, core.sem
    base = 140
    g.src_i = at("src_i", [P, ET], I32, base)
    g.dst_i = at("dst_i", [P, ET], I32, base + 1)
    dst_p = at("dst_groups", [GROUPS, GROUP * P], I32, base + 7)
    g.src_f = at("src_f", [P, ET], F32, base + 3)
    g.dst_f = at("dst_f", [P, ET], F32, base + 4)
    small = at("range_small", [128, 8], F32, base + 5)
    tile_first = at("tile_first", [128, NT], F32, base + 5.25)
    hit = at("hit", [128, NT], F32, base + 5.5)
    cand = at("cand", [128, 2 * NT], F32, base + 5.75)
    best = at("best", [128, 2 * NT], F32, base + 6)
    lohi_f = at("lohi_f", [128, 2 * NT], F32, base + 6.25)
    s_load, s_iota, s_cand, s_best = sem("edges_loaded"), sem("range_iota"), sem("range_cand"), sem("range_best")
    s_pool = sem("range_pool")
    g.ids_ready, g.x_loaded = sem("ids_ready"), sem("x_loaded")
    attr = at("edge_attr", [P, ET, EDGE_D], F32, 84)
    g.parts = at("edge_parts", [P, ET, PARTS], BF16, 12)
    HALF = ET // 2
    halves = [slice(i * HALF, (i + 1) * HALF) for i in range(2)]
    attr_loaded = [sem("attr_loaded0"), sem("attr_loaded1")]
    part_ready, rest_ready = sem("part_ready"), sem("rest_ready")

    with nc.Block() as block:
        @block.sync
        def _(sp):
            for name, n in CREDITS.items():
                sp.sem_inc(core.credits[name], n)
            sp.dma_start(dst_p[:], dst_groups).then_inc(s_load, 16)
            sp.dma_start(g.dst_i[:], dst_cols).then_inc(s_load, 16)
            sp.dma_start(g.src_i[:], src_cols).then_inc(s_load, 16)
            for i, h in enumerate(halves):
                sp.dma_start(attr[:, h, :], attr_in[:, h, :]).then_inc(attr_loaded[i], 16)
            sp.dma_start(g.x[:], x_in.rearrange("(t p) d -> p t d", p=P)).then_inc(g.x_loaded, 16)

        @block.gpsimd
        def _(pool):
            nc.gpsimd.memset(g.ident[:], 0.0).then_inc(s_pool, 1)
            nc.gpsimd.memset(cand[:], 0.0).then_inc(s_iota, 1)
            nc.gpsimd.iota(tile_first[:], pattern=[[P, NT]], base=0, channel_multiplier=0,
                           allow_small_or_imprecise_dtypes=True).then_inc(s_iota, 1)
            nc.gpsimd.iota(small[:, 0:1], pattern=[[0, 1]], base=1, channel_multiplier=1,
                           allow_small_or_imprecise_dtypes=True).then_inc(s_iota, 1)
            nc.gpsimd.iota(g.node_ids[:], pattern=[[1, N]], base=0, channel_multiplier=0,
                           allow_small_or_imprecise_dtypes=True).then_inc(g.ids_ready, 1)
            pool.wait_ge(s_pool, 1)
            nc.gpsimd.affine_select(out=g.ident[:], in_=g.ident[:], compare_op=ALU.not_equal, fill=1.0,
                                    base=0, pattern=[[-1, 128]], channel_multiplier=1).then_inc(s_pool, 1)
            pool.wait_ge(s_cand, 1)
            nc.gpsimd.partition_all_reduce(best[:], cand[:], 128, bass.bass_isa.ReduceOp.max).then_inc(s_best, 1)

        @block.scalar
        def _(act):
            for n in range(3):
                for i, h in enumerate(halves):
                    if n == 0:
                        act.wait_ge(attr_loaded[i], 16)
                    else:
                        act.wait_ge(rest_ready, 2 * (n - 1) + i + 1)
                    nc.scalar.activation(g.parts[:, h, n * EDGE_D:(n + 1) * EDGE_D], attr[:, h, :],
                                         ACT.Copy).then_inc(part_ready, 1)

        @block.vector
        def _(dve):
            link = core.link.on(dve)
            nc.vector.memset(g.parts[:, :, 3 * EDGE_D:], 1.0)
            dve.wait_ge(s_load, 48)
            dve.wait_ge(s_iota, 3)
            nc.vector.tensor_copy(g.dst_f[:], g.dst_i[:])
            nc.vector.tensor_copy(g.src_f[:], g.src_i[:])
            link(nc.vector.tensor_reduce(small[0:GROUPS, 1:2], dst_p[:], AX.X, ALU.max))
            link(nc.vector.tensor_reduce(small[0:GROUPS, 2:3], dst_p[:], AX.X, ALU.min))
            link(nc.vector.tensor_scalar(small[0:GROUPS, 3:4], small[0:GROUPS, 0:1], -1.0, GROUPS + 1.0, ALU.mult, ALU.add))
            link(nc.vector.tensor_scalar(hit[0:GROUPS, :], tile_first[0:GROUPS, :], small[0:GROUPS, 1:2], None, ALU.is_le))
            link(nc.vector.tensor_scalar(cand[0:GROUPS, 0:NT], tile_first[0:GROUPS, :], float(P), small[0:GROUPS, 2:3],
                                         ALU.add, ALU.is_gt))
            link(nc.vector.tensor_tensor(hit[0:GROUPS, :], hit[0:GROUPS, :], cand[0:GROUPS, 0:NT], ALU.mult))
            link(nc.vector.tensor_scalar(cand[0:GROUPS, 0:NT], hit[0:GROUPS, :], small[0:GROUPS, 0:1], None, ALU.mult))
            nc.vector.tensor_scalar(cand[0:GROUPS, NT:], hit[0:GROUPS, :], small[0:GROUPS, 3:4], None,
                                    ALU.mult).then_inc(s_cand, 1)
            dve.wait_ge(s_best, 1)
            hi, lo = lohi_f[:, NT:], lohi_f[:, 0:NT]
            link(nc.vector.tensor_scalar(hi, best[:, 0:NT], 1.0, None, ALU.max))
            link(nc.vector.tensor_scalar(lo, best[:, NT:], -1.0, float(GROUPS), ALU.mult, ALU.add))
            link(nc.vector.tensor_scalar(cand[:, 0:NT], hi, -1.0, None, ALU.add))
            link(nc.vector.tensor_tensor(lo, lo, cand[:, 0:NT], ALU.min))
            link(nc.vector.tensor_copy(g.lohi[:], lohi_f[:]))
            for n in range(2):
                for i, h in enumerate(halves):
                    dve.wait_ge(part_ready, 2 * n + i + 1)
                    nc.vector.tensor_tensor(attr[:, h, :], attr[:, h, :], g.parts[:, h, n * EDGE_D:(n + 1) * EDGE_D],
                                            ALU.subtract).then_inc(rest_ready, 1)


def group_range(eng, g, t):
    lo = eng.value_load(g.lohi[0:1, bass.ds(t, 1)], min_val=0, max_val=GROUPS - 1)
    hi = eng.value_load(g.lohi[0:1, bass.ds(t + NT, 1)], min_val=1, max_val=GROUPS)
    return lo, hi


def count_edges(core, g):
    nc, at, sem = core.nc, core.at, core.sem
    base = 84
    hot_src = at("hot_src", [P, GROUP, N], BF16, base)
    hot_dst = at("hot_dst", [P, GROUP, 128], BF16, base + 10)
    zero = at("zero_bf", [128, BANK], BF16, base + 11)
    sums = g.attr_sums
    out = at("counts_out", [P, 2, N], U16, base + 12)
    ready, free = sem("hot_ready"), sem("hot_free")
    tile_done = sem("count_tile_done")
    copied, zeroed = sem("count_copied"), sem("zeroed")
    stored = [sem("count_stored0"), sem("count_stored1")]
    rows = g.counts.rearrange("(t p) s -> t p s", p=P)

    with nc.Block() as block:
        @block.vector
        def _(dve):
            nc.vector.memset(zero[:], 0.0).then_inc(zeroed, 1)
            dve.wait_ge(g.ids_ready, 1)
            turn = dve.alloc_register("hot_turn_dve")
            dve.reg_mov(turn, 1)
            with dve.Fori(0, NT) as t:
                lo, hi = group_range(dve, g, t)
                with dve.Fori(lo, hi) as j:
                    for a in range(GROUP):
                        dve.wait_ge(free, turn)
                        dve.reg_add(turn, turn, 1)
                        nc.vector.tensor_scalar(hot_src[:, a, :], g.node_ids[0:P, :], g.src_f[:, bass.ds(GROUP * j + a, 1)],
                                                None, ALU.is_equal)
                        nc.vector.tensor_scalar(hot_dst[:, a, 0:P], g.node_ids[0:P, bass.ds(t * P, P)],
                                                g.dst_f[:, bass.ds(GROUP * j + a, 1)], None,
                                                ALU.is_equal).then_inc(ready, 1)

        @block.tensor
        def _(pe):
            pe.wait_ge(zeroed, 1)
            turn = pe.alloc_register("hot_turn_pe")
            pe.reg_mov(turn, 1)
            with pe.Fori(0, NT // 2) as t2:
                for par in range(2):
                    lo, hi = group_range(pe, g, 2 * t2 + par)
                    acc = core.psum[0:P, 3 * par:3 * par + 3, :].rearrange("p b n -> p (b n)")
                    pe.wait_ge(copied, 2 * t2 + par + 1)
                    att = core.bank(6 + par)[0:P, 0:PARTS]
                    for a, b in SPANS:
                        nc.tensor.matmul(acc[:, a:b], zero[:, 0:P], zero[:, 0:b - a], start=True, stop=False)
                    nc.tensor.matmul(att, zero[:, 0:P], zero[:, 0:PARTS], start=True, stop=False)
                    with pe.Fori(lo, hi) as j:
                        for s in range(GROUP):
                            pe.wait_ge(ready, turn)
                            pe.reg_add(turn, turn, 1)
                            for a, b in SPANS:
                                nc.tensor.matmul(acc[:, a:b], hot_dst[:, s, 0:P], hot_src[:, s, a:b],
                                                 start=False, stop=False)
                            last = nc.tensor.matmul(att, hot_dst[:, s, 0:P],
                                                    g.parts[:, bass.ds(GROUP * j + s, 1), :].rearrange("p a n -> p (a n)"),
                                                    start=False, stop=False)
                            last.then_inc(free, 1)
                    for a, b in SPANS:
                        nc.tensor.matmul(acc[:, a:b], zero[:, 0:P], zero[:, 0:b - a], start=False, stop=True)
                    last = nc.tensor.matmul(att, zero[:, 0:P], zero[:, 0:PARTS], start=False, stop=True)
                    last.then_inc(tile_done, 1)

        @block.scalar
        def _(act):
            with act.Fori(0, NT // 2) as t2:
                for par in range(2):
                    acc = core.psum[0:P, 3 * par:3 * par + 3, :].rearrange("p b n -> p (b n)")
                    act.wait_ge(tile_done, 2 * t2 + par + 1)
                    act.wait_ge(stored[par], 16 * t2 + 16)
                    nc.scalar.activation(sums[:, bass.ds(2 * t2 + par, 1), :].rearrange("p a n -> p (a n)"),
                                         core.bank(6 + par)[0:P, 0:PARTS], ACT.Copy)
                    nc.scalar.activation(out[:, par, :], acc[:, 0:N], ACT.Copy).then_inc(copied, 1)
            
        @block.sync
        def _(sp):
            with sp.Fori(0, NT // 2) as t2:
                for par in range(2):
                    sp.wait_ge(copied, 2 * t2 + par + 3)
                    sp.dma_start(rows[bass.ds(2 * t2 + par, 1), :, :].rearrange("a p s -> (a p) s"),
                                 out[:, par, :]).then_inc(stored[par], 16)
            for par in range(2):
                sp.wait_ge(stored[par], 16 * (NT // 2) + 16)


def f32(ap):
    return ap.bitcast(F32)


class Turned:

    def __init__(self, core):
        self.done, self.hi, self.lo = (core.sem(f"turned{x}") for x in ("", "_hi", "_lo"))
        self.before = -NT

    def again(self):
        self.before += NT
        return self

    def bank(self, core, t):
        return core.bank(t % 8)[:, 0:KT * P].rearrange("p (k n) -> p k n", k=KT)

    def tensor(self, core, pe, xs, ident, ready=None):
        for t in range(NT):
            if ready is not None:
                pe.wait_ge(ready, t + 1)
            if t >= 8:
                pe.wait_ge(self.lo, self.before + t - 7)
            for k in range(KT):
                last = core.nc.tensor.transpose(self.bank(core, t)[:, k, :], xs[:, t, k * 128:(k + 1) * 128],
                                                ident[0:P, 0:P])
            last.then_inc(self.done, 1)

    def scalar(self, core, act, hi):
        for t in range(NT):
            act.wait_ge(self.done, self.before + t + 1)
            core.nc.scalar.activation(hi[:, :, t * P:(t + 1) * P], self.bank(core, t),
                                      ACT.Copy).then_inc(self.hi, 1)

    def vector(self, core, dve, hi, lo):
        for t in range(NT):
            dve.wait_ge(self.hi, self.before + t + 1)
            core.nc.vector.tensor_tensor(lo[:, :, t * P:(t + 1) * P], self.bank(core, t),
                                         f32(hi[:, :, t * P:(t + 1) * P]), ALU.subtract).then_inc(self.lo, 1)


class Thin:
    ROWS = 8

    def __init__(self, core, name, pads_kb, rows_kb):
        self.core = core
        self.hi = core.at(f"{name}_hi", [128, KT, 128], F32R, pads_kb)
        self.lo = core.at(f"{name}_lo", [128, KT, 128], F32R, pads_kb + 2)
        self.rows = core.at(f"{name}_rows", [self.ROWS, N], F32, rows_kb)
        self.cleared, self.rounded, self.split, self.wide, self.rows_ready, self.done = (
            core.sem(f"{name}_{x}") for x in ("cleared", "rounded", "split", "wide", "rows_ready", "turned"))
        self.out = core.bank(3)[0:P, 0:NT * self.ROWS].rearrange("p (t e) -> p t e", e=self.ROWS)

    def gpsimd(self, nc):
        nc.gpsimd.memset(f32(self.hi[:]), 0.0)
        nc.gpsimd.memset(f32(self.lo[:]), 0.0).then_inc(self.cleared, 1)

    def scalar(self, nc, act, cols):
        act.wait_ge(self.cleared, 1)
        nc.scalar.activation(self.hi[:, :, 0:cols.shape[2]], cols, ACT.Copy).then_inc(self.rounded, 1)

    def vector(self, nc, dve, cols):
        dve.wait_ge(self.rounded, 1)
        n = cols.shape[2]
        nc.vector.tensor_tensor(self.lo[:, :, 0:n], cols, f32(self.hi[:, :, 0:n]), ALU.subtract).then_inc(self.split, 1)

    def tensor(self, nc, pe, xt):
        pe.wait_ge(self.split, 1)
        for q, (a, b) in enumerate(SPANS):
            for k in range(KT):
                last = three_pass(nc, self.core.bank(q)[:, 0:b - a], [x[:, k, :] for x in (self.hi, self.lo)],
                                  [x[:, k, a:b] for x in xt], k == 0, k == KT - 1)
            last.then_inc(self.wide, 1)

    def vector_rows(self, nc, dve):
        for q, (a, b) in enumerate(SPANS):
            dve.wait_ge(self.wide, q + 1)
            last = nc.vector.tensor_copy(self.rows[:, a:b], self.core.bank(q)[0:self.ROWS, 0:b - a])
        last.then_inc(self.rows_ready, 1)

    def tensor_turn(self, nc, pe, ident):
        pe.wait_ge(self.rows_ready, 1)
        for t in range(NT):
            last = nc.tensor.transpose(self.out[:, t, :], self.rows[:, t * P:(t + 1) * P],
                                       ident[0:self.ROWS, 0:self.ROWS])
        last.then_inc(self.done, 1)


def first_features(core, g, ln):
    nc, at, sem = core.nc, core.at, core.sem
    turned = g.turned.again()
    thin = Thin(core, "ucol", 200, 144)
    ucols = g.ucols[:].rearrange("p (h k) -> p k h", k=KT)
    bqk, bqbk = at("bqk_cols", [128, HEADS * KT], F32, g.small + .25), at("bqbk", [P, HEADS], F32, g.small + .375)
    ones = at("ones_cd", [128, P], F32, g.small + .5)
    ones_ready, agg_link, cnt_ready = sem("f0_ones"), sem("f0_agg_link"), sem("f0_cnt_ready")
    xs_ready, nm_hi = sem("f0_xs"), sem("f0_nm_hi")
    ln.turn += 1
    with nc.Block() as block:
        @block.vector
        def _(dve):
            link = core.link.on(dve)
            cnt = g.attr_sums[:, :, 3 * EDGE_D:3 * EDGE_D + 1]
            link(nc.vector.tensor_scalar(cnt, cnt, 1.0, None, ALU.max))
            nc.vector.reciprocal(cnt, cnt).then_inc(cnt_ready, 1)
            dve.wait_ge(g.x_loaded, 16)
            normalise(nc, link, g.x, g.xs, ln, ln.turn, xs_ready)
            link(nc.vector.tensor_tensor(bqk[:], g.bq[:], g.bk[:], ALU.mult))
            nc.vector.memset(ones[:], 1.0).then_inc(ones_ready, 1)
            dve.wait_ge(nm_hi, 1)
            nc.vector.tensor_tensor(g.xn_lo[:], g.xs[:], f32(g.xn_hi[:]), ALU.subtract)
            thin.vector(nc, dve, ucols)
            turned.vector(core, dve, g.xt_hi, g.xt_lo)
            thin.vector_rows(nc, dve)
            dve.wait_ge(thin.done, 1)
            link(nc.vector.tensor_reduce(bqbk[:], core.bank(4)[0:P, 0:HEADS * KT].rearrange("p (h k) -> p h k", k=KT),
                                         AX.X, ALU.add))
            nc.vector.tensor_tensor(g.cd[:].rearrange("p (t h) -> p t h", h=HEADS),
                                    thin.out[:, :, 0:HEADS],
                                    bc(bqbk[:], NT), ALU.add)

        @block.scalar
        def _(act):
            thin.scalar(nc, act, ucols)
            ln.root(nc, act)
            act.wait_ge(xs_ready, NT)
            nc.scalar.activation(g.xn_hi[:], g.xs[:], ACT.Copy).then_inc(nm_hi, 1)
            turned.scalar(core, act, g.xt_hi)

        @block.tensor
        def _(pe):
            turned.tensor(core, pe, g.xs, g.ident, xs_ready)
            pe.wait_ge(turned.lo, turned.before + NT)
            thin.tensor(nc, pe, (g.xt_hi, g.xt_lo))
            pe.wait_ge(ones_ready, 1)
            nc.tensor.matmul(core.bank(4)[0:P, 0:HEADS * KT], ones[:], bqk[:], start=True, stop=True)
            thin.tensor_turn(nc, pe, g.ident)

        @block.gpsimd
        def _(pool):
            thin.gpsimd(nc)
            link = Link(pool, agg_link)
            link(nc.gpsimd.memset(g.acc[:], 0.0))
            sums, cnt = g.attr_sums, g.attr_sums[:, :, 3 * EDGE_D:3 * EDGE_D + 1]
            link(nc.gpsimd.tensor_tensor(g.agg[:], sums[:, :, 0:EDGE_D], sums[:, :, EDGE_D:2 * EDGE_D], ALU.add))
            link(nc.gpsimd.tensor_tensor(g.agg[:], g.agg[:], sums[:, :, 2 * EDGE_D:3 * EDGE_D], ALU.add))
            pool.wait_ge(cnt_ready, 1)
            nc.gpsimd.tensor_tensor(g.agg[:], g.agg[:], cnt.broadcast_to([P, NT, EDGE_D]), ALU.mult)


def head_matrices(core, g, w):
    nc, at, sem = core.nc, core.at, core.sem
    names = ("WqT", "WkT", "WvT", "Wlin", "WskipT")
    Q, K, V, LIN, SKIP = range(5)
    raw = [at(f"raw_{n}", [128, KT, D], F32, kb) for n, kb in zip(names, (120, 128, 136, 144, 196))]
    halves = [[at(f"{n}_{x}", [128, KT, D], F32R, 20 + 16 * i + 8 * j) for j, x in enumerate(("hi", "lo"))]
              for i, n in enumerate(names)]
    out = [at("qk_out0", [128, KT, D], F32, 12), at("vl_out0", [128, KT, D], F32, 100)]
    zero = at("zero_head", [128, D], BF16, 180)
    bvs = at("bvs_cols", [128, 2, HEADS * KT], F32, g.small)
    raw_in = [sem(f"{n}_in") for n in names]
    split_hi, split_lo_ = sem("hm_hi"), [sem(f"{n}_lo") for n in names]
    v_done, v_free, zeroed = [sem("hm_v_done0"), sem("hm_v_done1")], sem("hm_v_free"), sem("hm_zeroed")
    lin_ready, p3_done = sem("hm_lin_ready"), sem("hm_p3_done")
    u_done, u_free = sem("hm_u_done"), sem("hm_u_free")
    stored = [sem("qk_stored"), sem("vl_stored")]
    flag, gs_ready, gs_stored = sem("hm_flag"), sem("hm_gs_ready"), sem("hm_gs_stored")
    bank = lambda u: core.bank(4 + u % 2)
    stores = (g.qk_store, g.vl_store)

    def wview(ap, h):
        return ap.rearrange("(h k p) n -> h p k n", p=128, k=KT)[bass.ds(h, 1)].rearrange("a p k n -> (a p) k n")

    with nc.Block() as block:
        @block.sync
        def _(sp):
            for dst, name in ((g.bq[:], "bq"), (g.bk[:], "bk"), (bvs[:, 0, :], "bv"), (bvs[:, 1, :], "bskip")):
                sp.dma_start(dst, w[name]).then_inc(g.cols_in, 16)
            with sp.Fori(0, HEADS) as h:
                for i in (Q, K, V, LIN, SKIP):
                    if i in (Q, K):
                        sp.wait_ge(v_free, h + 1)
                    elif i == LIN:
                        sp.wait_ge(v_done[1], h + 1)
                        sp.wait_ge(split_lo_[i], h + 1)
                    else:
                        sp.wait_ge(split_lo_[i], h + 1)
                    sp.dma_start(raw[i][:], wview(w[names[i]], h)).then_inc(raw_in[i], 16)
            sp.wait_ge(gs_ready, 1)
            sp.dma_start(g.gs_store, g.gs_acc[:]).then_inc(gs_stored, 16)
            sp.wait_ge(gs_stored, 16)

        @block.scalar
        def _(act):
            def hi(i, h):
                act.wait_ge(raw_in[i], 16 * h + 16)
                if i == LIN:
                    act.wait_ge(lin_ready, h + 1)
                    act.wait_ge(p3_done, h + 1)
                nc.scalar.activation(halves[i][0][:], raw[i][:], ACT.Copy).then_inc(split_hi, 1)

            units = Tick()
            with act.Fori(0, HEADS) as h:
                units.enter(h, 2 * KT)
                hi(Q, h), hi(K, h), hi(V, h), hi(LIN, h)
                for i in range(2):
                    if i == 1:
                        hi(SKIP, h)
                    act.wait_ge(stored[i], 16 * h + 16)
                    for m in range(KT):
                        act.wait_ge(u_done, units.step())
                        nc.scalar.activation(out[i][:, m, :], bank(m), ACT.Copy).then_inc(u_free, 1)
                    act.wait_ge(u_free, 2 + units.base + units.n)
                    act.dma_start(stores[i][bass.ds(h, 1)].rearrange("a p k n -> (a p) k n"),
                                  out[i][:]).then_inc(stored[i], 16)
                units.leave(HEADS)
            for i in range(2):
                act.wait_ge(stored[i], 16 * HEADS + 16)

        @block.vector
        def _(dve):
            nc.vector.memset(zero[:], 0.0).then_inc(zeroed, 1)
            nc.vector.memset(g.headflag[:], 0.0).then_inc(flag, 1)
            dve.wait_ge(flag, 1)
            nc.vector.memset(g.headflag[:, 0:1], 1.0).then_inc(flag, 1)
            dve.wait_ge(flag, 2)
            his = Tick()

            def lo(i):
                dve.wait_ge(split_hi, his.step())
                nc.vector.tensor_tensor(halves[i][1][:], raw[i][:], f32(halves[i][0][:]),
                                        ALU.subtract).then_inc(split_lo_[i], 1)

            with dve.Fori(0, HEADS) as h:
                his.enter(h, 5)
                lo(Q), lo(K)
                dve.wait_ge(raw_in[LIN], 16 * h + 16)
                for k in range(KT):
                    blk = raw[LIN][:, k, k * 128:(k + 1) * 128]
                    last = nc.vector.scalar_tensor_tensor(blk, g.ident[:], g.headflag[:, bass.ds(h, 1)], blk,
                                                          ALU.mult, ALU.add)
                last.then_inc(lin_ready, 1)
                lo(V), lo(LIN)
                dve.wait_ge(v_done[0], h + 1)
                nc.vector.tensor_copy(g.tcols[:, bass.ds(KT * h, KT)], core.bank(6)[:, 0:KT])
                nc.vector.tensor_copy(g.ucols[:, bass.ds(KT * h, KT)], core.bank(6)[:, KT:2 * KT]).then_inc(v_free, 1)
                lo(SKIP)
                his.leave(HEADS)
            dve.wait_ge(p3_done, HEADS + 2)
            nc.vector.tensor_copy(g.gcol[:], core.bank(7)[:, 0:2 * KT].rearrange("p (k i) -> p k i", i=2))
            nc.vector.tensor_copy(g.gs_acc[:], core.psum[:, 0:KT, :]).then_inc(gs_ready, 1)

        @block.tensor
        def _(pe):
            units = Tick()
            pe.wait_ge(zeroed, 1)
            for b in (0, 1, 2, 3, 7):
                nc.tensor.matmul(core.bank(b), zero[:, 0:128], zero[:], start=True, stop=False)

            def product(i, j, out_of, summed=False):
                for m in range(KT):
                    dst = out_of(m)
                    for k in range(KT):
                        last = three_pass(nc, dst, [x[:, k, m * 128:(m + 1) * 128] for x in halves[i]],
                                          [x[:, k, :] for x in halves[j]], not summed and k == 0,
                                          not summed and k == KT - 1)
                    if not summed:
                        last.then_inc(u_done, 1)
                return last

            def unit(m):
                pe.wait_ge(u_free, units.step())
                return bank(m)

            pe.wait_ge(g.cols_in, 64)
            with pe.Fori(0, HEADS) as h:
                units.enter(h, 2 * KT)
                pe.wait_ge(v_free, h + 1)
                pe.wait_ge(raw_in[Q], 16 * h + 16)
                pe.wait_ge(raw_in[K], 16 * h + 16)
                for c, (i, bias) in enumerate(((K, g.bq), (Q, g.bk))):
                    for m in range(KT):
                        for k in range(KT):
                            last = nc.tensor.matmul(core.bank(6)[:, c * KT + m:c * KT + m + 1],
                                                    raw[i][:, k, m * 128:(m + 1) * 128],
                                                    bias[:, bass.ds(KT * h + k, 1)], start=k == 0, stop=k == KT - 1)
                last.then_inc(v_done[0], 1)
                pe.wait_ge(split_lo_[Q], h + 2)
                pe.wait_ge(split_lo_[K], h + 2)
                product(Q, K, unit)
                pe.wait_ge(lin_ready, h + 1)
                for m in range(KT):
                    for k in range(KT):
                        last = nc.tensor.matmul(core.bank(7)[:, 2 * m:2 * m + 2], raw[LIN][:, k, m * 128:(m + 1) * 128],
                                                bvs[:, :, bass.ds(KT * h + k, 1)].rearrange("p i a -> p (i a)"),
                                                start=False, stop=False)
                last.then_inc(v_done[1], 1)
                pe.wait_ge(split_lo_[V], h + 2)
                pe.wait_ge(split_lo_[LIN], h + 2)
                product(V, LIN, unit)
                pe.wait_ge(split_lo_[SKIP], h + 2)
                product(SKIP, LIN, core.bank, summed=True).then_inc(p3_done, 1)
                units.leave(HEADS)
            for b in (0, 1, 2, 3, 7):
                last = nc.tensor.matmul(core.bank(b), zero[:, 0:128], zero[:], start=False, stop=True)
            last.then_inc(p3_done, 1)


def graph_attention(core, g, w):
    nc, at, sem = core.nc, core.at, core.sem
    scale = 1.0 / np.sqrt(float(D)).item()
    m_hi, m_lo = at("qk_hi", [128, KT, D], F32R, 112), at("qk_lo", [128, KT, D], F32R, 120)
    g_hi, g_lo = at("vl_hi", [128, KT, D], F32R, 128), at("vl_lo", [128, KT, D], F32R, 136)
    g.g_hi, g.g_lo = g_hi, g_lo
    raw1 = at("raw1", [128, KT, D], F32, 152)
    R = 160
    t_hi, t_lo = at("t_hi", [128, KT, CH], F32R, R), at("t_lo", [128, KT, CH], F32R, R + 4)
    yt_hi, yt_lo = at("yt_hi", [128, KT, CH], F32R, 144), at("yt_lo", [128, KT, CH], F32R, 148)
    pt_hi, pt_lo = at("pt_hi", [P, NT, CH], F32R, R + 8), at("pt_lo", [P, NT, CH], F32R, R + 18)
    prob = at("prob", [P, 2, N], F32, R + 28)
    cnt = at("cnt", [P, 2, N], U16, R + 38)
    maskb = at("maskb", [P, N], BF16, R + 43)
    S = g.small
    mx, mxc, nb = (at(n, [P, 2], F32, S + i / 32) for i, n in enumerate(("mx", "mxc", "nb")))
    den, rden = (at(n, [P, 2], F32, S + .125 + i / 32) for i, n in enumerate(("den", "rden")))

    raw_in, raw_free, split_hi = sem("heads_in"), sem("heads_free"), sem("heads_hi")
    pp_done, pp_free, pp_hi = sem("pp_done"), sem("pp_free"), sem("pp_hi")
    s_done, s_free, m_ready, e_ready = sem("s_done"), sem("s_free"), sem("m_ready"), sem("e_ready")
    p_ready, tcol_ready = sem("p_ready"), sem("tcol_ready")
    tcol = at("t_col", [128, KT], F32, g.small + .5)
    tp_done, tp_hi, tp_free = sem("tp_done"), sem("tp_hi"), sem("tp_free")
    cl, c_free = [sem("cnt_loaded0"), sem("cnt_loaded1")], [sem("cnt_free0"), sem("cnt_free1")]

    bank = lambda u: core.bank(6 + u % 2)
    score = core.psum[0:P, 0:3, :].rearrange("p b n -> p (b n)")
    rows = g.counts.rearrange("(t p) s -> t p s", p=P)
    PIECES = [(0, 4), (4, 8), (8, 10)]

    def piece(q):
        j0, j1 = PIECES[q]
        return core.bank(3 + q)[0:P, 0:(j1 - j0) * P].rearrange("p (j n) -> p j n", n=P)

    def pipeline(eng, chunk, last_outputs, vl_split, counts):
        chunk(0, 0, None, False)
        vl_split(0)
        with eng.Fori(0, HEADS - 1) as h:
            for tick, per in counts:
                tick.enter(h, NC * per)
            with eng.Fori(1, NC - 1) as c:
                for tick, per in counts:
                    tick.enter(c - 1, per)
                chunk(h, c, c - 1, False)
                for tick, per in counts:
                    tick.leave(NC - 2)
            chunk(h, NC - 1, NC - 2, True)
            chunk(h + 1, 0, NC - 1, False)
            vl_split(h + 1)
            for tick, per in counts:
                tick.leave(HEADS - 1)
        with eng.Fori(1, NC) as c:
            for tick, per in counts:
                tick.enter(c - 1, per)
            chunk(HEADS - 1, c, c - 1, False)
            for tick, per in counts:
                tick.leave(NC - 1)
        last_outputs()

    with nc.Block() as block:
        @block.sync
        def _(sp):
            def matrix_in(store, h):
                src = store[bass.ds(h, 1)].rearrange("a p k n -> (a p) k n")
                sp.dma_start(raw1[:], src).then_inc(raw_in, 16)

            def counts_in(h, c):
                for s in range(2):
                    sp.wait_ge(c_free[s], NC * h + c + 1)
                    sp.dma_start(cnt[:, s, :], rows[bass.ds(2 * c + s, 1), :, :].rearrange("a p s -> (a p) s")
                                 ).then_inc(cl[s], 16)

            matrix_in(g.qk_store, 0)
            sp.wait_ge(raw_free, 1)
            matrix_in(g.vl_store, 0)
            counts_in(0, 0)
            with sp.Fori(0, HEADS - 1) as h:
                sp.wait_ge(raw_free, 2 * h + 2)
                matrix_in(g.qk_store, h + 1)
                with sp.Fori(1, NC) as c:
                    counts_in(h, c)
                sp.wait_ge(raw_free, 2 * h + 3)
                matrix_in(g.vl_store, h + 1)
                counts_in(h + 1, 0)
            with sp.Fori(1, NC) as c:
                counts_in(HEADS - 1, c)

        @block.scalar
        def _(act):
            pp, tp, sub = Tick(), Tick(), Tick()

            def split_in(value, dst):
                act.wait_ge(raw_in, 16 * value)
                nc.scalar.activation(dst[:], raw1[:], ACT.Copy).then_inc(split_hi, 1)

            def unit_to(dst, rows_=128, n=D, bias=None):
                act.wait_ge(pp_done, 1 + pp.step())
                src = bank((pp.n - 1))[0:rows_, 0:n]
                if bias is None:
                    ins = nc.scalar.activation(dst, src, ACT.Copy)
                else:
                    ins = nc.scalar.activation(dst, src, ACT.Identity, bias=bias)
                ins.then_inc(pp_hi, 1)

            def t_units(h, c):
                if isinstance(c, int) and c == 0:
                    nc.scalar.activation(tcol[:], g.tcols[:, bass.ds(KT * h, KT)], ACT.Copy).then_inc(tcol_ready, 1)
                    act.wait_ge(tcol_ready, h + 1)
                for m in range(KT):
                    unit_to(t_hi[:, m, :], n=CH, bias=tcol[:, m:m + 1])

            def exponentials(s):
                act.wait_ge(m_ready, sub.step())
                nc.scalar.activation(prob[:, s, :], prob[:, s, :], ACT.Exp, bias=nb[:, s:s + 1],
                                     scale=scale).then_inc(e_ready, 1)

            def y_unit(m):
                unit_to(yt_hi[:, m, :], n=CH)

            def turn_hi(s):
                for q, (j0, j1) in enumerate(PIECES):
                    act.wait_ge(tp_done, 6 + tp.step())
                    nc.scalar.activation(pt_hi[:, j0:j1, s * P:(s + 1) * P], piece(q), ACT.Copy).then_inc(tp_hi, 1)

            def chunk(h, c, before, split):
                units = [lambda m=m: y_unit(m) for m in range(KT)] if before is not None else [lambda: None] * KT
                t_units(h, c)
                units[0]()
                exponentials(0)
                units[1](), units[2]()
                exponentials(1)
                units[3]()
                turn_hi(0)
                if split:
                    split_in(2 * h + 3, m_hi)
                if before is not None:
                    pp.step(2)
                turn_hi(1)

            def last_outputs():
                for m in range(KT):
                    y_unit(m)
                pp.step(2)

            split_in(1, m_hi)
            pipeline(act, chunk, last_outputs, lambda h: split_in(2 * h + 2, g_hi), ((pp, 10), (tp, 6), (sub, 2)))

        @block.vector
        def _(dve):
            link = core.link.on(dve)
            pp, tp, sub, hi = Tick(), Tick(), Tick(), Tick()

            def split_lo(value, dst_hi, dst_lo):
                dve.wait_ge(split_hi, value)
                nc.vector.tensor_tensor(dst_lo[:], raw1[:], f32(dst_hi[:]), ALU.subtract).then_inc(raw_free, 1)

            def unit():
                v = pp.step()
                return v, bank(pp.n - 1)

            def unit_lo(dst_hi, dst_lo, n=D, bias=None):
                _, b = unit()
                dve.wait_ge(pp_hi, hi.step())
                if bias is None:
                    ins = nc.vector.tensor_tensor(dst_lo, b[:, 0:n], f32(dst_hi), ALU.subtract)
                else:
                    ins = nc.vector.scalar_tensor_tensor(dst_lo, b[:, 0:n], bias, f32(dst_hi), ALU.add, ALU.subtract)
                ins.then_inc(pp_free, 1)

            def t_units(h):
                for m in range(KT):
                    unit_lo(t_hi[:, m, :], t_lo[:, m, :], CH, g.tcols[:, bass.ds(KT * h + m, 1)])

            def y_unit(m):
                unit_lo(yt_hi[:, m, :], yt_lo[:, m, :], CH)

            def mask(s, it):
                dve.wait_ge(cl[s], 16 * it + 16)
                link(nc.vector.tensor_scalar(maskb[:], cnt[:, s, :], 0.0, OFF, ALU.is_equal, ALU.mult))

            def maximum(s, const):
                v = sub.step()
                dve.wait_ge(tp_done, 3 * v)
                dve.wait_ge(s_done, v)
                nc.vector.memset(mxc[:, s:s + 1], 0.0)
                nc.vector.tensor_tensor_reduce(out=prob[:, s, :], in0=score[:, 0:N], in1=maskb[:], scale=1.0,
                                               scalar=NO_EDGE, op0=ALU.add, op1=ALU.max,
                                               accum_out=mx[:, s:s + 1]).then_inc(s_free, 1)
                dve.wait_ge(s_free, v + 1)
                link(nc.vector.tensor_tensor(mxc[:, s:s + 1], mx[:, s:s + 1], const, ALU.add))
                nc.vector.tensor_scalar(nb[:, s:s + 1], mxc[:, s:s + 1], const, -scale,
                                        ALU.subtract, ALU.mult).then_inc(m_ready, 1)

            def normalise_sum(s, it, tile):
                dve.wait_ge(e_ready, sub.base + sub.n)
                nc.vector.tensor_tensor_reduce(out=prob[:, s, :], in0=prob[:, s, :], in1=cnt[:, s, :], scale=1.0,
                                               scalar=0.0, op0=ALU.mult, op1=ALU.add,
                                               accum_out=den[:, s:s + 1]).then_inc(c_free[s], 1)
                dve.wait_ge(c_free[s], it + 2)
                link(nc.vector.tensor_scalar(g.has_edge[:, bass.ds(tile, 1)], den[:, s:s + 1], 0.5, None, ALU.is_ge))
                link(nc.vector.tensor_scalar(den[:, s:s + 1], den[:, s:s + 1], 0.5, None, ALU.max))
                link(nc.vector.reciprocal(rden[:, s:s + 1], den[:, s:s + 1]))
                nc.vector.tensor_scalar(prob[:, s, :], prob[:, s, :], rden[:, s:s + 1], None,
                                        ALU.mult).then_inc(p_ready, 1)

            def turn_lo(s):
                for q, (j0, j1) in enumerate(PIECES):
                    dve.wait_ge(tp_hi, tp.step())
                    nc.vector.tensor_tensor(pt_lo[:, j0:j1, s * P:(s + 1) * P], piece(q),
                                            f32(pt_hi[:, j0:j1, s * P:(s + 1) * P]), ALU.subtract).then_inc(tp_free, 1)

            def add_out(c):
                for s in range(2):
                    v, b = unit()
                    dve.wait_ge(pp_done, 1 + v)
                    dst = g.acc[:, bass.ds(2 * c + s, 1), :].rearrange("p a n -> p (a n)")
                    nc.vector.tensor_tensor(dst, dst, b[0:P, :], ALU.add).then_inc(pp_free, 1)

            def chunk(h, c, before, split):
                def y(m):
                    if before is not None:
                        y_unit(m)

                it = NC * h + c
                const = [g.cd[:, bass.ds(HEADS * (2 * c + s) + h, 1)] for s in range(2)]
                t_units(h)
                mask(0, it)
                y(0)
                maximum(0, const[0])
                y(1)
                normalise_sum(0, it, 2 * c)
                y(2)
                mask(1, it)
                maximum(1, const[1])
                y(3)
                normalise_sum(1, it, 2 * c + 1)
                turn_lo(0)
                if split:
                    split_lo(2 * h + 3, m_hi, m_lo)
                if before is not None:
                    add_out(before)
                turn_lo(1)

            def last_outputs():
                for m in range(KT):
                    y_unit(m)
                add_out(NC - 1)

            split_lo(1, m_hi, m_lo)
            pipeline(dve, chunk, last_outputs, lambda h: split_lo(2 * h + 2, g_hi, g_lo),
                     ((pp, 10), (tp, 6), (sub, 2), (hi, 8), (link, 10)))

        @block.tensor
        def _(pe):
            pp, tp, sub = Tick(), Tick(), Tick()

            def unit():
                v = pp.step()
                pe.wait_ge(pp_free, v)
                return bank(pp.n - 1)

            def t_units(c):
                for m in range(KT):
                    out = unit()
                    for k in range(KT):
                        last = three_pass(nc, out[:, 0:CH], [x[:, k, m * 128:(m + 1) * 128] for x in (m_hi, m_lo)],
                                          [x[:, k, bass.ds(CH * c, CH)] for x in (g.xt_hi, g.xt_lo)],
                                          k == 0, k == KT - 1)
                    last.then_inc(pp_done, 1)

            def scores(s, t_end):
                if s == 0:
                    pe.wait_ge(pp_free, t_end + 2)
                pe.wait_ge(s_free, sub.step())
                for a, b in SPANS:
                    for k in range(KT):
                        last = three_pass(nc, score[:, a:b], [x[:, k, s * P:(s + 1) * P] for x in (t_hi, t_lo)],
                                          [x[:, k, a:b] for x in (g.xt_hi, g.xt_lo)], k == 0, k == KT - 1)
                last.then_inc(s_done, 1)

            def turn(s):
                v = tp.step()
                pe.wait_ge(p_ready, v)
                pe.wait_ge(tp_free, 3 * v)
                for q, (j0, j1) in enumerate(PIECES):
                    for j in range(j0, j1):
                        last = nc.tensor.transpose(piece(q)[:, j - j0, :], prob[:, s, j * P:(j + 1) * P],
                                                   g.ident[0:P, 0:P])
                    last.then_inc(tp_done, 1)

            def y_unit(m):
                if m == 0:
                    pe.wait_ge(tp_free, 3 * (tp.base + tp.n) + 3)
                out = unit()
                for j in range(NT):
                    last = three_pass(nc, out[:, 0:CH], [x[:, j, m * 128:(m + 1) * 128] for x in (g.xn_hi, g.xn_lo)],
                                      [x[:, j, :] for x in (pt_hi, pt_lo)], j == 0, j == NT - 1)
                last.then_inc(pp_done, 1)

            def out_units():
                pe.wait_ge(pp_free, pp.base + pp.n + 2)
                for s in range(2):
                    out = unit()
                    for k in range(KT):
                        last = three_pass(nc, out[0:P, :], [x[:, k, s * P:(s + 1) * P] for x in (yt_hi, yt_lo)],
                                          [x[:, k, :] for x in (g_hi, g_lo)], k == 0, k == KT - 1)
                    last.then_inc(pp_done, 1)

            def chunk(h, c, before, split):
                def y(m):
                    if before is not None:
                        y_unit(m)

                if isinstance(c, int) and c == 0:
                    pe.wait_ge(raw_free, 2 * h + 1)
                t_units(c)
                t_end = pp.base + pp.n
                y(0)
                scores(0, t_end)
                y(1), y(2)
                scores(1, t_end)
                y(3)
                turn(0)
                if before is not None:
                    pe.wait_ge(raw_free, 2 * h + (0 if isinstance(c, int) and c == 0 else 2))
                    out_units()
                turn(1)

            def last_outputs():
                for m in range(KT):
                    y_unit(m)
                out_units()

            pipeline(pe, chunk, last_outputs, lambda h: None, ((pp, 10), (tp, 2), (sub, 2)))


def row_view(ap, rows=P):
    return ap.rearrange("(a n) -> a n", a=1).broadcast_to([rows, ap.shape[0]])


def tiles(ap):
    return ap.rearrange("(t p) d -> p t d", p=P)


def graph_output(core, g, w, ln):
    nc, at, sem = core.nc, core.at, core.sem
    ones = at("ones_f", [128, P], F32, 170)
    diag = at("diag", [128, 2 * KT, 128], F32, 4)
    rows = at("bias_rows", [P, 2, D], F32, 160)
    gamma, beta, blin = (at(n, [P, D], F32, 164 + 2 * i) for i, n in enumerate(("gamma", "beta", "blin")))
    x = g.x
    loaded, x_in, gs_in = sem("go_rows_loaded"), sem("go_x_loaded"), sem("go_gs_in")
    gs_hi, gs_lo, diag_ready = sem("go_gs_hi"), sem("go_gs_lo"), sem("go_diag")
    row_done, done, free = sem("go_row_done"), sem("go_done"), sem("go_free")
    xb = sem("go_x_beta")
    ln.turn += 1
    turn = ln.turn
    with nc.Block() as block:
        @block.sync
        def _(sp):
            for dst, src in ((blin, w["blin"]), (gamma, w["gamma"]), (beta, w["beta"])):
                sp.dma_start(dst[:], row_view(src)).then_inc(loaded, 16)
            sp.dma_start(g.gs_acc[:], g.gs_store).then_inc(gs_in, 16)
            sp.dma_start(x[:], tiles(w["x"])).then_inc(x_in, 16)

        @block.gpsimd
        def _(pool):
            pool.wait_ge(loaded, 48)
            pool.wait_ge(x_in, 16)
            for t in range(NT):
                last = nc.gpsimd.tensor_tensor(x[:, t, :], x[:, t, :], beta[:], ALU.add)
            last.then_inc(xb, 1)

        @block.scalar
        def _(act):
            act.wait_ge(gs_in, 16)
            nc.scalar.activation(g.g_hi[:], g.gs_acc[:], ACT.Copy).then_inc(gs_hi, 1)
            ln.root(nc, act)

        @block.vector
        def _(dve):
            link = core.link.on(dve)
            nc.vector.memset(ones[:], 1.0)
            for i in range(2):
                for k in range(KT):
                    last = nc.vector.tensor_scalar(diag[:, i * KT + k, :], g.ident[:], g.gcol[:, k, i:i + 1], None,
                                                   ALU.mult)
            last.then_inc(diag_ready, 1)
            dve.wait_ge(gs_hi, 1)
            nc.vector.tensor_tensor(g.g_lo[:], g.gs_acc[:], f32(g.g_hi[:]), ALU.subtract).then_inc(gs_lo, 1)
            dve.wait_ge(row_done, 2)
            link(nc.vector.tensor_copy(rows[:, 0, :], core.bank(6)[0:P, :]))
            dve.wait_ge(loaded, 48)
            link(nc.vector.tensor_tensor(rows[:, 1, :], blin[:], core.bank(7)[0:P, :], ALU.add))
            for t in range(NT):
                last = nc.vector.scalar_tensor_tensor(g.acc[:, t, :], rows[:, 0, :], g.has_edge[:, t:t + 1],
                                                      g.acc[:, t, :], ALU.mult, ALU.add)
            link(last)
            link(nc.vector.tensor_tensor(g.acc[:], g.acc[:], rows[:, 1:2, :].broadcast_to([P, NT, D]), ALU.add))
            for t in range(NT):
                dve.wait_ge(done, t + 1)
                nc.vector.tensor_tensor(g.acc[:, t, :], g.acc[:, t, :], core.bank(t % 6)[0:P, :],
                                        ALU.add).then_inc(free, 1)
            dve.wait_ge(free, NT)
            layer_stats(nc, link, g.acc, ln, turn)
            for t in range(NT):
                nc.vector.scalar_tensor_tensor(g.acc[:, t, :], g.acc[:, t, :], ln.mv[:, t, 0:1], gamma[:],
                                               ALU.subtract, ALU.mult)
            link(nc.vector.memset(ln.r2[:], 0.0))
            dve.wait_ge(xb, 1)
            for t in range(NT):
                nc.vector.scalar_tensor_tensor(x[:, t, :], g.acc[:, t, :], ln.r[:, t:t + 1], x[:, t, :],
                                               ALU.mult, ALU.add)

        @block.tensor
        def _(pe):
            pe.wait_ge(diag_ready, 1)
            for i in range(2):
                for k in range(KT):
                    last = nc.tensor.matmul(core.bank(6 + i)[0:P, k * 128:(k + 1) * 128], ones[:],
                                            diag[:, i * KT + k, :], start=True, stop=True)
                last.then_inc(row_done, 1)
            pe.wait_ge(gs_lo, 1)
            for t in range(NT):
                if t >= 6:
                    pe.wait_ge(free, t - 5)
                for k in range(KT):
                    last = three_pass(nc, core.bank(t % 6)[0:P, :],
                                      [a[:, k, t * P:(t + 1) * P] for a in (g.xt_hi, g.xt_lo)],
                                      [a[:, k, :] for a in (g.g_hi, g.g_lo)], k == 0, k == KT - 1)
                last.then_inc(done, 1)


def expert_lora(core, g, w, ln):
    nc, at, sem = core.nc, core.at, core.sem
    NE, R = 4, 16
    x, xs = g.x, g.xs
    fc1_hi, fc1_lo = at("fc1_hi", [128, NE, KT, D], F32R, 92), at("fc1_lo", [128, NE, KT, D], F32R, 124)
    a_hi, a_lo = at("lora_a_hi", [128, NE, KT, 128], F32R, 156), at("lora_a_lo", [128, NE, KT, 128], F32R, 164)
    raw = [at(f"ffn_raw{i}", [128, KT, D], F32, 172 + 8 * i) for i in range(2)]
    wt, wrep = at("weights_t", [NE * R, N], F32, 172), at("weights_rep", [P, NT, NE, R], F32, 177)
    a_raw, b_raw = at("lora_a_raw", [128, NE, KT, R], F32, 188), at("lora_b_raw", [128, NE, KT, R], F32, 189)
    h_hi = [at(f"hid_hi{i}", [128, KT, CH], F32R, 188 + 8 * i) for i in range(2)]
    h_lo = [at(f"hid_lo{i}", [128, KT, CH], F32R, 192 + 8 * i) for i in range(2)]
    b_pad = at("lora_b_pad", [128, NE, KT, NE * R], F32, 4)
    f_sb = at("lora_f", [NE * R, D], F32, 204)
    lw = at("lora_weighted", [NE * R, CH], F32, 206)
    S = g.small
    gw = at("gate_cols", [128, KT, 6], F32, S)
    thin = Thin(core, "gates", 192, 196)
    lg = at("gate_logits", [P, NT, 6], F32, S + .375)
    ex, wgt = at("gate_exp", [P, NT, 6], F32, S + .625), at("gate_weight", [P, NT, NE], F32, S + .875)
    m1, m2 = at("gate_m1", [P, NT, 1], F32, S + 1.0625), at("gate_m2", [P, NT, 1], F32, S + 1.125)

    small_in, raw_in = sem("ffn_small_in"), [sem("ffn_raw_in0"), sem("ffn_raw_in1")]
    raw_free = [sem("ffn_raw_free0"), sem("ffn_raw_free1")]
    xs_ready, hi_done = sem("ffn_xs"), sem("ffn_hi_done")
    small_hi, pads, small_lo = sem("ffn_small_hi"), sem("ffn_pads"), sem("ffn_small_lo")
    gl_ready, ex_ready, wrep_ready, wt_done = (
        sem(f"ffn_{n}") for n in ("gl_ready", "ex_ready", "wrep", "wt_done"))
    start = sem("ffn_prepared")
    u_done, u_hi, u_free = sem("hid_done"), sem("hid_hi_done"), sem("hid_free")
    lora_done, lw_ready, out_done, x_added = sem("lora_done"), sem("lw_ready"), sem("ffn_out_done"), sem("ffn_x_added")
    turned = g.turned.again()
    ln.turn += 1
    turn = ln.turn
    bank = lambda u: core.bank(6 + u % 2)
    UNITS = NE * KT

    with nc.Block() as block:
        @block.sync
        def _(sp):
            sp.dma_start(gw[:], w["gates"]).then_inc(small_in, 16)
            sp.dma_start(a_raw[:], w["lora_A"]).then_inc(small_in, 16)
            sp.dma_start(b_raw[:], w["lora_B"]).then_inc(small_in, 16)
            for i in range(2 * NE):
                if i >= 2:
                    sp.wait_ge(raw_free[i % 2], i // 2)
                src = (w["fc1T"], w["fc2T"])[i // NE][i % NE].rearrange("(k p) n -> p k n", p=128)
                sp.dma_start(raw[i % 2][:], src).then_inc(raw_in[i % 2], 16)

        @block.gpsimd
        def _(pool):
            nc.gpsimd.memset(f32(a_hi[:]), 0.0)
            nc.gpsimd.memset(f32(a_lo[:]), 0.0)
            nc.gpsimd.memset(b_pad[:], 0.0).then_inc(pads, 1)
            thin.gpsimd(nc)

        @block.scalar
        def _(act):
            ln.root(nc, act)
            act.wait_ge(small_in, 48)
            act.wait_ge(pads, 1)
            thin.scalar(nc, act, gw[:])
            for e in range(NE):
                last = nc.scalar.activation(a_hi[:, e, :, R * e:R * e + R], a_raw[:, e, :, :], ACT.Copy)
            last.then_inc(small_hi, 1)
            for e in range(NE):
                if e == 2:
                    turned.scalar(core, act, g.xt_hi)
                act.wait_ge(raw_in[e % 2], 16 * (e // 2 + 1))
                nc.scalar.activation(fc1_hi[:, e, :, :], raw[e % 2][:], ACT.Copy).then_inc(hi_done, 1)
            act.wait_ge(gl_ready, 1)
            nc.scalar.activation(ex[:, :, 0:4], lg[:, :, 0:4], ACT.Exp)
            nc.scalar.activation(ex[:, :, 4:5], lg[:, :, 4:5], ACT.Exp, scale=-1.0).then_inc(ex_ready, 1)
            pp = Tick()
            act.wait_ge(start, 1)
            with act.Fori(0, NC) as c:
                pp.enter(c, UNITS)
                for e in range(NE):
                    act.wait_ge(lora_done, NE * c + e + 1)
                    for m in range(KT):
                        act.wait_ge(u_done, pp.step())
                        nc.scalar.activation(h_hi[e % 2][:, m, :], bank(m)[:, 0:CH], ACT.Relu).then_inc(u_hi, 1)
                pp.leave(NC)

        @block.vector
        def _(dve):
            link = core.link.on(dve)
            normalise(nc, link, x, xs, ln, turn, xs_ready)
            dve.wait_ge(small_hi, 1)
            thin.vector(nc, dve, gw[:])
            for e in range(NE):
                cols = slice(R * e, R * e + R)
                nc.vector.tensor_tensor(a_lo[:, e, :, cols], a_raw[:, e, :, :], f32(a_hi[:, e, :, cols]), ALU.subtract)
            for e in range(NE):
                last = nc.vector.tensor_copy(b_pad[:, e, :, R * e:R * e + R], b_raw[:, e, :, :])
            last.then_inc(small_lo, 1)
            for e in range(NE):
                if e == 2:
                    turned.vector(core, dve, g.xt_hi, g.xt_lo)
                    thin.vector_rows(nc, dve)
                dve.wait_ge(hi_done, e + 1)
                nc.vector.tensor_tensor(fc1_lo[:, e, :, :], raw[e % 2][:], f32(fc1_hi[:, e, :, :]),
                                        ALU.subtract).then_inc(raw_free[e % 2], 1)
            dve.wait_ge(thin.done, 1)
            link(nc.vector.tensor_copy(lg[:], thin.out[:, :, 0:6]))
            link(nc.vector.tensor_reduce(m1[:], lg[:, :, 0:4], AX.X, ALU.max))
            nc.vector.tensor_tensor(lg[:, :, 0:4], lg[:, :, 0:4], m1[:].broadcast_to([P, NT, 4]),
                                    ALU.subtract).then_inc(gl_ready, 1)
            dve.wait_ge(ex_ready, 1)
            link(nc.vector.tensor_reduce(m1[:], ex[:, :, 0:4], AX.X, ALU.add))
            link(nc.vector.reciprocal(m1[:], m1[:]))
            link(nc.vector.tensor_tensor(wgt[:], ex[:, :, 0:4], m1[:].broadcast_to([P, NT, 4]), ALU.mult))
            link(nc.vector.tensor_scalar(m2[:], ex[:, :, 4:5], 1.0, None, ALU.add))
            link(nc.vector.reciprocal(m2[:], m2[:]))
            link(nc.vector.tensor_scalar(m2[:], m2[:], 0.25, None, ALU.mult))
            link(nc.vector.tensor_tensor(wgt[:], wgt[:], m2[:].broadcast_to([P, NT, 4]), ALU.subtract))
            link(nc.vector.tensor_scalar(wgt[:], wgt[:], 0.0, None, ALU.max))
            link(nc.vector.tensor_reduce(m1[:], wgt[:], AX.X, ALU.add))
            link(nc.vector.tensor_scalar(m2[:], m1[:], 0.0, None, ALU.is_equal))
            link(nc.vector.tensor_tensor(m1[:], m1[:], m2[:], ALU.add))
            link(nc.vector.reciprocal(m1[:], m1[:]))
            link(nc.vector.tensor_tensor(wgt[:], wgt[:], m1[:].broadcast_to([P, NT, 4]), ALU.mult))
            dve.wait_ge(raw_free[1], 4)
            nc.vector.tensor_copy(wrep[:], wgt[:].unsqueeze(3).broadcast_to([P, NT, NE, R])).then_inc(wrep_ready, 1)
            link(nc.vector.tensor_copy(f_sb[:], core.bank(4)[0:NE * R, :]))
            for q in range(3):
                n = min(4, NT - 4 * q) * P
                dve.wait_ge(wt_done, q + 1)
                last = nc.vector.tensor_copy(wt[:, 4 * q * P:4 * q * P + n], core.bank(q)[0:NE * R, 0:n])
            last.then_inc(start, 1)
            pp = Tick()
            with dve.Fori(0, NC) as c:
                pp.enter(c, UNITS)
                for e in range(NE):
                    for m in range(KT):
                        dve.wait_ge(u_hi, pp.step())
                        nc.vector.scalar_tensor_tensor(h_lo[e % 2][:, m, :], bank(m)[:, 0:CH], 0.0,
                                                       f32(h_hi[e % 2][:, m, :]), ALU.max,
                                                       ALU.subtract).then_inc(u_free, 1)
                dve.wait_ge(lora_done, NE * c + 6)
                nc.vector.tensor_tensor(lw[:], core.bank(5)[0:NE * R, 0:CH], wt[:, bass.ds(CH * c, CH)],
                                        ALU.mult).then_inc(lw_ready, 1)
                for s in range(2):
                    dve.wait_ge(out_done, 2 * c + s + 1)
                    dst = x[:, bass.ds(2 * c + s, 1), :].rearrange("p a n -> p (a n)")
                    nc.vector.tensor_tensor(dst, dst, core.bank(s)[0:P, :], ALU.add).then_inc(x_added, 1)
                pp.leave(NC)

        @block.tensor
        def _(pe):
            turned.tensor(core, pe, xs, g.ident, xs_ready)
            pe.wait_ge(turned.lo, turned.before + NT)
            pe.wait_ge(small_lo, 1)
            thin.tensor(nc, pe, (g.xt_hi, g.xt_lo))
            thin.tensor_turn(nc, pe, g.ident)
            for e in range(NE):
                pe.wait_ge(raw_in[e % 2], 32 + 16 * (e // 2 + 1))
                for k in range(KT):
                    last = nc.tensor.matmul(core.bank(4)[0:NE * R, :], b_pad[:, e, k, :], raw[e % 2][:, k, :],
                                            start=e == k == 0, stop=e == NE - 1 and k == KT - 1)
                last.then_inc(raw_free[e % 2], 1)
            pe.wait_ge(wrep_ready, 1)
            for t in range(NT):
                q, r = divmod(t, 4)
                last = nc.tensor.transpose(core.bank(q)[0:NE * R, r * P:(r + 1) * P],
                                           wrep[:, t, :, :].rearrange("p e r -> p (e r)"), g.ident[0:P, 0:P])
                if r == 3 or t == NT - 1:
                    last.then_inc(wt_done, 1)
            pe.wait_ge(start, 1)
            pp = Tick()

            def hidden(c, e):
                for m in range(KT):
                    pe.wait_ge(u_free, pp.step())
                    for k in range(KT):
                        last = three_pass(nc, bank(m)[:, 0:CH],
                                          [a[:, e, k, m * 128:(m + 1) * 128] for a in (fc1_hi, fc1_lo)],
                                          [a[:, k, bass.ds(CH * c, CH)] for a in (g.xt_hi, g.xt_lo)],
                                          k == 0, k == KT - 1)
                    last.then_inc(u_done, 1)

            def lora(c, e):
                pe.wait_ge(u_free, pp.base + KT * (e + 1) + 2)
                if e == 0:
                    pe.wait_ge(lw_ready, c + 1)
                for k in range(KT):
                    last = three_pass(nc, core.bank(5)[:, 0:CH], [a[:, e, k, :] for a in (a_hi, a_lo)],
                                      [a[:, k, :] for a in (h_hi[e % 2], h_lo[e % 2])],
                                      e == k == 0, e == NE - 1 and k == KT - 1)
                last.then_inc(lora_done, 1)

            with pe.Fori(0, NC) as c:
                pp.enter(c, UNITS)
                hidden(c, 0)
                for e in range(1, NE):
                    hidden(c, e)
                    lora(c, e - 1)
                lora(c, NE - 1)
                pe.wait_ge(lw_ready, c + 2)
                for s in range(2):
                    pe.wait_ge(x_added, 2 * c + s + 1)
                    nc.tensor.matmul(core.bank(s)[0:P, :], lw[:, s * P:(s + 1) * P], f_sb[:], start=True,
                                     stop=True).then_inc(out_done, 1)
                pp.leave(NC)


def edge_mean_gnn(core, g, w, ln):
    nc, at, sem = core.nc, core.at, core.sem
    HID = 1024
    MT = HID // 128
    x, xs = g.x, g.xs
    w1_hi, w1_lo = at("w1_hi", [128, KT, HID], F32R, 92), at("w1_lo", [128, KT, HID], F32R, 108)
    e1_hi, e1_lo = at("w1e_hi", [EDGE_D, HID], F32R, 124), at("w1e_lo", [EDGE_D, HID], F32R, 128)
    w2_hi, w2_lo = at("w2_hi", [128, MT, D], F32R, 132), at("w2_lo", [128, MT, D], F32R, 148)
    raw = [at(f"gnn_raw{i}", [128, KT, D], F32, 164 + 8 * i) for i in range(2)]
    at_hi, at_lo = at("agg_t_hi", [EDGE_D, N], F32R, 164), at("agg_t_lo", [EDGE_D, N], F32R, 169)
    h_hi, h_lo = at("gh_hi", [128, MT, CH], F32R, 180), at("gh_lo", [128, MT, CH], F32R, 188)
    r = at("gh_relu", [128, 2, CH], F32, 196)
    b2 = at("gnn_b2", [P, D], F32, 4)
    b1 = at("gnn_b1", [128, MT], F32, g.small)

    small_in, raw_in = sem("gnn_small_in"), [sem("gnn_raw_in0"), sem("gnn_raw_in1")]
    raw_free, hi_done = [sem("gnn_raw_free0"), sem("gnn_raw_free1")], sem("gnn_hi_done")
    xs_ready, xres = sem("gnn_xs"), sem("gnn_xres")
    ag_done, ag_hi, prep = sem("gnn_ag_done"), sem("gnn_ag_hi"), sem("gnn_prepared")
    u_done, u_bank, u_hi, u_lo = sem("gh_done"), sem("gh_bank_free"), sem("gh_hi_done"), sem("gh_lo_done")
    out_done, x_added = sem("gnn_out_done"), sem("gnn_x_added")
    turned = g.turned.again()
    ln.turn += 1
    turn = ln.turn
    w1v = w["W1"][0:D, :].rearrange("(k p) n -> p k n", p=128)
    w2v = w["W2"].rearrange("(k p) n -> p k n", p=128)
    loads = [(w1v[:, :, 0:D], lambda b: b[:], (w1_hi[:, :, 0:D], w1_lo[:, :, 0:D])),
             (w1v[:, :, D:], lambda b: b[:], (w1_hi[:, :, D:], w1_lo[:, :, D:])),
             (w2v[:, 0:KT, :], lambda b: b[:], (w2_hi[:, 0:KT, :], w2_lo[:, 0:KT, :])),
             (w2v[:, KT:, :], lambda b: b[:], (w2_hi[:, KT:, :], w2_lo[:, KT:, :])),
             (w["W1"][D:, :], lambda b: b[0:EDGE_D, 0:2, :].rearrange("p a n -> p (a n)"), (e1_hi[:], e1_lo[:]))]
    agg_bank = lambda q: core.bank(q)[0:EDGE_D, 0:min(4, NT - 4 * q) * P]
    agg_cols = lambda q: slice(4 * q * P, 4 * q * P + min(4, NT - 4 * q) * P)

    with nc.Block() as block:
        @block.sync
        def _(sp):
            sp.dma_start(b1[:], w["b1"]).then_inc(small_in, 16)
            sp.dma_start(b2[:], row_view(w["b2"])).then_inc(small_in, 16)
            for i, (src, dst, _) in enumerate(loads):
                if i >= 2:
                    sp.wait_ge(raw_free[i % 2], i // 2)
                sp.dma_start(dst(raw[i % 2]), src).then_inc(raw_in[i % 2], 16)

        @block.gpsimd
        def _(pool):
            pool.wait_ge(xs_ready, NT)
            pool.wait_ge(small_in, 32)
            nc.gpsimd.tensor_tensor(x[:], x[:], xs[:], ALU.add).then_inc(xres, 1)
            pool.wait_ge(xres, 1)
            for t in range(NT):
                last = nc.gpsimd.tensor_tensor(x[:, t, :], x[:, t, :], b2[:], ALU.add)
            last.then_inc(xres, 1)

        @block.scalar
        def _(act):
            ln.root(nc, act)
            for i, (_, dst, (hi, _)) in enumerate(loads):
                act.wait_ge(raw_in[i % 2], 16 * (i // 2 + 1))
                nc.scalar.activation(hi, dst(raw[i % 2]), ACT.Copy).then_inc(hi_done, 1)
            turned.scalar(core, act, g.xt_hi)
            act.wait_ge(raw_free[0], 3)
            act.wait_ge(raw_free[1], 2)
            for q in range(3):
                act.wait_ge(ag_done, q + 1)
                nc.scalar.activation(at_hi[:, agg_cols(q)], agg_bank(q), ACT.Copy).then_inc(ag_hi, 1)
            pp = Tick()
            act.wait_ge(small_in, 32)
            with act.Fori(0, NC) as c:
                pp.enter(c, MT)
                for m in range(MT):
                    v = pp.step()
                    act.wait_ge(u_done, v)
                    act.wait_ge(u_lo, v)
                    nc.scalar.activation(r[:, m % 2, :], core.bank(6 + m % 2)[:, 0:CH], ACT.Relu,
                                         bias=b1[:, m:m + 1]).then_inc(u_bank, 1)
                    act.wait_ge(u_bank, v + 2)
                    nc.scalar.activation(h_hi[:, m, :], r[:, m % 2, :], ACT.Copy).then_inc(u_hi, 1)
                pp.leave(NC)

        @block.vector
        def _(dve):
            link = core.link.on(dve)
            normalise(nc, link, x, xs, ln, turn, xs_ready)
            for i, (_, dst, (hi, lo)) in enumerate(loads):
                dve.wait_ge(hi_done, i + 1)
                nc.vector.tensor_tensor(lo, dst(raw[i % 2]), f32(hi), ALU.subtract).then_inc(raw_free[i % 2], 1)
            turned.vector(core, dve, g.xt_hi, g.xt_lo)
            for q in range(3):
                dve.wait_ge(ag_hi, q + 1)
                last = nc.vector.tensor_tensor(at_lo[:, agg_cols(q)], agg_bank(q), f32(at_hi[:, agg_cols(q)]),
                                               ALU.subtract)
            last.then_inc(prep, 1)
            dve.wait_ge(xres, 2)
            pp = Tick()
            with dve.Fori(0, NC) as c:
                pp.enter(c, MT)
                for m in range(MT):
                    dve.wait_ge(u_hi, pp.step())
                    nc.vector.tensor_tensor(h_lo[:, m, :], r[:, m % 2, :], f32(h_hi[:, m, :]),
                                            ALU.subtract).then_inc(u_lo, 1)
                for s in range(2):
                    dve.wait_ge(out_done, 2 * c + s + 1)
                    dst = x[:, bass.ds(2 * c + s, 1), :].rearrange("p a n -> p (a n)")
                    nc.vector.tensor_tensor(dst, dst, core.bank(s)[0:P, :], ALU.add).then_inc(x_added, 1)
                pp.leave(NC)

        @block.tensor
        def _(pe):
            turned.tensor(core, pe, xs, g.ident, xs_ready)
            pe.wait_ge(turned.lo, turned.before + NT)
            for t in range(NT):
                q, j = divmod(t, 4)
                last = nc.tensor.transpose(core.bank(q)[0:EDGE_D, j * P:(j + 1) * P], g.agg[:, t, :], g.ident[0:P, 0:P])
                if j == 3 or t == NT - 1:
                    last.then_inc(ag_done, 1)
            pe.wait_ge(prep, 1)
            pp = Tick()
            with pe.Fori(0, NC) as c:
                pp.enter(c, MT)
                for m in range(MT):
                    out = core.bank(6 + m % 2)[:, 0:CH]
                    cols = slice(m * 128, (m + 1) * 128)
                    pe.wait_ge(u_bank, pp.step())
                    for k in range(KT):
                        three_pass(nc, out, [a[:, k, cols] for a in (w1_hi, w1_lo)],
                                   [a[:, k, bass.ds(CH * c, CH)] for a in (g.xt_hi, g.xt_lo)], k == 0, False)
                    three_pass(nc, out, [a[:, cols] for a in (e1_hi, e1_lo)],
                               [a[:, bass.ds(CH * c, CH)] for a in (at_hi, at_lo)], False, True).then_inc(u_done, 1)
                pe.wait_ge(u_lo, pp.base + pp.n + 2)
                for s in range(2):
                    pe.wait_ge(x_added, 2 * c + s + 1)
                    for k in range(MT):
                        last = three_pass(nc, core.bank(s)[0:P, :], [a[:, k, s * P:(s + 1) * P] for a in (h_hi, h_lo)],
                                          [a[:, k, :] for a in (w2_hi, w2_lo)], k == 0, k == MT - 1)
                    last.then_inc(out_done, 1)
                pp.leave(NC)


def keys_values(core, g, w, ln):
    nc, at, sem = core.nc, core.at, core.sem
    x, xs = g.x, g.xs
    g.k_hi, g.k_lo = at("k_hi", [128, KT, N], F32R, 92), at("k_lo", [128, KT, N], F32R, 112)
    g.v_hi, g.v_lo = at("v_hi", [P, NT, D], F32R, 132), at("v_lo", [P, NT, D], F32R, 152)
    q_hi, q_lo = at("q_hi", [128, KT, N], F32R, 132), at("q_lo", [128, KT, N], F32R, 152)
    w_hi, w_lo = at("kv_w_hi", [128, KT, D], F32R, 172), at("kv_w_lo", [128, KT, D], F32R, 180)
    raw = at("kv_raw", [128, KT, D], F32, 188)
    vsum = at("v_sum", [P, 2, D], F32, 196)
    bv = at("mha_bv", [P, D], F32, 4)
    bqk = at("mha_bqk", [128, 2, KT], F32, g.small)
    small_in, raw_in, hi_done, lo_done = sem("kv_small_in"), sem("kv_raw_in"), sem("kv_hi_done"), sem("kv_lo_done")
    xs_ready, stash = sem("kv_xs"), sem("kv_stashed")
    done, hi, lo, vs = sem("kv_done"), sem("kv_out_hi"), sem("kv_out_lo"), sem("kv_vsum")
    turned = g.turned.again()
    ln.turn += 1
    turn = ln.turn
    kq_units = [(m, a, b) for m in range(KT) for a, b in SPANS]
    first_k, first_v = len(kq_units), 2 * len(kq_units)
    total = first_v + NT
    q_stored = sem("kv_q_stored")

    def features(u):
        halves, j = ((q_hi, q_lo), 0) if u < first_k else ((g.k_hi, g.k_lo), 1)
        m, a, b = kq_units[u % first_k]
        return *halves, j, m, a, b

    with nc.Block() as block:
        @block.sync
        def _(sp):
            sp.dma_start(bqk[:, 0, :], w["bq2"]).then_inc(small_in, 16)
            sp.dma_start(bqk[:, 1, :], w["bk2"]).then_inc(small_in, 16)
            sp.dma_start(bv[:], row_view(w["bv2"])).then_inc(small_in, 16)
            for i, src in enumerate((w["Wq2"], w["Wk2"], w["Wv2"])):
                if i:
                    sp.wait_ge(lo_done, i)
                sp.dma_start(raw[:], src.rearrange("(k p) n -> p k n", p=128)).then_inc(raw_in, 16)
            sp.dma_start(tiles(g.x3_store), x[:]).then_inc(stash, 16)
            sp.wait_ge(xs_ready, NT)
            sp.dma_start(tiles(g.xs_store), xs[:]).then_inc(stash, 16)
            sp.wait_ge(lo, first_k)
            for dst, src in zip(g.q_store, (q_hi, q_lo)):
                sp.dma_start(dst, f32(src[:])).then_inc(q_stored, 16)
            sp.wait_ge(stash, 32)

        @block.scalar
        def _(act):
            ln.root(nc, act)
            act.wait_ge(raw_in, 16)
            nc.scalar.activation(w_hi[:], raw[:], ACT.Copy).then_inc(hi_done, 1)
            turned.scalar(core, act, g.xt_hi)
            act.wait_ge(small_in, 48)
            for u in range(total):
                if u in (first_k, first_v):
                    act.wait_ge(raw_in, 32 if u == first_k else 48)
                    act.wait_ge(done, u)
                    nc.scalar.activation(w_hi[:], raw[:], ACT.Copy).then_inc(hi_done, 1)
                if u == first_v:
                    act.wait_ge(q_stored, 32)
                if u >= first_v:
                    t = u - first_v
                    act.wait_ge(vs, t + 1)
                    nc.scalar.activation(g.v_hi[:, t, :], vsum[:, t % 2, :], ACT.Copy).then_inc(hi, 1)
                    continue
                dst, _, j, m, a, b = features(u)
                act.wait_ge(done, u + 1)
                nc.scalar.activation(dst[:, m, a:b], core.bank(u % 8)[:, 0:b - a], ACT.Identity,
                                     bias=bqk[:, j, m:m + 1]).then_inc(hi, 1)

        @block.vector
        def _(dve):
            link = core.link.on(dve)
            normalise(nc, link, x, xs, ln, turn, xs_ready)

            def split(n):
                dve.wait_ge(hi_done, n)
                nc.vector.tensor_tensor(w_lo[:], raw[:], f32(w_hi[:]), ALU.subtract).then_inc(lo_done, 1)

            split(1)
            turned.vector(core, dve, g.xt_hi, g.xt_lo)
            dve.wait_ge(small_in, 48)
            for u in range(total):
                if u in (first_k, first_v):
                    split(2 if u == first_k else 3)
                if u >= first_v:
                    t = u - first_v
                    dve.wait_ge(done, u + 1)
                    nc.vector.tensor_tensor(vsum[:, t % 2, :], core.bank(u % 8)[0:P, :], bv[:], ALU.add).then_inc(vs, 1)
                    dve.wait_ge(hi, u + 1)
                    nc.vector.tensor_tensor(g.v_lo[:, t, :], vsum[:, t % 2, :], f32(g.v_hi[:, t, :]),
                                            ALU.subtract).then_inc(lo, 1)
                    continue
                dh, dl, j, m, a, b = features(u)
                dve.wait_ge(hi, u + 1)
                nc.vector.scalar_tensor_tensor(dl[:, m, a:b], core.bank(u % 8)[:, 0:b - a], bqk[:, j, m:m + 1],
                                               f32(dh[:, m, a:b]), ALU.add, ALU.subtract).then_inc(lo, 1)

        @block.tensor
        def _(pe):
            turned.tensor(core, pe, xs, g.ident, xs_ready)
            pe.wait_ge(turned.lo, turned.before + NT)
            for u in range(total):
                if u in (0, first_k, first_v):
                    pe.wait_ge(lo_done, 1 + (u >= first_k) + (u >= first_v))
                if u >= 8:
                    pe.wait_ge(lo, u - 7)
                for k in range(KT):
                    if u >= first_v:
                        t = u - first_v
                        last = three_pass(nc, core.bank(u % 8)[0:P, :],
                                          [a[:, k, t * P:(t + 1) * P] for a in (g.xt_hi, g.xt_lo)],
                                          [a[:, k, :] for a in (w_hi, w_lo)], k == 0, k == KT - 1)
                    else:
                        m, lo_, hi_ = features(u)[-3:]
                        last = three_pass(nc, core.bank(u % 8)[:, 0:hi_ - lo_],
                                          [a[:, k, m * 128:(m + 1) * 128] for a in (w_hi, w_lo)],
                                          [a[:, k, lo_:hi_] for a in (g.xt_hi, g.xt_lo)], k == 0, k == KT - 1)
                last.then_inc(done, 1)


def self_attention(core, g, w):
    nc, at, sem = core.nc, core.at, core.sem
    NH, DH = 8, 64
    scale = DH ** -0.5
    qs_hi, qs_lo = at("qs_hi", [128, KT, CH], F32R, 52), at("qs_lo", [128, KT, CH], F32R, 56)
    ctx_hi, ctx_lo = at("ctx_hi", [128, KT, CH], F32R, 60), at("ctx_lo", [128, KT, CH], F32R, 64)
    wo_hi, wo_lo = at("wo_hi", [128, KT, D], F32R, 68), at("wo_lo", [128, KT, D], F32R, 76)
    raw = at("wo_raw", [128, KT, D], F32, 84)
    pt = [(at("ptm_hi0", [P, NT, CH], F32R, 172), at("ptm_lo0", [P, NT, CH], F32R, 182)),
          (at("ptm_hi1", [P, NT, CH], F32R, 12), at("ptm_lo1", [P, NT, CH], F32R, 22))]
    prob = at("mprob", [P, 4, N], F32, 32)
    xin = at("mha_xin", [P, 2, D], F32, 4)
    bo = at("mha_bo", [P, D], F32, 8)
    S = g.small
    mx, dens = at("mmax", [P, 2, 4], F32, S), at("mden", [P, 2, 4], F32, S + .0625)
    nmx, den, rden = (at(n, [P, 4], F32, S + .125 + i / 16) for i, n in enumerate(("nmx", "mdsum", "mrden")))

    small_in, raw_in, wo_h, wo_ready = sem("at_small_in"), sem("at_raw_in"), sem("at_wo_hi"), sem("at_wo_ready")
    q_in = sem("at_q_in")
    s_done, m_ready, e_ready = sem("at_s_done"), sem("at_m_ready"), sem("at_e_ready")
    r_ready, p_ready = sem("at_r_ready"), sem("at_p_ready")
    tp_done, tp_hi, tp_free = sem("at_tp_done"), sem("at_tp_hi"), sem("at_tp_free")
    c_done, c_hi, c_free = sem("at_c_done"), sem("at_c_hi"), sem("at_c_free")
    o_done, xin_in, summed, stored = sem("at_o_done"), sem("at_xin_in"), sem("at_summed"), sem("at_stored")
    SUBS = 2 * NH
    score = core.psum[0:P, 0:3, :].rearrange("p b n -> p (b n)")
    ctx_bank = core.bank(6)
    PIECES = [(0, 4), (4, 8), (8, 10)]
    OUT = 5

    def piece(q):
        j0, j1 = PIECES[q]
        return core.bank(3 + q)[0:P, 0:(j1 - j0) * P].rearrange("p (j n) -> p j n", n=P)

    def place(n):
        hh, s = n // 2, n % 2
        return slice(DH * (hh % 2), DH * (hh % 2) + DH), hh // 2, slice(s * P, (s + 1) * P)

    def chunks(eng, chunk, counts):
        chunk(0, range(SUBS), lambda j: j >= 0)
        with eng.Fori(1, NC) as c:
            for tick, per in counts:
                tick.enter(c - 1, per)
            chunk(c, range(SUBS), lambda j: True)
            for tick, per in counts:
                tick.leave(NC - 1)
        chunk(NC, range(OUT + 2), lambda j: j < 0)

    def pt_part(n, half, j0, j1):
        return pt[n // 2 % 2][half][:, j0:j1, n % 2 * P:(n % 2 + 1) * P]

    with nc.Block() as block:
        @block.sync
        def _(sp):
            sp.dma_start(raw[:], w["Wo"].rearrange("(k p) n -> p k n", p=128)).then_inc(raw_in, 16)
            sp.dma_start(bo[:], row_view(w["bo"])).then_inc(small_in, 16)

            def load_q(c):
                sp.dma_start(f32(qs_hi[:]), g.q_store[0][:, :, bass.ds(CH * c, CH)]).then_inc(q_in, 16)
                sp.dma_start(f32(qs_lo[:]), g.q_store[1][:, :, bass.ds(CH * c, CH)]).then_inc(q_in, 16)

            def residual_in(c):
                sp.wait_ge(stored, 16 * c + 16)
                sp.dma_start(xin[:], tiles(g.xs_store)[:, bass.ds(2 * c, 2), :]).then_inc(xin_in, 16)

            def rows_out(c):
                sp.wait_ge(summed, 2 * c + 3)
                sp.dma_start(tiles(g.pre_store)[:, bass.ds(2 * c, 2), :], xin[:]).then_inc(stored, 16)

            load_q(0)
            residual_in(0)
            with sp.Fori(0, NC - 1) as c:
                sp.wait_ge(s_done, 3 * SUBS * (c + 1))
                load_q(c + 1)
                rows_out(c)
                residual_in(c + 1)
            rows_out(NC - 1)
            sp.wait_ge(stored, 16 * NC + 16)

        @block.gpsimd
        def _(pool):
            sub = Tick()
            with pool.Fori(0, NC) as c:
                sub.enter(c, SUBS)
                for n in range(SUBS):
                    pool.wait_ge(r_ready, sub.step())
                    nc.gpsimd.tensor_tensor(prob[:, n % 4, :], prob[:, n % 4, :], rden[:, n % 4:n % 4 + 1].broadcast_to([P, N]),
                                            ALU.mult).then_inc(p_ready, 1)
                sub.leave(NC)

        @block.scalar
        def _(act):
            act.wait_ge(raw_in, 16)
            nc.scalar.activation(wo_hi[:], raw[:], ACT.Copy).then_inc(wo_h, 1)
            sub, tp, ctx = Tick(), Tick(), Tick()

            def exponentials(n):
                s = n % 2
                act.wait_ge(m_ready, sub.step())
                for q, (a, b) in enumerate(SPANS):
                    nc.scalar.activation(prob[:, n % 4, a:b], score[:, a:b], ACT.Exp, bias=nmx[:, s:s + 1],
                                         scale=scale, accum_out=dens[:, s, q:q + 1]).then_inc(e_ready, 1)

            def turned_hi(n):
                for q, (j0, j1) in enumerate(PIECES):
                    act.wait_ge(tp_done, tp.step())
                    nc.scalar.activation(pt_part(n, 0, j0, j1), piece(q), ACT.Copy).then_inc(tp_hi, 1)

            def context_hi(hh):
                rows, k, _ = place(2 * hh)
                act.wait_ge(c_done, ctx.step())
                nc.scalar.activation(ctx_hi[rows, k, :], ctx_bank[rows, 0:CH], ACT.Copy).then_inc(c_hi, 1)

            def chunk(c, steps, live):
                for n in steps:
                    if live(n):
                        exponentials(n)
                    if n % 2 == 0 and live(n - 6):
                        context_hi((n - 6) % SUBS // 2)
                    if live(n - 2):
                        turned_hi((n - 2) % SUBS)

            chunks(act, chunk, ((sub, SUBS), (tp, 3 * SUBS), (ctx, NH)))

        @block.vector
        def _(dve):
            link = core.link.on(dve)
            dve.wait_ge(wo_h, 1)
            nc.vector.tensor_tensor(wo_lo[:], raw[:], f32(wo_hi[:]), ALU.subtract).then_inc(wo_ready, 1)
            dve.wait_ge(small_in, 16)
            spans, tp, ctx, exps = Tick(), Tick(), Tick(), Tick()

            def inverse(n):
                s = n % 2
                dve.wait_ge(e_ready, 3 + exps.step(3))
                link(nc.vector.tensor_reduce(den[:, s:s + 1], dens[:, s, 0:3], AX.X, ALU.add))
                nc.vector.reciprocal(rden[:, n % 4:n % 4 + 1], den[:, s:s + 1]).then_inc(r_ready, 1)

            def maximum(n):
                s = n % 2
                for q, (a, b) in enumerate(SPANS):
                    dve.wait_ge(s_done, spans.step())
                    last = nc.vector.tensor_reduce(mx[:, s, q:q + 1], score[:, a:b], AX.X, ALU.max)
                link(last)
                link(nc.vector.tensor_reduce(nmx[:, s:s + 1], mx[:, s, 0:3], AX.X, ALU.max))
                nc.vector.tensor_scalar(nmx[:, s:s + 1], nmx[:, s:s + 1], -scale, None, ALU.mult).then_inc(m_ready, 1)

            def turned_lo(n):
                for q, (j0, j1) in enumerate(PIECES):
                    dve.wait_ge(tp_hi, tp.step())
                    nc.vector.tensor_tensor(pt_part(n, 1, j0, j1), piece(q), f32(pt_part(n, 0, j0, j1)),
                                            ALU.subtract).then_inc(tp_free, 1)

            def context_lo(hh):
                rows, k, _ = place(2 * hh)
                dve.wait_ge(c_hi, ctx.step())
                nc.vector.tensor_tensor(ctx_lo[rows, k, :], ctx_bank[rows, 0:CH], f32(ctx_hi[rows, k, :]),
                                        ALU.subtract).then_inc(c_free, 1)

            def chunk(c, steps, live):
                for n in steps:
                    if live(n - 1):
                        inverse((n - 1) % SUBS)
                    if n % 2 and live(n - 7):
                        context_lo((n - 7) % SUBS // 2)
                    if live(n):
                        maximum(n)
                    if live(n - 3):
                        turned_lo((n - 3) % SUBS)
                    if n == OUT - 2 and live(-1):
                        dve.wait_ge(xin_in, 16 * c)
                        for s in range(2):
                            link(nc.vector.tensor_tensor(xin[:, s, :], xin[:, s, :], bo[:], ALU.add))
                    if n in (OUT, OUT + 1) and live(-1):
                        s = n - OUT
                        dve.wait_ge(o_done, 2 * (c - 1) + s + 1)
                        nc.vector.tensor_tensor(xin[:, s, :], xin[:, s, :], core.bank(7)[0:P, :],
                                                ALU.add).then_inc(summed, 1)

            chunks(dve, chunk, ((spans, 3 * SUBS), (exps, 3 * SUBS), (tp, 3 * SUBS), (ctx, NH), (link, 3 * SUBS + 2)))

        @block.tensor
        def _(pe):
            pe.wait_ge(wo_ready, 1)
            spans, sub, tp, ctx = Tick(), Tick(), Tick(), Tick()

            def scores(n):
                rows, k, cols = place(n)
                for a, b in SPANS:
                    pe.wait_ge(e_ready, spans.step())
                    three_pass(nc, score[:, a:b], [x[rows, k, cols] for x in (qs_hi, qs_lo)],
                               [x[rows, k, a:b] for x in (g.k_hi, g.k_lo)], True, True).then_inc(s_done, 1)

            def turn(n):
                for q, (j0, j1) in enumerate(PIECES):
                    if q == 0:
                        pe.wait_ge(p_ready, sub.step())
                    pe.wait_ge(tp_free, tp.step())
                    for j in range(j0, j1):
                        last = nc.tensor.transpose(piece(q)[:, j - j0, :], prob[:, n % 4, j * P:(j + 1) * P],
                                                   g.ident[0:P, 0:P])
                    last.then_inc(tp_done, 1)

            def context(hh, half):
                if half == 0:
                    v = ctx.step()
                    pe.wait_ge(c_free, v)
                    pe.wait_ge(tp_free, 6 * v + 3)
                for j in range(half * NT // 2, (half + 1) * NT // 2):
                    last = three_pass(nc, ctx_bank[:, 0:CH],
                                      [x[:, j, 128 * (hh // 2):128 * (hh // 2) + 128] for x in (g.v_hi, g.v_lo)],
                                      [x[:, j, :] for x in pt[hh % 2]], j == 0, j == NT - 1)
                if half == 1:
                    last.then_inc(c_done, 1)

            def output(c, s):
                if s == 0:
                    pe.wait_ge(c_free, ctx.base + ctx.n + 1)
                pe.wait_ge(summed, 2 * c + s + 1)
                for k in range(KT):
                    last = three_pass(nc, core.bank(7)[0:P, :],
                                      [x[:, k, s * P:(s + 1) * P] for x in (ctx_hi, ctx_lo)],
                                      [x[:, k, :] for x in (wo_hi, wo_lo)], k == 0, k == KT - 1)
                last.then_inc(o_done, 1)

            def chunk(c, steps, live):
                if live(0):
                    pe.wait_ge(q_in, 32 * (c + 1))
                for n in steps:
                    if live(n):
                        scores(n)
                    if n in (OUT, OUT + 1) and live(-1):
                        output(c - 1, n - OUT)
                    if live(n - 5):
                        context((n - 5) % SUBS // 2, (n - 5) % 2)
                    if live(n - 2):
                        turn((n - 2) % SUBS)

            chunks(pe, chunk, ((spans, 3 * SUBS), (sub, SUBS), (tp, 3 * SUBS), (ctx, NH)))


def expert_mixture(core, g, w, ln):
    nc, at, sem = core.nc, core.at, core.sem
    NE, HID = 8, 256
    MT = HID // 128
    t_, pre = at("moe_t", [P, NT, D], F32, 12), at("moe_pre", [P, NT, D], F32, 32)
    raw1, raw2 = at("moe_raw1", [128, KT, HID], F32, 92), at("moe_raw2", [128, MT, D], F32, 96)
    w1 = [[at(f"moe_w1_{x}{i}", [128, KT, HID], F32R, 100 + 8 * i + 4 * j) for j, x in enumerate(("hi", "lo"))]
          for i in range(2)]
    w2 = [[at(f"moe_w2_{x}{i}", [128, MT, D], F32R, 116 + 8 * i + 4 * j) for j, x in enumerate(("hi", "lo"))]
          for i in range(2)]
    r = at("moe_gelu", [128, MT, CH], F32, 132)
    h_hi, h_lo = at("moe_h_hi", [128, MT, CH], F32R, 134), at("moe_h_lo", [128, MT, CH], F32R, 136)
    g1, beta1, g2, beta2 = (at(n, [P, D], F32, 140 + 2 * i) for i, n in enumerate(("g1", "beta1", "g2", "beta2")))
    b2 = at("moe_b2", [NE, D], F32, 148)
    b2_hi, b2_lo = at("moe_b2_hi", [NE, D], F32R, 189), at("moe_b2_lo", [NE, D], F32R, 191)
    bg, b1 = at("moe_bg", [P, NE], F32, 150), at("moe_b1", [128, NE * MT], F32, 150.125)
    wg = at("moe_wg", [128, KT, NE], F32, 150.25)
    thin = Thin(core, "wg", 180, 184)
    x3 = at("moe_x3", [P, NT, D], F32, 152)
    hot_t = at("moe_hot_t", [NE, N], F32R, 172)
    S = 177
    lg, hot, rank = at("moe_lg", [P, NT, NE], F32, S), at("moe_hot", [P, NT * NE], F32, S + .5), at("moe_rank", [P, NE], F32, S + 1)
    held = at("moe_held", [P, 4], F32, S + 1.25)
    best = at("moe_best", [P, NT, 1], F32, S + 1.125)
    hot3 = hot[:].rearrange("p (t e) -> p t e", e=NE)

    pre_in, small_in = sem("moe_pre_in"), sem("moe_small_in")
    raw1_in, raw2_in = sem("moe_raw1_in"), sem("moe_raw2_in")
    late_in, b2_hi_done, b2_split = sem("moe_late_in"), sem("moe_b2_hi_done"), sem("moe_b2_split")
    x3_ready = sem("moe_x3")
    t_ready, hot_ready = sem("moe_t_ready"), sem("moe_hot_ready")
    ht_done, ht_ready, b2_done, b2_added = sem("moe_ht_done"), sem("moe_ht_ready"), sem("moe_b2_done"), sem("moe_b2_added")
    w_hi, w_lo = sem("moe_w_hi"), sem("moe_w_lo")
    u_done, u_bank, u_hi, u_lo = sem("moe_u_done"), sem("moe_bank_free"), sem("moe_hi"), sem("moe_lo")
    out_done, added = sem("moe_out_done"), sem("moe_added")
    final, stored = sem("final_ready"), sem("out_stored")
    turned = g.turned.again()
    ln.turn += 2
    turn = ln.turn - 1
    w1_rows = w["W1e"].rearrange("e (k p) n -> e p k n", p=128)
    w2_rows = w["W2e"].rearrange("e (k p) n -> e p k n", p=128)

    def experts(eng, body, counts):
        with eng.Fori(0, NE // 2 - 1) as pair:
            for tick, per in counts:
                tick.enter(pair, 2 * per)
            for par in range(2):
                body(2 * pair + par, par, True)
            for tick, per in counts:
                tick.leave(NE // 2 - 1)
        for par in range(2):
            body(NE - 2 + par, par, par == 0)

    with nc.Block() as block:
        @block.sync
        def _(sp):
            sp.dma_start(pre[:], tiles(g.pre_store)).then_inc(pre_in, 16)
            for dst, src in ((g1[:], row_view(w["g1"])), (beta1[:], row_view(w["beta1"])), (b2[:], w["b2e"]),
                             (wg[:], w["Wg"].rearrange("(k p) n -> p k n", p=128)), (bg[:], row_view(w["bg"])),
                             (b1[:], w["b1e"])):
                sp.dma_start(dst, src).then_inc(small_in, 16)
            sp.dma_start(raw1[:], w1_rows[0]).then_inc(raw1_in, 16)
            sp.dma_start(raw2[:], w2_rows[0]).then_inc(raw2_in, 16)
            for dst, src in ((beta2[:], row_view(w["beta2"])), (g2[:], row_view(w["g2"])), (x3[:], tiles(g.x3_store))):
                sp.dma_start(dst, src).then_inc(late_in, 16)
            with sp.Fori(1, NE) as e:
                sp.wait_ge(w_lo, 2 * e - 1)
                sp.dma_start(raw1[:], w1_rows[bass.ds(e, 1)].rearrange("a p k n -> (a p) k n")).then_inc(raw1_in, 16)
                sp.wait_ge(w_lo, 2 * e)
                sp.dma_start(raw2[:], w2_rows[bass.ds(e, 1)].rearrange("a p k n -> (a p) k n")).then_inc(raw2_in, 16)
            for t in range(NT):
                sp.wait_ge(final, t + 1)
                sp.dma_start(w["out"][t * P:(t + 1) * P, :], t_[:, t, :]).then_inc(stored, 16)
            sp.wait_ge(stored, 16 * NT)

        @block.gpsimd
        def _(pool):
            thin.gpsimd(nc)
            pool.wait_ge(small_in, 96)
            before = Tick()

            def split(e, par):
                pool.wait_ge(raw1_in, 16 * e + 16)
                spot = held[:, 2 * par + 0:2 * par + 0 + 1]
                nc.gpsimd.tensor_tensor(spot, bg[:, 0:1], bg[:, 0:1], ALU.add)
                nc.gpsimd.tensor_copy(w1[par][0][:], raw1[:]).then_inc(w_hi, 1)
                pool.wait_ge(raw2_in, 16 * e + 16)
                spot = held[:, 2 * par + 1:2 * par + 1 + 1]
                nc.gpsimd.tensor_tensor(spot, bg[:, 0:1], bg[:, 0:1], ALU.add)
                nc.gpsimd.tensor_copy(w2[par][0][:], raw2[:]).then_inc(w_hi, 1)

            def expert(e, par, more):
                if more:
                    pool.wait_ge(out_done, 2 + before.base + before.n)
                    split(e + 1, 1 - par)
                before.step(2 * NC)

            split(0, 0)
            experts(pool, expert, ((before, 2 * NC),))
            pool.wait_ge(late_in, 48)
            for t in range(NT):
                last = nc.gpsimd.tensor_tensor(x3[:, t, :], x3[:, t, :], beta2[:], ALU.add)
            last.then_inc(x3_ready, 1)

        @block.scalar
        def _(act):
            ln.root_at(nc, act, turn)
            act.wait_ge(small_in, 96)
            nc.scalar.activation(b2_hi[:], b2[:], ACT.Copy).then_inc(b2_hi_done, 1)
            thin.scalar(nc, act, wg[:])
            turned.scalar(core, act, g.xt_hi)

            units = Tick()

            def hidden(e):
                for m in range(MT):
                    v = units.step()
                    act.wait_ge(u_done, v)
                    act.wait_ge(u_lo, v)
                    nc.scalar.activation(r[:, m, :], core.bank(6 + m)[:, 0:CH], ACT.Gelu,
                                         bias=b1[:, bass.ds(MT * e + m, 1)]).then_inc(u_bank, 1)

            def expert(e, par, more):
                with act.Fori(0, NC) as c:
                    units.enter(c, MT)
                    hidden(e)
                    units.leave(NC)

            experts(act, expert, ((units, MT * NC),))
            ln.root_at(nc, act, turn + 1)

        @block.vector
        def _(dve):
            link = core.link.on(dve)
            dve.wait_ge(pre_in, 16)
            dve.wait_ge(small_in, 96)
            affine(nc, link, pre, t_, ln, turn, g1, [beta1[:]] * NT, None)
            dve.sem_inc(t_ready, 1)
            thin.vector(nc, dve, wg[:])
            dve.wait_ge(b2_hi_done, 1)
            nc.vector.tensor_tensor(b2_lo[:], b2[:], f32(b2_hi[:]), ALU.subtract).then_inc(b2_split, 1)
            turned.vector(core, dve, g.xt_hi, g.xt_lo)
            thin.vector_rows(nc, dve)
            for e in range(NE):
                last = nc.vector.memset(rank[:, e:e + 1], float(NE - e))
            link(last)
            dve.wait_ge(thin.done, 1)
            link(nc.vector.tensor_tensor(lg[:], thin.out, bc(bg[:], NT), ALU.add))
            link(nc.vector.tensor_reduce(best[:], lg[:], AX.X, ALU.max))
            link(nc.vector.tensor_tensor(lg[:], lg[:], best[:].broadcast_to([P, NT, NE]), ALU.is_equal))
            link(nc.vector.tensor_tensor(lg[:], lg[:], bc(rank[:], NT), ALU.mult))
            link(nc.vector.tensor_reduce(best[:], lg[:], AX.X, ALU.max))
            nc.vector.tensor_tensor(hot3, lg[:], best[:].broadcast_to([P, NT, NE]), ALU.is_equal).then_inc(hot_ready, 1)
            for q in range(3):
                n = min(4, NT - 4 * q) * P
                dve.wait_ge(ht_done, q + 1)
                last = nc.vector.tensor_copy(hot_t[:, 4 * q * P:4 * q * P + n], core.bank(q)[0:NE, 0:n])
            last.then_inc(ht_ready, 1)
            halves, units, subs, its = Tick(), Tick(), Tick(), Tick()

            def split(par):
                for dst, src in ((w1[par], raw1), (w2[par], raw2)):
                    dve.wait_ge(w_hi, halves.step())
                    nc.vector.tensor_tensor(dst[1][:], src[:], f32(dst[0][:]), ALU.subtract).then_inc(w_lo, 1)

            split(0)
            for t in range(NT):
                dve.wait_ge(b2_done, t + 1)
                nc.vector.tensor_tensor(t_[:, t, :], t_[:, t, :], core.bank(2 + t % 4)[0:P, :],
                                        ALU.add).then_inc(b2_added, 1)

            def rests():
                dve.wait_ge(out_done, 2 * its.step())
                for m in range(MT):
                    dve.wait_ge(u_bank, 2 + units.step())
                    nc.vector.tensor_copy(h_hi[:, m, :], r[:, m, :]).then_inc(u_hi, 1)
                for m in range(MT):
                    dve.wait_ge(u_hi, units.base + units.n - MT + 1 + m)
                    nc.vector.tensor_tensor(h_lo[:, m, :], r[:, m, :], f32(h_hi[:, m, :]), ALU.subtract).then_inc(u_lo, 1)

            def add_out(c, e):
                for s in range(2):
                    dve.wait_ge(out_done, subs.step() + 2)
                    dst = t_[:, bass.ds(2 * c + s, 1), :].rearrange("p a n -> p (a n)")
                    nc.vector.scalar_tensor_tensor(dst, core.bank(s)[0:P, :], hot[:, bass.ds(NE * (2 * c + s) + e, 1)],
                                                   dst, ALU.mult, ALU.add).then_inc(added, 1)

            def expert(e, par, more):
                rests()
                with dve.Fori(1, NC - 1) as c:
                    units.enter(c - 1, MT), subs.enter(c - 1, 2), its.enter(c - 1, 1)
                    rests()
                    add_out(c - 1, e)
                    units.leave(NC - 2), subs.leave(NC - 2), its.leave(NC - 2)
                if more:
                    split(1 - par)
                rests()
                add_out(NC - 2, e), add_out(NC - 1, e)

            experts(dve, expert, ((halves, 2), (units, MT * NC), (subs, 2 * NC), (its, NC)))
            dve.wait_ge(added, 2 * NC * NE + 2)
            dve.wait_ge(x3_ready, 1)
            affine(nc, link, t_, t_, ln, turn + 1, g2, [x3[:, t, :] for t in range(NT)], final)

        @block.tensor
        def _(pe):
            pe.wait_ge(t_ready, 1)
            turned.tensor(core, pe, t_, g.ident)
            pe.wait_ge(turned.lo, turned.before + NT)
            thin.tensor(nc, pe, (g.xt_hi, g.xt_lo))
            thin.tensor_turn(nc, pe, g.ident)
            pe.wait_ge(hot_ready, 1)
            for t in range(NT):
                q, j = divmod(t, 4)
                last = nc.tensor.transpose(core.bank(q)[0:NE, j * P:(j + 1) * P], hot3[:, t, :], g.ident[0:P, 0:P])
                if j == 3 or t == NT - 1:
                    last.then_inc(ht_done, 1)
            pe.wait_ge(ht_ready, 1)
            pe.wait_ge(b2_split, 1)
            for t in range(NT):
                if t >= 4:
                    pe.wait_ge(b2_added, t - 3)
                for half in (b2_hi, b2_lo):
                    last = nc.tensor.matmul(core.bank(2 + t % 4)[0:P, :], hot_t[:, t * P:(t + 1) * P], half[:],
                                            start=half is b2_hi, stop=half is b2_lo)
                last.then_inc(b2_done, 1)
            units, subs = Tick(), Tick()

            def hidden(c, par):
                for m in range(MT):
                    pe.wait_ge(u_bank, units.step())
                    for k in range(KT):
                        last = three_pass(nc, core.bank(6 + m)[:, 0:CH],
                                          [a[:, k, m * 128:(m + 1) * 128] for a in w1[par]],
                                          [a[:, k, bass.ds(CH * c, CH)] for a in (g.xt_hi, g.xt_lo)],
                                          k == 0, k == KT - 1)
                    last.then_inc(u_done, 1)

            def outputs(c, par, ahead):
                pe.wait_ge(u_lo, units.base + units.n - ahead + 2)
                for s in range(2):
                    pe.wait_ge(added, subs.step())
                    for k in range(MT):
                        last = three_pass(nc, core.bank(s)[0:P, :], [a[:, k, s * P:(s + 1) * P] for a in (h_hi, h_lo)],
                                          [a[:, k, :] for a in w2[par]], k == 0, k == MT - 1)
                    last.then_inc(out_done, 1)

            def expert(e, par, more):
                pe.wait_ge(w_lo, 2 * e + 2)
                hidden(0, par)
                with pe.Fori(1, NC) as c:
                    units.enter(c - 1, MT), subs.enter(c - 1, 2)
                    hidden(c, par)
                    outputs(c - 1, par, MT)
                    units.leave(NC - 1), subs.leave(NC - 1)
                outputs(NC - 1, par, 0)

            experts(pe, expert, ((units, MT * NC), (subs, 2 * NC)))


class Shared:
    pass


def program(nc, w):
    with ExitStack() as stack:
        core = Core(nc, stack)
        at = core.at
        g = Shared()
        g.ident, g.lohi = at("ident", [128, 128], F32, 0), at("lohi", [128, 2 * NT], I32, 0.5)
        g.node_ids = at("node_ids", [128, N], F16, 1)
        g.small = 1
        ln, g.turned = NormState(core, 2.5), Turned(core)
        core.parts = []
        g.gcol, g.headflag = at("gcol", [128, KT, 2], F32, 3.5), at("headflag", [128, HEADS], F32, 3.5625)
        g.has_edge = at("has_edge", [P, NT], F32, 3.625)
        g.bq, g.bk = at("bq_cols", [128, HEADS * KT], F32, 4), at("bk_cols", [128, HEADS * KT], F32, 4.125)
        g.tcols, g.ucols = at("t_cols", [128, HEADS * KT], F32, 4.25), at("u_cols", [128, HEADS * KT], F32, 4.375)
        g.cd, g.cols_in = at("score_consts", [P, NT * HEADS], F32, 4.5), core.sem("bias_cols_in")
        g.agg = at("edge_mean", [P, NT, EDGE_D], F32, 8)
        g.x, g.xs = at("x_first", [P, NT, D], F32, 160), at("xs_first", [P, NT, D], F32, 180)
        g.xn_hi, g.xn_lo = at("xn_hi", [P, NT, D], F32R, 12), at("xn_lo", [P, NT, D], F32R, 32)
        g.xt_hi, g.xt_lo = at("xt_hi", [128, KT, N], F32R, 52), at("xt_lo", [128, KT, N], F32R, 72)
        g.acc, g.gs_acc = at("acc", [P, NT, D], F32, 92), at("gs_acc", [128, KT, D], F32, 144)
        g.attr_sums = at("attr_sums", [P, NT, PARTS], F32, 112)
        g.counts = nc.dram_tensor("edge_counts", [N, N], U16, kind="Internal").ap()
        g.x3_store, g.xs_store, g.pre_store = (
            nc.dram_tensor(n, [N, D], F32, kind="Internal").ap() for n in ("x3_store", "xs_store", "pre_store"))

        g.qk_store, g.vl_store = (
            nc.dram_tensor(n, [HEADS, 128, KT, D], F32, kind="Internal").ap() for n in ("qk_store", "vl_store"))
        g.gs_store = nc.dram_tensor("skip_store", [128, KT, D], F32, kind="Internal").ap()
        g.q_store = [nc.dram_tensor(n, [128, KT, N], F32, kind="Internal").ap() for n in ("q_hi_store", "q_lo_store")]

        edge_ranges(core, g, w["dst_groups"], w["src_cols"], w["dst_cols"], w["x"], w["attr"])
        count_edges(core, g)
        head_matrices(core, g, w)
        first_features(core, g, ln)
        graph_attention(core, g, w)
        core.next_part()
        g.x, g.xs = at("x_res", [P, NT, D], F32, 12), at("xs_res", [P, NT, D], F32, 32)
        graph_output(core, g, w, ln)
        expert_lora(core, g, w, ln)
        edge_mean_gnn(core, g, w, ln)
        keys_values(core, g, w, ln)
        self_attention(core, g, w)
        expert_mixture(core, g, w, ln)


def lay_out(i):
    def turned(a):
        return a.swapaxes(-1, -2)

    def cols(a, *lead):
        return np.moveaxis(a.reshape(*a.shape[:-1], -1, 128), -1, 0)

    more = ET * P - EDGES
    src, dst = (np.concatenate([i[n], np.full(more, N, i[n].dtype)]) for n in ("src", "dst"))
    attr = np.concatenate([i["edge_attr_64"], np.zeros((more, EDGE_D), np.float32)])
    gates = np.concatenate([i["L0_ffn_gate_w"], i["L0_ffn_thr_w"], np.zeros((1, D), np.float32)])
    out = {
        "x": i["x"],
        "dst_groups": dst.reshape(GROUPS, GROUP * P), "src_cols": src.reshape(ET, P).T,
        "dst_cols": dst.reshape(ET, P).T,
        "attr": attr.reshape(ET, P, EDGE_D).transpose(1, 0, 2),
        "WqT": turned(i["L0_gnn_Wq"]), "WkT": turned(i["L0_gnn_Wk"]), "WvT": turned(i["L0_gnn_Wv"]),
        "WskipT": turned(i["L0_gnn_Wskip"]), "Wlin": i["L0_gnn_Wlin"],
        "bq": cols(i["L0_gnn_bq"]), "bk": cols(i["L0_gnn_bk"]), "bv": cols(i["L0_gnn_bv"]),
        "bskip": cols(i["L0_gnn_bskip"]),
        "blin": i["L0_gnn_blin"], "gamma": i["L0_gnn_gamma"], "beta": i["L0_gnn_beta"],
        "gates": gates.reshape(6, KT, 128).transpose(2, 1, 0),
        "lora_A": i["L0_ffn_lora_A"].reshape(4, KT, 128, 16).transpose(2, 0, 1, 3),
        "lora_B": turned(i["L0_ffn_lora_B"]).reshape(4, KT, 128, 16).transpose(2, 0, 1, 3),
        "fc1T": turned(i["L0_ffn_fc1_w"]), "fc2T": turned(i["L0_ffn_fc2_w"]),
        "W1": i["L1_gnn_W1"], "b1": cols(i["L1_gnn_b1"]), "W2": i["L1_gnn_W2"], "b2": i["L1_gnn_b2"],
        "Wq2": i["L1_ffn_Wq"], "Wk2": i["L1_ffn_Wk"], "Wv2": i["L1_ffn_Wv"], "Wo": i["L1_ffn_Wo"],
        "bq2": cols(i["L1_ffn_bq"]), "bk2": cols(i["L1_ffn_bk"]), "bv2": i["L1_ffn_bv"], "bo": i["L1_ffn_bo"],
        "g1": i["L1_ffn_g1"], "beta1": i["L1_ffn_beta1"], "g2": i["L1_ffn_g2"], "beta2": i["L1_ffn_beta2"],
        "Wg": i["L1_ffn_Wg"], "bg": i["L1_ffn_bg"],
        "W1e": i["L1_ffn_W1"], "b1e": cols(i["L1_ffn_b1"].reshape(-1)), "W2e": i["L1_ffn_W2"], "b2e": i["L1_ffn_b2"],
    }
    return {name: np.ascontiguousarray(a) for name, a in out.items()}


def kernel(**inputs):
    import concourse.bacc as bacc
    from concourse.bass_utils import run_bass_kernel_spmd

    arrays = lay_out({name: np.asarray(a) for name, a in inputs.items()})
    nc = bacc.Bacc("TRN2", target_bir_lowering=False, num_devices=1)
    handles = {name: nc.dram_tensor(f"in_{name}", a.shape, mybir.dt.from_np(a.dtype), kind="ExternalInput").ap()
               for name, a in arrays.items()}
    handles["out"] = nc.dram_tensor("out", [N, D], F32, kind="ExternalOutput").ap()
    program(nc, handles)
    result = run_bass_kernel_spmd(nc, [{f"in_{name}": a for name, a in arrays.items()}], core_ids=[0])
    return result.results[0]["out"]
```
